# Optimizing a Trainium2 kernel written in Bass

```python
import numpy as np
import jax
import jax.numpy as jnp

def _softmax(x, axis=-1):
    return jax.nn.softmax(x, axis=axis)

def _gelu(x):
    return jax.nn.gelu(x, approximate=True)

def _silu(x):
    return jax.nn.silu(x)

def _sigmoid(x):
    return jax.nn.sigmoid(x)

def _layernorm(x, axis=-1, eps=1e-05):
    m = jnp.mean(x, axis=axis, keepdims=True)
    v = jnp.var(x, axis=axis, keepdims=True)
    return (x - m) / jnp.sqrt(v + eps)

def _scatter_add(tgt, idx, src, axis=0):
    return tgt.at[idx].add(src)

def _segment_sum(src, seg, n):
    return jax.ops.segment_sum(src, seg, n)
kernel_name = 'mk_gps_d1_gnn_r64_3a4393'

def setup_inputs(seed: int=0):
    np.random.seed(seed)
    _w = jnp.asarray

    def _rec_inputs():
        import jax
        import jax.numpy as jnp
        _gk = jax.random.key(seed)
        x = -6.415e-05 + 1 * jax.random.normal(jax.random.fold_in(_gk, 1), (10000, 512), jnp.float32)
        src = jax.random.randint(jax.random.fold_in(_gk, 2), (2500,), 0, 10000, jnp.int32)
        dst = jax.random.randint(jax.random.fold_in(_gk, 3), (2500,), 0, 10000, jnp.int32)
        _o = jnp.argsort(dst, stable=True)
        src = src[_o]
        dst = dst[_o]
        return (x, src, dst)
    x, src, dst = _rec_inputs()

    def _L0_gnn_setup():
        import jax, jax.numpy as jnp
        import numpy as np
        NEG_SLOPE = 0.2
        HEADS = 8

        def gat_conv(x, src, dst, W, att_src, att_dst, bias, heads, out_ch):
            N = x.shape[0]
            h = (x @ W).reshape(N, heads, out_ch)
            a_src = jnp.einsum('nhc,hc->nh', h, att_src)
            a_dst = jnp.einsum('nhc,hc->nh', h, att_dst)
            e = jax.nn.leaky_relu(a_src[src] + a_dst[dst], NEG_SLOPE)
            m = jax.ops.segment_max(e, dst, num_segments=N)
            m = jnp.where(jnp.isfinite(m), m, jnp.zeros_like(m))
            ex = jnp.exp(e - m[dst])
            s = jax.ops.segment_sum(ex, dst, num_segments=N)
            alpha = ex / (s[dst] + 1e-16)
            msg = h[src] * alpha[:, :, None]
            out = jax.ops.segment_sum(msg, dst, num_segments=N)
            return out.reshape(N, heads * out_ch) + bias
        key = jax.random.key(seed)
        ks = jax.random.split(key, 12)
        N, F_in, nhid, heads, ncls, E = (20000, 512, 128, HEADS, 64, 3125)
        x = jax.random.normal(ks[0], (N, F_in), dtype=jnp.float32)
        edge_index = jax.random.randint(ks[1], (2, E), 0, N, dtype=jnp.int32)

        def lin(k, fi, fo):
            return jax.random.normal(k, (fi, fo), dtype=jnp.float32) / np.sqrt(fi)
        W1 = lin(ks[2], F_in, heads * nhid)
        att_src1 = jax.random.normal(ks[3], (heads, nhid), dtype=jnp.float32) / np.sqrt(nhid)
        att_dst1 = jax.random.normal(ks[4], (heads, nhid), dtype=jnp.float32) / np.sqrt(nhid)
        b1 = jnp.zeros((heads * nhid,), dtype=jnp.float32)
        W2 = lin(ks[5], heads * nhid, heads * ncls)
        att_src2 = jax.random.normal(ks[6], (heads, ncls), dtype=jnp.float32) / np.sqrt(ncls)
        att_dst2 = jax.random.normal(ks[7], (heads, ncls), dtype=jnp.float32) / np.sqrt(ncls)
        b2 = jnp.zeros((heads * ncls,), dtype=jnp.float32)
        return {'x': x, 'edge_index': edge_index, 'W1': W1, 'att_src1': att_src1, 'att_dst1': att_dst1, 'b1': b1, 'W2': W2, 'att_src2': att_src2, 'att_dst2': att_dst2, 'b2': b2}
    _L0_gnn_all = _L0_gnn_setup()
    _L0_gnn_in = {k: v for k, v in _L0_gnn_all.items() if k in ('W1', 'att_src1', 'att_dst1', 'b1', 'W2', 'att_src2', 'att_dst2', 'b2')}
    del _L0_gnn_all

    def _L0_mix_setup():
        import jax, jax.numpy as jnp
        import numpy as np
        DIM, HEADS, DIM_HEAD = (512, 8, 64)
        key = jax.random.key(seed)
        ks = jax.random.split(key, 9)
        B, T = (4, 64)
        s = 1.0 / np.sqrt(DIM)
        x = jax.random.normal(ks[0], (B, T, DIM), dtype=jnp.float32)
        Wq = jax.random.uniform(ks[1], (DIM, DIM), jnp.float32, -s, s)
        Wk = jax.random.uniform(ks[2], (DIM, DIM), jnp.float32, -s, s)
        Wv = jax.random.uniform(ks[3], (DIM, DIM), jnp.float32, -s, s)
        Wp = jax.random.uniform(ks[4], (DIM, DIM), jnp.float32, -s, s)
        bq = jax.random.uniform(ks[5], (DIM,), jnp.float32, -s, s)
        bk = jax.random.uniform(ks[6], (DIM,), jnp.float32, -s, s)
        bv = jax.random.uniform(ks[7], (DIM,), jnp.float32, -s, s)
        bp = jax.random.uniform(ks[8], (DIM,), jnp.float32, -s, s)
        return {'x': x, 'Wq': Wq, 'bq': bq, 'Wk': Wk, 'bk': bk, 'Wv': Wv, 'bv': bv, 'Wp': Wp, 'bp': bp}
    _L0_mix_all = _L0_mix_setup()
    _L0_mix_in = {k: v for k, v in _L0_mix_all.items() if k in ('Wq', 'bq', 'Wk', 'bk', 'Wv', 'bv', 'Wp', 'bp')}
    del _L0_mix_all

    def _L0_ffn_setup():
        import jax, jax.numpy as jnp
        import numpy as np
        CAPACITY_FACTOR = 1.2
        key = jax.random.key(seed)
        k1, k2, k3 = jax.random.split(key, 3)
        B, S, D, E = (8, 64, 512, 16)
        x = jax.random.normal(k1, (B, S, D), dtype=jnp.float32)
        switch_w = jax.random.normal(k2, (E, D), dtype=jnp.float32) * 0.02
        switch_b = jnp.zeros((E,), dtype=jnp.float32)
        expert_w = jax.random.normal(k3, (E, D, D), dtype=jnp.float32) * 0.02
        expert_b = jnp.zeros((E, D), dtype=jnp.float32)
        return {'x': x, 'switch_w': switch_w, 'switch_b': switch_b, 'expert_w': expert_w, 'expert_b': expert_b}
    _L0_ffn_all = _L0_ffn_setup()
    _L0_ffn_in = {k: v for k, v in _L0_ffn_all.items() if k in ('switch_w', 'switch_b', 'expert_w', 'expert_b')}
    del _L0_ffn_all
    return {'x': x, 'src': src, 'dst': dst, 'L0_gnn_W1': _L0_gnn_in['W1'], 'L0_gnn_att_src1': _L0_gnn_in['att_src1'], 'L0_gnn_att_dst1': _L0_gnn_in['att_dst1'], 'L0_gnn_b1': _L0_gnn_in['b1'], 'L0_gnn_W2': _L0_gnn_in['W2'], 'L0_gnn_att_src2': _L0_gnn_in['att_src2'], 'L0_gnn_att_dst2': _L0_gnn_in['att_dst2'], 'L0_gnn_b2': _L0_gnn_in['b2'], 'L0_mix_Wq': _L0_mix_in['Wq'], 'L0_mix_bq': _L0_mix_in['bq'], 'L0_mix_Wk': _L0_mix_in['Wk'], 'L0_mix_bk': _L0_mix_in['bk'], 'L0_mix_Wv': _L0_mix_in['Wv'], 'L0_mix_bv': _L0_mix_in['bv'], 'L0_mix_Wp': _L0_mix_in['Wp'], 'L0_mix_bp': _L0_mix_in['bp'], 'L0_ffn_switch_w': _L0_ffn_in['switch_w'], 'L0_ffn_switch_b': _L0_ffn_in['switch_b'], 'L0_ffn_expert_w': _L0_ffn_in['expert_w'], 'L0_ffn_expert_b': _L0_ffn_in['expert_b']}

def reference(x, src, dst, L0_gnn_W1, L0_gnn_att_src1, L0_gnn_att_dst1, L0_gnn_b1, L0_gnn_W2, L0_gnn_att_src2, L0_gnn_att_dst2, L0_gnn_b2, L0_mix_Wq, L0_mix_bq, L0_mix_Wk, L0_mix_bk, L0_mix_Wv, L0_mix_bv, L0_mix_Wp, L0_mix_bp, L0_ffn_switch_w, L0_ffn_switch_b, L0_ffn_expert_w, L0_ffn_expert_b):
    import jax
    import jax.numpy as jnp

    def _L0_gnn_ref(x, edge_index, W1, att_src1, att_dst1, b1, W2, att_src2, att_dst2, b2):
        import jax, jax.numpy as jnp
        import numpy as np
        NEG_SLOPE = 0.2
        HEADS = 8

        def gat_conv(x, src, dst, W, att_src, att_dst, bias, heads, out_ch):
            N = x.shape[0]
            h = (x @ W).reshape(N, heads, out_ch)
            a_src = jnp.einsum('nhc,hc->nh', h, att_src)
            a_dst = jnp.einsum('nhc,hc->nh', h, att_dst)
            e = jax.nn.leaky_relu(a_src[src] + a_dst[dst], NEG_SLOPE)
            m = jax.ops.segment_max(e, dst, num_segments=N)
            m = jnp.where(jnp.isfinite(m), m, jnp.zeros_like(m))
            ex = jnp.exp(e - m[dst])
            s = jax.ops.segment_sum(ex, dst, num_segments=N)
            alpha = ex / (s[dst] + 1e-16)
            msg = h[src] * alpha[:, :, None]
            out = jax.ops.segment_sum(msg, dst, num_segments=N)
            return out.reshape(N, heads * out_ch) + bias
        N = x.shape[0]
        nhid = att_src1.shape[1]
        ncls = att_src2.shape[1]
        loop = jnp.arange(N, dtype=edge_index.dtype)
        src = jnp.concatenate([edge_index[0], loop])
        dst = jnp.concatenate([edge_index[1], loop])
        h = gat_conv(x, src, dst, W1, att_src1, att_dst1, b1, HEADS, nhid)
        h = jax.nn.relu(h)
        out = gat_conv(h, src, dst, W2, att_src2, att_dst2, b2, HEADS, ncls)
        return jax.nn.log_softmax(out, axis=1)

    def _L0_mix_ref(x, Wq, bq, Wk, bk, Wv, bv, Wp, bp):
        import jax, jax.numpy as jnp
        import numpy as np
        DIM, HEADS, DIM_HEAD = (512, 8, 64)
        B, T, _ = x.shape
        H, D = (HEADS, DIM_HEAD)

        def proj(W, b):
            return (x @ W.T + b).reshape(B, T, H, D).transpose(0, 2, 1, 3)
        q = jax.nn.softmax(proj(Wq, bq), axis=-1)
        k = jax.nn.softmax(proj(Wk, bk), axis=-1)
        v = proj(Wv, bv)
        k_sum = k.sum(axis=2, keepdims=True)
        D_inv = 1.0 / (q * k_sum).sum(axis=-1, keepdims=True)
        context = jnp.einsum('bhtd,bhte->bhde', k, v)
        out = jnp.einsum('bhtd,bhde->bhte', q, context) * D_inv + q
        out = out.transpose(0, 2, 1, 3).reshape(B, T, H * D)
        return out @ Wp.T + bp

    def _L0_ffn_ref(x, switch_w, switch_b, expert_w, expert_b):
        import jax, jax.numpy as jnp
        import numpy as np
        CAPACITY_FACTOR = 1.2
        B, S, D = x.shape
        E = switch_w.shape[0]
        N = B * S
        xf = x.reshape(N, D)
        logits = xf @ switch_w.T + switch_b
        probs = jax.nn.softmax(logits, axis=-1)
        route_probs = jnp.max(probs, axis=-1)
        routes = jnp.argmax(probs, axis=-1)
        oh = jax.nn.one_hot(routes, E, dtype=jnp.int32)
        pos = jnp.take_along_axis(jnp.cumsum(oh, axis=0), routes[:, None], axis=1)[:, 0] - 1
        capacity = int(CAPACITY_FACTOR * N / E)
        keep = pos < capacity
        buf = jnp.zeros((E, capacity, D), dtype=xf.dtype).at[routes, pos].set(xf)
        y = jnp.einsum('ecd,efd->ecf', buf, expert_w) + expert_b[:, None, :]
        gathered = y[routes, jnp.minimum(pos, capacity - 1)]
        out = jnp.where(keep[:, None], gathered, xf) * route_probs[:, None]
        return out.reshape(B, S, D)
    edge_index = jnp.stack([src, dst])
    xn = _layernorm(x, axis=-1)
    x = x + _L0_gnn_ref(xn, edge_index, L0_gnn_W1, L0_gnn_att_src1, L0_gnn_att_dst1, L0_gnn_b1, L0_gnn_W2, L0_gnn_att_src2, L0_gnn_att_dst2, L0_gnn_b2) + _L0_mix_ref(xn[None], L0_mix_Wq, L0_mix_bq, L0_mix_Wk, L0_mix_bk, L0_mix_Wv, L0_mix_bv, L0_mix_Wp, L0_mix_bp)[0]
    x = x + _L0_ffn_ref(_layernorm(x, axis=-1)[None], L0_ffn_switch_w, L0_ffn_switch_b, L0_ffn_expert_w, L0_ffn_expert_b)[0]
    return x

_drawn_inputs = setup_inputs


def setup_inputs(seed=0):
    import zlib

    import numpy as np

    out = dict(_drawn_inputs(seed))
    spreads = {'L0_gnn_b1': (0.0, 0.707),
     'L0_gnn_b2': (0.0, 0.474),
     'L0_ffn_switch_b': (0.0, 0.8),
     'L0_ffn_expert_b': (0.0, 0.8)}
    factors = {'L0_gnn_att_src1': 7.868,
     'L0_gnn_att_dst1': 8.0,
     'L0_gnn_att_src2': 8.0,
     'L0_gnn_att_dst2': 8.0,
     'L0_mix_Wq': 8.0,
     'L0_mix_bq': 8.0,
     'L0_mix_Wk': 8.0,
     'L0_mix_bk': 8.0,
     'L0_mix_Wv': 8.0,
     'L0_mix_bv': 8.0,
     'L0_mix_Wp': 8.0,
     'L0_mix_bp': 8.0,
     'L0_ffn_switch_w': 5.233,
     'L0_ffn_expert_w': 6.549}
    for name, (base, spread) in spreads.items():
        noise = np.random.default_rng([zlib.crc32(name.encode()), seed]).standard_normal(out[name].shape)
        drawn = base * np.exp(spread * noise) if base else spread * noise
        out[name] = jnp.asarray(drawn.astype(out[name].dtype))
    for name, factor in factors.items():
        out[name] = (out[name] * factor).astype(out[name].dtype)
    return out
```

```python
from contextlib import ExitStack

import concourse.bass as bass
from concourse import mybir

F32 = mybir.dt.float32
F32R = mybir.dt.float32r
BF16 = mybir.dt.bfloat16
I32 = mybir.dt.int32
U32 = mybir.dt.uint32
ALU = mybir.AluOpType
ACT = mybir.ActivationFunctionType
AX = mybir.AxisListType

P = 128
ROWS = 125
SUBS = 4
FAR = 1 << 20
EPS = 1e-5


SEM_BASE = (190, 130)


class Chain:

    def __init__(self, eng, sem):
        self.eng, self.sem, self.done, self.base, self.k = eng, sem, 0, None, 0

    def enter(self, trip, per_trip):
        self.per, self.k = per_trip, 0
        self.base = self.eng.snap(trip * per_trip + self.done)

    def leave(self, trips):
        assert self.k == self.per, f"the loop links {self.k} instructions, not {self.per}"
        self.done, self.base, self.k = self.done + trips * self.per, None, 0

    def link(self, ins, settle=None):
        ins.then_inc(self.sem, 1)
        if self.base is None:
            self.done += 1
            self.eng.wait_ge(self.sem, self.done)
        else:
            self.k += 1
            self.eng.wait_ge(self.sem, self.base + self.k)
            if settle is not None:
                self.eng.sem_inc(settle, 1)


def in_step(eng, count, unroll, stages, before_loop=None, chain=None, links=0):
    assert max(lag for _, lag in stages) <= unroll

    def step(q, r, known):
        for work, lag in stages:
            if known is None:
                dq, rr = divmod(r - lag, unroll)
                work(q + dq if dq else q, rr)
            elif 0 <= known - lag < count:
                work((known - lag) // unroll, (known - lag) % unroll)

    for n in range(unroll):
        step(0, n, n)
    trips = count // unroll - 1
    with eng.Fori(0, trips) as i:
        if chain is not None:
            chain.enter(i, links)
        for r in range(unroll):
            step(i + 1, r, None)
    if chain is not None:
        chain.leave(trips)
    for n in range(count, count + max(lag for _, lag in stages)):
        step(0, 0, n)


def scratch_tables(n, d, experts):
    capacity = int(1.2 * n / experts)
    return [("y2_table", (n, d), F32), ("q_table", (n, d), F32), ("x1_table", (n, d + 4), F32),
            ("token_of_slot", (P * experts * -(-capacity // P), 1), I32)]


def gps_layer(nc, x, src, dst, W1, att_src1, att_dst1, b1, W2, att_src2, att_dst2, b2,
              Wq, bq, Wk, bk, Wv, bv, Wp, bp, switch_w, switch_b, expert_w, expert_b, out,
              y2_table, q_table, x1_table, token_of_slot):
    N, D = x.shape
    E = src.shape[0]
    HEADS, HID = att_src1.shape
    CLS = att_src2.shape[1]
    HD = D // HEADS
    DH = HEADS * HID
    EXPERTS = switch_w.shape[0]
    CAP = int(1.2 * N / EXPERTS)
    SLOTS = -(-CAP // P)
    DC = D // P
    FC = DH // P
    MACRO = ROWS * SUBS
    MACROS = N // MACRO
    ET = E // ROWS
    META = 4
    assert N % MACRO == 0 and E % (2 * ROWS) == 0 and D == 512 and HEADS * CLS == D and HID == P
    assert EXPERTS == 16 and HD == 64 and CLS == HD

    with ExitStack() as ctx:
        shared = [[], []]
        now = [None]
        given = []

        def for_phase(n):
            for handle in given:
                nc.release_semaphore(handle)
            given.clear()
            now[0] = n

        def sem(name):
            if now[0] is None:
                return ctx.enter_context(nc.semaphore(name))
            numbers = shared[now[0] % 2]
            if len(given) < len(numbers):
                handle = nc.alloc_semaphore(name=name, num=numbers[len(given)])
            else:
                handle = nc.alloc_semaphore(name=name, num=SEM_BASE[now[0] % 2] + len(given))
                numbers.append(SEM_BASE[now[0] % 2] + len(given))
            given.append(handle)
            return handle

        cursor = [nc.sbuf_base + (-nc.sbuf_base) % 32]

        def place(name, shape, dt=F32):
            size = 2 if dt == BF16 else 4
            for n in shape[1:]:
                size *= n
            at = cursor[0] + (-cursor[0]) % 32
            cursor[0] = at + size
            return nc.alloc_sbuf_tensor_at(name, list(shape), dt, offset=at)

        ident = place("ident", [P, P])
        before = place("before", [ROWS, ROWS], BF16)
        ones_bf = place("ones_bf", [ROWS, ROWS], BF16)
        iota16 = place("iota16", [P, 16])
        rowid = place("rowid", [P, 2])
        last_row = place("last_row", [ROWS, 1])
        ones_f = place("ones_f", [ROWS, 2])
        minus_half = place("minus_half", [ROWS, SUBS])
        ones_r = place("ones_r", [ROWS, 2], F32R)
        ctx_acc = place("ctx_acc", [P, DC, P])
        ksum_acc = place("ksum_acc", [P, DC, 2])
        b1_col = place("b1_col", [P, FC])
        LOW = cursor[0]

        W1h = place("W1h", [P, DC, DH], F32R)
        W1l = place("W1l", [P, DC, DH], F32R)
        W2h = place("W2h", [P, FC, D], F32R)
        W2l = place("W2l", [P, FC, D], F32R)
        att1 = place("att1", [P, DC, 2 * 40])
        AFTER_GNN_WEIGHTS = cursor[0]

        WTh, WTl = {}, {}
        for n in "kvq":
            WTh[n] = place(f"W{n}Th", [P, DC, D], F32R)
            WTl[n] = place(f"W{n}Tl", [P, DC, D], F32R)
        bk_bc = place("bk_bc", [ROWS, D])
        bq_bc = place("bq_bc", [ROWS, D])
        xn = place("xn", [ROWS, SUBS, D])
        SCRATCH = cursor[0]
        xTh = place("xTh", [P, DC, MACRO], F32R)
        xTl = place("xTl", [P, DC, MACRO], F32R)
        kvh = place("kvh", [ROWS, 2, 2, D], F32R)
        kvl = place("kvl", [ROWS, 2, 2, D], F32R)
        kbuf = place("kbuf", [ROWS, 2, D])
        qbuf = place("qbuf", [ROWS, 2, D])
        y2o = place("y2o", [ROWS, 2, D])
        relu = place("relu", [P, 2, MACRO])
        h1h = place("h1h", [P, FC, MACRO], F32R)
        h1l = place("h1l", [P, FC, MACRO], F32R)
        stats = place("stats", [ROWS, SUBS, 6])
        mv = place("mv", [ROWS, SUBS, 2])
        veps = place("veps", [ROWS, SUBS])
        rstd = place("rstd", [ROWS, SUBS])
        newt = place("newt", [ROWS, 2, SUBS])
        kq_max = place("kq_max", [ROWS, 2, 2, HEADS])
        kq_rec = place("kq_rec", [ROWS, 2, 2, HEADS])
        cursor[0] = SCRATCH
        wk_st = place("wk_st", [P, DC, D])
        wv_st = place("wv_st", [P, DC, D])
        wq_st = place("wq_st", [P, DC, D])
        att_bc = place("att_bc", [P, 2, DH])
        att_tmp = place("att_tmp", [P, 2, DH])
        w1_st = place("w1_st", [P, DC, DH])
        w2_st = place("w2_st", [P, FC, D])

        cursor[0] = AFTER_GNN_WEIGHTS
        src_i = place("src_i", [ROWS, ET], I32)
        dst_i = place("dst_i", [ROWS, ET], I32)
        next_i = place("next_i", [ROWS, ET], I32)
        dst_f = place("dst_f", [ROWS, ET])
        next_f = place("next_f", [ROWS, ET])
        scat_i = place("scat_i", [ROWS, ET], I32)
        SL = EXPERTS * SLOTS
        dst_bc = place("dst_bc", [P, E + 2])
        at = cursor[0]
        xsT = place("xsT", [P, DC, E])
        xdT = place("xdT", [P, DC, E])
        cursor[0] = at
        ys_all = place("ys_all", [ROWS, ET, D])
        yd_all = place("yd_all", [ROWS, ET, D])
        EDGE_SCRATCH = cursor[0] = max(cursor[0], at + 2 * (DC * E * 4 + 32))
        run = place("run", [HEADS, E])
        head_e = place("head_e", [HEADS, E])
        head_s = place("head_s", [HEADS, E])
        same = place("same", [HEADS, E + 1])
        wall = place("wall", [HEADS, E + 1])
        cursor[0] = EDGE_SCRATCH
        dst_bi = place("dst_bi", [P, E], I32)
        gath = place("gath", [ROWS, 2, 2, D])
        e_idx = place("e_idx", [ROWS, 2, 2], I32)
        e_stats = place("e_stats", [ROWS, 2, 6])
        e_mv = place("e_mv", [ROWS, 2, 2])
        e_veps = place("e_veps", [ROWS, 2])
        e_rstd = place("e_rstd", [ROWS, 2])
        e_newt = place("e_newt", [ROWS, 2, 2])
        cursor[0] = EDGE_SCRATCH
        xsh = place("xsh", [P, 2, DC, ROWS], F32R)
        xsl = place("xsl", [P, 2, DC, ROWS], F32R)
        msg = place("msg", [ROWS, 2, D])
        msg_self = place("msg_self", [ROWS, 2, D])
        msgh = place("msgh", [ROWS, DH], F32R)
        msgl = place("msgl", [ROWS, DH], F32R)
        same_dst = place("same_dst", [ROWS, ROWS + 1], F32R)
        goes_on = place("goes_on", [P, ROWS])
        aggT = place("aggT", [P, FC, ROWS])
        aggh = place("aggh", [P, FC, ROWS], F32R)
        aggl = place("aggl", [P, FC, ROWS], F32R)
        carry = place("carry", [P, FC])
        y_edge = place("y_edge", [ROWS, D])
        scat_st = place("scat_st", [ROWS, 2], I32)
        alpha_e = place("alpha_e", [ROWS, ET, HEADS])
        alpha_s = place("alpha_s", [ROWS, ET, HEADS])
        no_token = place("no_token", [P, SL], I32)
        cursor[0] = LOW
        att2_bc = place("att2_bc", [ROWS, 2, D])
        g2 = place("g2", [ROWS, 2, 2, D])
        prod2 = place("prod2", [ROWS, 3, D])
        dots = place("dots", [ROWS, 3, HEADS])
        logit2 = place("logit2", [ROWS, 2, 2 * HEADS])
        idx2 = place("idx2", [ROWS, 2, 2], I32)
        m2 = place("m2", [ROWS, 2, D])
        m2s = place("m2s", [ROWS, 2, D])
        m2h = place("m2h", [ROWS, 2, D], F32R)
        m2l = place("m2l", [ROWS, 2, D], F32R)
        same2 = place("same2", [ROWS, 2, ROWS], F32R)
        goes2 = place("goes2", [ROWS, 2, ROWS], F32R)
        z32 = place("z32", [ROWS, 2, D])
        zh = place("zh", [ROWS, 2, D], F32R)
        zl = place("zl", [ROWS, 2, D], F32R)
        scat2 = place("scat2", [ROWS, 2], I32)

        G = 4
        cursor[0] = LOW
        wp_st = place("wp_st", [P, DC, D])
        WpTh = place("WpTh", [P, DC, D], F32R)
        WpTl = place("WpTl", [P, DC, D], F32R)
        sw_st = place("sw_st", [EXPERTS, D])
        swT = place("swT", [P, DC, EXPERTS])
        sb_bc = place("sb_bc", [ROWS, EXPERTS])
        bv_bc = place("bv_bc", [P, D])
        bp_bc = place("bp_bc", [ROWS, D])
        b2_bc = place("b2_bc", [ROWS, D])
        ctxh = place("ctxh", [P, DC, P], F32R)
        ctxl = place("ctxl", [P, DC, P], F32R)
        ksum2 = place("ksum2", [P, DC, 2])
        ksh = place("ksh", [P, DC, 2], F32R)
        ksl = place("ksl", [P, DC, 2], F32R)
        iota_f = place("iota_f", [P, 16], I32)
        row_0 = place("row_0", [ROWS, 1], I32)
        steps_i = place("steps_i", [ROWS, max(SLOTS - 1, 1)], I32)
        used = place("used", [ROWS, EXPERTS])
        steps128 = place("steps128", [ROWS, max(SLOTS - 1, 1)])
        x_in = place("x_in", [ROWS, G, D])
        y_in = place("y_in", [ROWS, G, D])
        q_in = place("q_in", [ROWS, G, D])
        qTh = place("qTh", [P, 2, DC, ROWS], F32R)
        qTl = place("qTl", [P, 2, DC, ROWS], F32R)
        den = place("den", [ROWS, 2, HEADS])
        attn = place("attn", [ROWS, 2, D])
        oTh = place("oTh", [P, 2, DC, ROWS], F32R)
        oTl = place("oTl", [P, 2, DC, ROWS], F32R)
        exp_y = place("exp_y", [ROWS, D])
        y_stat = place("y_stat", [ROWS, 2, 4])
        x1row = place("x1row", [ROWS, G, D + META])
        stats4 = place("stats4", [ROWS, 6])
        mv4 = place("mv4", [ROWS, 2, 2])
        veps4 = place("veps4", [ROWS, 2, 1])
        r4 = place("r4", [ROWS, 2, 1])
        newt4 = place("newt4", [ROWS, 2, 1])
        xf = place("xf", [ROWS, G, D])
        xfT = place("xfT", [P, 2, DC, ROWS])
        lgt = place("lgt", [ROWS, 2, EXPERTS])
        lstat = place("lstat", [ROWS, 2, 4])
        ex16 = place("ex16", [ROWS, 2, EXPERTS])
        top8 = place("top8", [ROWS, 8])
        arg8 = place("arg8", [ROWS, 8], U32)
        argf = place("argf", [ROWS, 2, 1])
        onehot = place("onehot", [ROWS, 2, EXPERTS], BF16)
        rank = place("rank", [ROWS, EXPERTS])
        small = place("small", [ROWS, 8])
        slot_i = place("slot_i", [ROWS, 2], I32)
        row_i = place("row_i", [ROWS, 2], I32)
        steps_tmp = place("steps_tmp", [ROWS, max(SLOTS - 1, 1)])
        token_i = place("token_i", [ROWS, 2], I32)
        orow = place("orow", [ROWS, 2, D])

        SL = EXPERTS * SLOTS
        cursor[0] = LOW
        tok_i = place("tok_i", [P, SL], I32)
        tok_f = place("tok_f", [P, SL])
        from_i = place("from_i", [P, SL], I32)
        we_st = place("we_st", [P, 2, DC, D])
        WeTh = place("WeTh", [P, 2, DC, D], F32R)
        WeTl = place("WeTl", [P, 2, DC, D], F32R)
        eb_bc = place("eb_bc", [P, 2, D])
        row5 = place("row5", [P, 2, D + META])
        xf5 = place("xf5", [P, 2, D])
        fTh = place("fTh", [P, 2, DC, P], F32R)
        fTl = place("fTl", [P, 2, DC, P], F32R)
        yb5 = place("yb5", [P, 2, D])
        res5 = place("res5", [P, 2, D])
        from_st = place("from_st", [P, 2], I32)
        to_st = place("to_st", [P, 2], I32)

        banks = [nc.alloc_psum_tensor(f"bank{i}", [P, 512], F32) for i in range(8)]

        def groups(ap, n):
            return ap.rearrange("p (h c) -> p h c", h=n)

        def spread(ap, n):
            return ap.unsqueeze(2).to_broadcast([ap.shape[0], ap.shape[1], n])

        def products(out_, terms, rows=P):
            last = None
            for n, (ah, al, bh, bl) in enumerate(terms):
                nc.tensor.matmul(out_, ah, bh, start=n == 0, stop=False)
                nc.tensor.matmul(out_, ah, bl, start=False, stop=False)
                last = nc.tensor.matmul(out_, al, bh, start=False, stop=n == len(terms) - 1)
            return last


        const_done = sem("const_done")
        pool_chain = sem("pool_chain")
        dve_chain = sem("dve_chain")
        act_chain = sem("act_chain")
        pool_settled = sem("pool_settled")
        dve_settled = sem("dve_settled")
        sp_settled = sem("sp_settled")
        phase_done = sem("phase_done")
        e_gath = [sem(f"e_gath{j}") for j in range(2)]
        ye_store = sem("ye_store")
        g2_load = [sem(f"g2_load{j}") for j in range(2)]
        z_store = [sem(f"z_store{j}") for j in range(2)]
        tok_store = [sem(f"tok_store{j}") for j in range(2)]
        orow_store = [sem(f"orow_store{j}") for j in range(2)]
        row5_load = [sem(f"row5_load{j}") for j in range(2)]
        res_store = [sem(f"res_store{j}") for j in range(2)]
        for_phase(1)
        wload = {n: sem(f"wload_{n}") for n in ("k", "v", "q", "W1", "W2", "att0", "att1")}
        bias_load = [sem(f"bias_load{n}") for n in range(3)]
        ones_done = sem("ones_done")
        wt_bank = sem("wt_bank")
        wt_hi = sem("wt_hi")
        wt_lo = sem("wt_lo")
        w_hi = sem("w_hi")
        w_lo = sem("w_lo")
        w2_lo = sem("w2_lo")
        att_sum = sem("att_sum")
        x_load = sem("x_load")
        var_ready = sem("var_ready")
        rstd0 = sem("rstd0")
        xn_ready = sem("xn_ready")
        xt_bank = sem("xt_bank")
        xt_hi = sem("xt_hi")
        xt_lo = sem("xt_lo")
        kvq_bank = sem("kvq_bank")
        kvq_free = sem("kvq_free")
        smax = sem("smax")
        ssub = sem("ssub")
        sexp = sem("sexp")
        srec = sem("srec")
        snorm_k = sem("snorm_k")
        snorm_q = sem("snorm_q")
        v_hi = sem("v_hi")
        k_hi = sem("k_hi")
        k_lo = sem("k_lo")
        ctx_bank = sem("ctx_bank")
        ctx_free = sem("ctx_free")
        h_bank = sem("h_bank")
        h_hi = sem("h_hi")
        h_lo = sem("h_lo")
        y_bank = sem("y_bank")
        y_free = sem("y_free")
        q_store = [sem(f"q_store{j}") for j in range(2)]
        y_store = [sem(f"y_store{j}") for j in range(2)]
        for_phase(2)
        edge_load = {n: sem(f"edge_load_{n}") for n in ("src", "dst", "next", "all")}
        next_clear = sem("next_clear")
        edge_f = sem("edge_f")
        e_staged = sem("e_staged")
        e_var = sem("e_var")
        e_rstd0 = sem("e_rstd0")
        e_xn = sem("e_xn")
        e_bank = sem("e_bank")
        e_src_out = sem("e_src_out")
        e_dst_out = sem("e_dst_out")
        lg_bank = sem("lg_bank")
        lg_out = sem("lg_out")
        st_hi = sem("st_hi")
        st_lo = sem("st_lo")
        hm_bank = sem("hm_bank")
        m_self = sem("m_self")
        m_sum = sem("m_sum")
        m_hi = sem("m_hi")
        m_lo = sem("m_lo")
        mask_set = sem("mask_set")
        ag_bank = sem("ag_bank")
        ag_out = sem("ag_out")
        ag_hi = sem("ag_hi")
        ag_lo = sem("ag_lo")
        ye_bank = sem("ye_bank")
        ye_out = sem("ye_out")
        pool_scat = sem("pool_scat")
        tok_init = sem("tok_init")
        no_tok = sem("no_tok")
        sc_sub_1 = sem("sc_sub_1")
        sc_exp_1 = sem("sc_exp_1")
        sc_done_1 = sem("sc_done_1")
        al_bank_1 = sem("al_bank_1")
        al_out_1 = sem("al_out_1")
        for_phase(3)
        att2_load = sem("att2_load")
        g2_staged = sem("g2_staged")
        g2_copied = sem("g2_copied")
        p2_pool = sem("p2_pool")
        logit2_set = sem("logit2_set")
        lt_bank = sem("lt_bank")
        lt_out = sem("lt_out")
        m2s_set = sem("m2s_set")
        m2_set = sem("m2_set")
        m2_hi = sem("m2_hi")
        m2_lo = sem("m2_lo")
        z_bank = sem("z_bank")
        mask2_set = sem("mask2_set")
        z_hi = sem("z_hi")
        z_lo = sem("z_lo")
        z_staged = sem("z_staged")
        sc_sub_2 = sem("sc_sub_2")
        sc_exp_2 = sem("sc_exp_2")
        sc_done_2 = sem("sc_done_2")
        al_bank_2 = sem("al_bank_2")
        al_out_2 = sem("al_out_2")
        sc_sub = (sc_sub_1, sc_sub_2)
        sc_exp = (sc_exp_1, sc_exp_2)
        sc_done = (sc_done_1, sc_done_2)
        al_bank = (al_bank_1, al_bank_2)
        al_out = (al_out_1, al_out_2)
        for_phase(4)
        p4_load = sem("p4_load")
        p4_bias = sem("p4_bias")
        p4_sw = sem("p4_sw")
        p4_sb = sem("p4_sb")
        p4_bv = sem("p4_bv")
        wp_bank = sem("wp_bank")
        wp_hi = sem("wp_hi")
        wp_lo = sem("wp_lo")
        sw_bank = sem("sw_bank")
        sw_out = sem("sw_out")
        ctx_ready = sem("ctx_ready")
        b_added = sem("b_added")
        qt_bank = sem("qt_bank")
        qt_hi = sem("qt_hi")
        qt_lo = sem("qt_lo")
        num_bank = sem("num_bank")
        num_out = sem("num_out")
        o_set = sem("o_set")
        ot_bank = sem("ot_bank")
        ot_hi = sem("ot_hi")
        ot_lo = sem("ot_lo")
        mix_bank = sem("mix_bank")
        x1_set = sem("x1_set")
        y_max = sem("y_max")
        lse_set = sem("lse_set")
        v4_set = sem("v4_set")
        r4_set = sem("r4_set")
        ln4_set = sem("ln4_set")
        xf_set = sem("xf_set")
        xft_bank = sem("xft_bank")
        xft_out = sem("xft_out")
        rt_bank = sem("rt_bank")
        rt_max = sem("rt_max")
        rt_exp = sem("rt_exp")
        oh_set = sem("oh_set")
        pf_bank = sem("pf_bank")
        row_set = sem("row_set")
        row_free = sem("row_free")
        const4 = sem("const4")
        rank_set = sem("rank_set")
        x4_load = [sem(f"x4_load{j}") for j in range(G)]
        y4_load = [sem(f"y4_load{j}") for j in range(G)]
        q4_load = [sem(f"q4_load{j}") for j in range(G)]
        x1_store = [sem(f"x1_store{j}") for j in range(G)]
        for_phase(5)
        tok_load = sem("tok_load")
        tok_set = sem("tok_set")
        we_bank = sem("we_bank")
        we_hi = sem("we_hi")
        we_lo = sem("we_lo")
        x5_set = sem("x5_set")
        f_bank = sem("f_bank")
        f_hi = sem("f_hi")
        f_lo = sem("f_lo")
        y5_bank = sem("y5_bank")
        y5_out = sem("y5_out")
        res_set = sem("res_set")
        idx5_set = sem("idx5_set")
        to_set = sem("to_set")
        we_load = [sem(f"we_load{j}") for j in range(2)]
        eb_load = [sem(f"eb_load{j}") for j in range(2)]
        for_phase(None)

        CONSTS = 9
        LINKS4 = 4 + 1 + 4 + 3 + 1 + 6
        DVE_LINKS = 2 + 4 + 2 * SUBS

        def refine(dve, chain, r, v, tmp):
            chain.link(nc.vector.tensor_tensor(tmp[:, 0, :], r, r, ALU.mult))
            chain.link(nc.vector.tensor_tensor(tmp[:, 0, :], tmp[:, 0, :], v, ALU.mult))
            chain.link(nc.vector.tensor_scalar(tmp[:, 0, :], tmp[:, 0, :], -0.5, 1.5, ALU.mult, ALU.add))
            chain.link(nc.vector.tensor_tensor(r, r, tmp[:, 0, :], ALU.mult))

        def add_context(dve, chain, sub0, s):
            dve.wait_ge(ctx_bank, sub0 + (s + 1))
            dve.wait_ge(ctx_free, sub0 * 2 + (2 * s + 2))
            nc.vector.tensor_tensor(ctx_acc[:, :, :], groups(banks[6][:, :], DC), ctx_acc[:, :, :], ALU.add).then_inc(ctx_free, 1)
            nc.vector.tensor_tensor(ksum_acc[:, :, :], groups(banks[7][:, 0:2 * DC], DC), ksum_acc[:, :, :],
                                    ALU.add).then_inc(ctx_free, 1)

        def phase_end(eng, n):
            eng.drain().then_inc(phase_done, 1)
            eng.wait_ge(phase_done, 5 * n)
            if eng is nc.gpsimd:
                eng.sem_clear(range(shared[n % 2][0], shared[n % 2][-1] + 1))

        def edge_softmax(dve, chain, layer):
            for t in (head_e, head_s):
                chain.link(nc.vector.scalar_tensor_tensor(out=t[:, :], in0=t[:, :], scalar=0.2, in1=t[:, :],
                                                          op0=ALU.mult, op1=ALU.max))
            chain.link(nc.vector.tensor_tensor(same[:, :], dst_bc[0:HEADS, 1:E + 2], dst_bc[0:HEADS, 0:E + 1], ALU.is_equal))
            chain.link(nc.vector.tensor_scalar(wall[:, :], same[:, :], 1e30, -1e30, ALU.mult, ALU.add))
            chain.link(nc.vector.tensor_tensor_scan(run[:, :], wall[:, 0:E], head_e[:, :], -1e30, ALU.add, ALU.max))
            chain.link(nc.vector.tensor_tensor_scan(run[:, ::-1], wall[:, :0:-1], run[:, ::-1], -1e30, ALU.add, ALU.max))
            chain.link(nc.vector.tensor_tensor(run[:, :], run[:, :], head_s[:, :], ALU.max))
            for t in (head_e, head_s):
                last = nc.vector.tensor_tensor(t[:, :], t[:, :], run[:, :], ALU.subtract)
                last.then_inc(sc_sub[layer], 1)
            dve.wait_ge(sc_exp[layer], 2)
            chain.link(nc.vector.tensor_tensor_scan(run[:, :], same[:, 0:E], head_e[:, :], 0.0, ALU.mult, ALU.add))
            chain.link(nc.vector.tensor_scalar(wall[:, :], same[:, :], -1.0, 1.0, ALU.mult, ALU.add))
            chain.link(nc.vector.tensor_tensor(run[:, :], run[:, :], wall[:, 1:E + 1], ALU.mult))
            chain.link(nc.vector.tensor_tensor_scan(run[:, ::-1], same[:, :0:-1], run[:, ::-1], 0.0, ALU.mult, ALU.add))
            chain.link(nc.vector.scalar_tensor_tensor(out=run[:, :], in0=run[:, :], scalar=1e-16, in1=head_s[:, :],
                                                      op0=ALU.add, op1=ALU.add))
            chain.link(nc.vector.reciprocal(run[:, :], run[:, :]))
            chain.link(nc.vector.tensor_tensor(head_s[:, :], head_s[:, :], wall[:, 0:E], ALU.mult))
            nc.vector.tensor_tensor(head_e[:, :], head_e[:, :], run[:, :], ALU.mult).then_inc(sc_done[layer], 1)
            nc.vector.tensor_tensor(head_s[:, :], head_s[:, :], run[:, :], ALU.mult).then_inc(sc_done[layer], 1)

        def exp_logits(act, layer):
            for n, t in enumerate((head_e, head_s)):
                act.wait_ge(sc_sub[layer], n + 1)
                nc.scalar.activation(t[:, :], t[:, :], ACT.Exp).then_inc(sc_exp[layer], 1)

        def weights_by_edge(pe, layer):
            for n, t in enumerate((head_e, head_s)):
                pe.wait_ge(sc_done[layer], n + 1)
                for k in range(ET):
                    last = nc.tensor.transpose(banks[n][0:ROWS, k * HEADS:(k + 1) * HEADS],
                                               t[:, k * ROWS:(k + 1) * ROWS], ident[0:HEADS, 0:HEADS])
                last.then_inc(al_bank[layer], 1)

        def take_weights(act, layer):
            for n, t in enumerate((alpha_e, alpha_s)):
                act.wait_ge(al_bank[layer], n + 1)
                nc.scalar.activation(t[:, :, :], groups(banks[n][0:ROWS, 0:ET * HEADS], ET), ACT.Copy).then_inc(al_out[layer], 1)

        block = ctx.enter_context(nc.Block())

        @block.sync
        def _(sp):
            for n, w, st in (("k", Wk, wk_st), ("v", Wv, wv_st), ("q", Wq, wq_st)):
                sp.dma_start(st[:, :, :], w.rearrange("(c p) i -> p c i", p=P)).then_inc(wload[n], 16)
            sp.dma_start(xn[:, :, :], x[0:MACRO, :].rearrange("(s p) d -> p s d", p=ROWS)).then_inc(x_load, 16)
            sp.dma_start(w1_st[:, :, :], W1.rearrange("(c p) i -> p c i", p=P)).then_inc(wload["W1"], 16)
            sp.dma_start(w2_st[:, :, :], W2.rearrange("(c p) i -> p c i", p=P)).then_inc(wload["W2"], 16)
            for j in range(2):
                sp.sem_inc(q_store[j], 16)

            def store_q(m):
                for s in range(SUBS):
                    sp.wait_ge(snorm_q, m * SUBS + (s + 1))
                    sp.sem_inc(sp_settled, 1)
                    sp.dma_start(q_table[bass.ds((m * SUBS + s) * ROWS, ROWS), :],
                                 qbuf[:, s % 2, :]).then_inc(q_store[s % 2], 16)

            with sp.Fori(0, MACROS - 1) as m:
                store_q(m)
                sp.wait_ge(xt_bank, m * SUBS + SUBS)
                sp.sem_inc(sp_settled, 1)
                sp.dma_start(xn[:, :, :], x[bass.ds(m * MACRO + MACRO, MACRO), :]
                             .rearrange("(s p) d -> p s d", p=ROWS)).then_inc(x_load, 16)
            store_q(MACROS - 1)
            for j in range(2):
                sp.wait_ge(q_store[j], 16 * (MACROS * SUBS // 2 + 1))
            phase_end(sp, 1)
            slow = dict(allow_slow_non_contiguous=True)
            sp.wait_ge(no_tok, 1)
            sp.dma_start(token_of_slot.rearrange("(p s) o -> p (s o)", p=P), no_token[:, :]).then_inc(tok_init, 16)
            sp.wait_ge(tok_init, 16)
            sp.dma_start(src_i[:, :], src.rearrange("(t p) -> p t", p=ROWS), **slow).then_inc(edge_load["src"], 16)
            sp.dma_start(dst_i[:, :], dst.rearrange("(t p) -> p t", p=ROWS), **slow).then_inc(edge_load["dst"], 16)
            sp.dma_start(dst_bi[:, :], dst.partition_broadcast(P)).then_inc(edge_load["all"], 16)
            sp.wait_ge(next_clear, 1)
            sp.dma_start(next_i[:, 0:ET - 1], dst[1:1 + (ET - 1) * ROWS].rearrange("(t p) -> p t", p=ROWS),
                         **slow).then_inc(edge_load["next"], 16)
            sp.dma_start(next_i[0:ROWS - 1, ET - 1:ET], dst[E - ROWS + 1:E].rearrange("(p t) -> p t", t=1),
                         **slow).then_inc(edge_load["next"], 16)
            phase_end(sp, 2)
            for r, a in enumerate((att_src2, att_dst2)):
                sp.dma_start(att2_bc[:, r, :], a.rearrange("h c -> (h c)").partition_broadcast(ROWS)).then_inc(att2_load, 16)
            phase_end(sp, 3)
            sp.dma_start(wp_st[:, :, :], Wp.rearrange("(c p) i -> p c i", p=P)).then_inc(p4_load, 16)
            sp.dma_start(bv_bc[:, :], bv.partition_broadcast(P)).then_inc(p4_bv, 16)
            sp.dma_start(sw_st[:, :], switch_w).then_inc(p4_sw, 16)
            for d, b in ((bp_bc, bp), (b2_bc, b2)):
                sp.dma_start(d[:, :], b.partition_broadcast(ROWS)).then_inc(p4_bias, 16)
            sp.dma_start(sb_bc[:, :], switch_b.partition_broadcast(ROWS)).then_inc(p4_sb, 16)
            for j in range(G):
                sp.sem_inc(x1_store[j], 16)

            def load_nodes(q, r):
                t = q * G + r
                if not isinstance(t, int):
                    sp.wait_ge(o_set, t - (G - 1))
                    sp.sem_inc(sp_settled, 1)
                    sp.wait_ge(x1_set, t - (G - 2))
                    sp.sem_inc(sp_settled, 1)
                rows = bass.ds(t * ROWS, ROWS)
                for d, s_, done in ((q_in, q_table, q4_load), (x_in, x, x4_load), (y_in, y2_table, y4_load)):
                    sp.dma_start(d[:, r, :], s_[rows, :]).then_inc(done[r], 16)

            def store_x1(q, r):
                sp.wait_ge(row_set, q * G + (r + 1))
                sp.sem_inc(sp_settled, 1)
                sp.dma_start(x1_table[bass.ds((q * G + r) * ROWS, ROWS), :], x1row[:, r, :]).then_inc(x1_store[r], 16)

            in_step(sp, MACROS * SUBS, G, [(load_nodes, 0), (store_x1, 4)])
            for j in range(G):
                sp.wait_ge(x1_store[j], 16 * (MACROS * SUBS // G + 1))
            phase_end(sp, 4)
            sp.dma_start(tok_i[:, :], token_of_slot.rearrange("(p s) o -> p (s o)", p=P)).then_inc(tok_load, 16)

            def load_expert(q, r):
                if r % SLOTS:
                    return
                e, j = q * 2 + r // SLOTS, r // SLOTS
                if not isinstance(e, int):
                    sp.wait_ge(we_bank, e * DC - DC)
                    sp.sem_inc(sp_settled, 1)
                    sp.wait_ge(y5_out, e * SLOTS - SLOTS + 2)
                    sp.sem_inc(sp_settled, 1)
                sp.dma_start(we_st[:, j, :, :], expert_w[bass.ds(e, 1), :, :].rearrange("o (c p) i -> p (o c) i", p=P))\
                  .then_inc(we_load[j], 16)
                sp.dma_start(eb_bc[:, j, :], expert_b[bass.ds(e, 1), :].rearrange("o f -> (o f)").partition_broadcast(P))\
                  .then_inc(eb_load[j], 16)

            in_step(sp, SL, 2 * SLOTS, [(load_expert, 0)])

        @block.gpsimd
        def _(pool):
            chain = Chain(pool, pool_chain)
            settle = lambda: pool.sem_inc(pool_settled, 1)
            chain.link(nc.gpsimd.memset(ident[:, :], 0.0))
            nc.gpsimd.affine_select(out=ident[:, :], in_=ident[:, :], compare_op=ALU.not_equal, fill=1.0, base=0,
                                    pattern=[[-1, P]], channel_multiplier=1).then_inc(const_done, 1)
            nc.gpsimd.memset(ones_bf[:, :], 1.0).then_inc(const_done, 1)
            chain.link(nc.gpsimd.memset(before[:, :], 1.0))
            nc.gpsimd.affine_select(out=before[:, :], in_=before[:, :], compare_op=ALU.is_gt, fill=0.0, base=0,
                                    pattern=[[1, ROWS]], channel_multiplier=-1).then_inc(const_done, 1)
            nc.gpsimd.memset(ones_f[:, :], 1.0).then_inc(const_done, 1)
            nc.gpsimd.memset(minus_half[:, :], -0.5).then_inc(const_done, 1)
            chain.link(nc.gpsimd.memset(last_row[:, :], 0.0))
            nc.gpsimd.affine_select(out=last_row[:, :], in_=last_row[:, :], compare_op=ALU.not_equal, fill=1.0,
                                    base=1 - ROWS, pattern=[[0, 1]], channel_multiplier=1).then_inc(const_done, 1)
            nc.gpsimd.memset(ctx_acc[:, :, :], 0.0).then_inc(const_done, 1)
            nc.gpsimd.memset(ksum_acc[:, :, :], 0.0).then_inc(const_done, 1)
            nc.gpsimd.memset(att1[:, :, :], 0.0).then_inc(const_done, 1)
            pool.wait_ge(const_done, CONSTS)
            pool.wait_ge(w_hi, 2)
            nc.gpsimd.tensor_tensor(W2l[:, :, :], w2_st[:, :, :], W2h[:, :, :].bitcast(F32),
                                    ALU.subtract).then_inc(w2_lo, 1)
            with pool.Fori(0, MACROS) as m:
                sub0 = pool.snap(m * SUBS)
                pool.wait_ge(var_ready, m + 1)
                settle()
                nc.gpsimd.tensor_tensor(rstd[:, :], veps[:, :], minus_half[:, :], ALU.pow).then_inc(rstd0, 1)
                for s in range(SUBS):
                    j = s % 2
                    for n, buf in ((0, kbuf), (1, qbuf)):
                        pool.wait_ge(smax, sub0 * 2 + (2 * s + n + 1))
                        nc.gpsimd.tensor_tensor(groups(buf[:, j, :], HEADS), groups(buf[:, j, :], HEADS),
                                                spread(kq_max[:, j, n, :], HD), ALU.subtract).then_inc(ssub, 1)
                    for n, buf, done in ((0, kbuf, snorm_k), (1, qbuf, snorm_q)):
                        pool.wait_ge(srec, sub0 * 2 + (2 * s + n + 1))
                        nc.gpsimd.tensor_tensor(groups(buf[:, j, :], HEADS), groups(buf[:, j, :], HEADS),
                                                spread(kq_rec[:, j, n, :], HD), ALU.mult).then_inc(done, 1)
                    for f in (2 * s, 2 * s + 1):
                        pool.wait_ge(h_hi, sub0 * 2 + (f + 1))
                        nc.gpsimd.tensor_tensor(h1l[:, f, :], relu[:, f % 2, :], h1h[:, f, :].bitcast(F32),
                                                ALU.subtract).then_inc(h_lo, 1)

            phase_end(pool, 1)
            nc.gpsimd.memset(no_token[:, :], FAR).then_inc(no_tok, 1)
            nc.gpsimd.memset(next_i[:, :], -1).then_inc(next_clear, 1)
            pool.wait_ge(edge_load["src"], 16)
            pool.wait_ge(edge_load["dst"], 16)
            with pool.Fori(0, ET // 2) as i:
                for j in range(2):
                    t = i * 2 + j
                    if j == 0:
                        pair = pool.snap(i * 2)
                    pool.wait_ge(e_bank, pair * 2 + (2 * j + 2))
                    settle()
                    for r, idx in enumerate((src_i, dst_i)):
                        nc.gpsimd.tensor_copy(e_idx[:, j, r:r + 1], idx[:, bass.ds(t, 1)]).then_inc(e_staged, 1)
                    pool.wait_ge(e_staged, pair * 2 + (2 * j + 2))
                    settle()
                    for r in range(2):
                        pool.indirect_dma_start(gath[:, j, r, :], None, x, bass.IndirectOffsetOnAxis(
                            e_idx[:, j, r:r + 1].bitcast(U32), 0)).then_inc(e_gath[j], 16)
                for j in range(2):
                    pool.wait_ge(e_var, pair + (j + 1))
                    settle()
                    nc.gpsimd.tensor_tensor(e_rstd[:, :], e_veps[:, :], minus_half[:, 0:2], ALU.pow).then_inc(e_rstd0, 1)

            def stage_low(t):
                for r, xT in enumerate((xsT, xdT)):
                    pool.wait_ge(st_hi, t * 2 + (r + 1))
                    nc.gpsimd.tensor_tensor(xsl[:, r, :, :], xT[:, :, bass.ds(t * ROWS, ROWS)],
                                            xsh[:, r, :, :].bitcast(F32), ALU.subtract).then_inc(st_lo, 1)

            def message_low(t):
                for h in range(2):
                    pool.wait_ge(m_self, t * 2 + (h + 1))
                    settle()
                    nc.gpsimd.tensor_tensor(msg[:, h, :], msg[:, h, :], msg_self[:, h, :], ALU.add).then_inc(m_sum, 1)
                    pool.wait_ge(m_hi, t * 2 + (h + 1))
                    nc.gpsimd.tensor_tensor(msgl[:, h * D:(h + 1) * D], msg[:, h, :],
                                            msgh[:, h * D:(h + 1) * D].bitcast(F32), ALU.subtract).then_inc(m_lo, 1)

            def scatter_rows(t):
                pool.wait_ge(ag_hi, t + 1)
                nc.gpsimd.tensor_tensor(aggl[:, :, :], aggT[:, :, :], aggh[:, :, :].bitcast(F32), ALU.subtract).then_inc(ag_lo, 1)
                pool.wait_ge(ye_out, t + 2)
                settle()
                nc.gpsimd.tensor_copy(scat_st[:, 0:1], scat_i[:, bass.ds(t, 1)]).then_inc(pool_scat, 1)
                pool.wait_ge(pool_scat, t + 1)
                settle()
                pool.indirect_dma_start(y2_table, bass.IndirectOffsetOnAxis(scat_st[:, 0:1].bitcast(U32), 0), y_edge[:, :],
                                        None, bounds_check=N - 1, oob_is_err=False).then_inc(ye_store, 16)

            stage_low(0)
            with pool.Fori(0, ET - 1) as t:
                message_low(t)
                stage_low(t + 1)
                scatter_rows(t)
            message_low(ET - 1)
            scatter_rows(ET - 1)
            pool.wait_ge(ye_store, 16 * ET)
            phase_end(pool, 2)
            pool.wait_ge(att2_load, 32)
            with pool.Fori(0, ET // 2) as i:
                pair = pool.snap(i * 2)
                for j in range(2):
                    pool.wait_ge(g2_copied, pair + (j + 1))
                    pool.wait_ge(logit2_set, pair + (j + 1))
                    settle()
                    for r, idx in enumerate((src_i, dst_i)):
                        nc.gpsimd.tensor_copy(idx2[:, j, r:r + 1], idx[:, bass.ds(i * 2 + j, 1)]).then_inc(g2_staged, 1)
                    pool.wait_ge(g2_staged, pair * 2 + (2 * j + 2))
                    settle()
                    for r in range(2):
                        pool.indirect_dma_start(g2[:, j, r, :], None, y2_table, bass.IndirectOffsetOnAxis(
                            idx2[:, j, r:r + 1].bitcast(U32), 0)).then_inc(g2_load[j], 16)
                for j in range(2):
                    pool.wait_ge(g2_load[j], i * 32 + 32)
                    pool.wait_ge(logit2_set, pair + (j + 2))
                    settle()
                    nc.gpsimd.tensor_tensor(prod2[:, 2, :], g2[:, j, 1, :], att2_bc[:, 1, :], ALU.mult).then_inc(p2_pool, 1)
            with pool.Fori(0, ET // 2) as i:
                pair = pool.snap(i * 2)
                for j in range(2):
                    pool.wait_ge(al_out[1], 2)
                    pool.wait_ge(m2_set, pair + (j + 1))
                    settle()
                    nc.gpsimd.tensor_tensor(groups(m2s[:, j, :], HEADS), groups(yd_all[:, bass.ds(i * 2 + j, 1), :]
                                            .rearrange("p t d -> p (t d)"), HEADS),
                                            spread(alpha_s[:, bass.ds(i * 2 + j, 1), :].rearrange("p t h -> p (t h)"), HD),
                                            ALU.mult).then_inc(m2s_set, 1)
                    pool.wait_ge(m2_hi, pair + (j + 1))
                    nc.gpsimd.tensor_tensor(m2l[:, j, :], m2[:, j, :], m2h[:, j, :].bitcast(F32), ALU.subtract).then_inc(m2_lo, 1)
                    pool.wait_ge(z_hi, pair * 2 + (2 * j + 1))
                    settle()
                    nc.gpsimd.tensor_copy(scat2[:, j:j + 1], scat_i[:, bass.ds(i * 2 + j, 1)]).then_inc(z_staged, 1)
                    pool.wait_ge(z_staged, pair + (j + 1))
                    settle()
                    pool.indirect_dma_start(y2_table, bass.IndirectOffsetOnAxis(scat2[:, j:j + 1].bitcast(U32), 0), z32[:, j, :],
                                            None, bounds_check=N - 1, oob_is_err=False).then_inc(z_store[j], 16)
                for j in range(2):
                    pool.wait_ge(z_store[j], i * 16 + 16)
                    settle()
            phase_end(pool, 3)
            nc.gpsimd.iota(iota_f[:, :], pattern=[[1, EXPERTS]], base=0, channel_multiplier=0).then_inc(const4, 1)
            nc.gpsimd.iota(row_0[:, :], pattern=[[0, 1]], base=0, channel_multiplier=1).then_inc(const4, 1)
            nc.gpsimd.iota(steps_i[:, :], pattern=[[P, steps_i.shape[1]]], base=P, channel_multiplier=0).then_inc(const4, 1)
            pool.wait_ge(p4_bias, 32)
            NT = MACROS * SUBS

            def add_biases(q, r):
                for d, b, done in ((y_in, b2_bc, y4_load), (x_in, bp_bc, x4_load)):
                    pool.wait_ge(done[r], q * 16 + 16)
                    settle()
                    nc.gpsimd.tensor_tensor(d[:, r, :], d[:, r, :], b[:, :], ALU.add).then_inc(b_added, 1)

            def start_rstd(q, r):
                pool.wait_ge(v4_set, q * G + (r + 1))
                nc.gpsimd.tensor_tensor(r4[:, r % 2, :], veps4[:, r % 2, :], minus_half[:, 0:1], ALU.pow).then_inc(r4_set, 1)

            def add_q(q, r):
                pool.wait_ge(num_out, q * G + (r + 2))
                nc.gpsimd.tensor_tensor(attn[:, r % 2, :], attn[:, r % 2, :], q_in[:, r, :], ALU.add).then_inc(o_set, 1)

            def send_tokens(q, r):
                t, j = q * G + r, r % 2
                pool.wait_ge(row_set, t + 1)
                if r or not isinstance(t, int):
                    for store in (tok_store, orow_store):
                        pool.wait_ge(store[1 - j], q * 32 + 16 * ((r + 1) // 2))
                pool.sem_inc(row_free, 1)
                pool.indirect_dma_start(token_of_slot, bass.IndirectOffsetOnAxis(slot_i[:, j:j + 1].bitcast(U32), 0),
                                        token_i[:, j:j + 1], None, bounds_check=P * SL - 1, oob_is_err=False)\
                    .then_inc(tok_store[j], 16)
                pool.indirect_dma_start(out, bass.IndirectOffsetOnAxis(row_i[:, j:j + 1].bitcast(U32), 0), orow[:, j, :],
                                        None, bounds_check=N - 1, oob_is_err=False).then_inc(orow_store[j], 16)

            in_step(pool, NT, G, [(add_biases, 0), (start_rstd, 1), (add_q, 0), (send_tokens, 3)])
            for j in range(2):
                pool.wait_ge(tok_store[j], 16 * (NT // 2))
                pool.wait_ge(orow_store[j], 16 * (NT // 2))
            phase_end(pool, 4)
            pool.wait_ge(tok_set, 1)

            def gather_rows(q, r):
                u, j = q * (2 * SLOTS) + r, r % 2
                if not isinstance(u, int) or u >= 2:
                    pool.wait_ge(res_set, u - 1)
                    settle()
                nc.gpsimd.tensor_copy(from_st[:, j:j + 1], from_i[:, bass.ds(u, 1)]).then_inc(idx5_set, 1)
                pool.wait_ge(idx5_set, u + 1)
                settle()
                pool.indirect_dma_start(row5[:, j, :], None, x1_table, bass.IndirectOffsetOnAxis(
                    from_st[:, j:j + 1].bitcast(U32), 0)).then_inc(row5_load[j], 16)

            def scatter_results(q, r):
                u, j = q * (2 * SLOTS) + r, r % 2
                pool.wait_ge(res_set, u + 1)
                settle()
                nc.gpsimd.tensor_copy(to_st[:, j:j + 1], tok_i[:, bass.ds(u, 1)]).then_inc(to_set, 1)
                pool.wait_ge(to_set, u + 1)
                settle()
                pool.indirect_dma_start(out, bass.IndirectOffsetOnAxis(to_st[:, j:j + 1].bitcast(U32), 0), res5[:, j, :],
                                        None, bounds_check=N - 1, oob_is_err=False).then_inc(res_store[j], 16)

            in_step(pool, SL, 2 * SLOTS, [(gather_rows, 0), (scatter_results, 3)])
            for j in range(2):
                pool.wait_ge(res_store[j], 16 * (SL // 2))

        @block.scalar
        def _(act):
            chain = Chain(act, act_chain)
            nc.scalar.preload_act_table_set("natural_log_exp_and_others")
            for n, d, s in ((0, bk_bc, bk), (1, bq_bc, bq)):
                act.dma_start(d[:, :], s.partition_broadcast(ROWS)).then_inc(bias_load[n], 16)
            act.dma_start(b1_col[:, :], b1.rearrange("(f p) -> p f", p=P), allow_slow_non_contiguous=True)\
               .then_inc(bias_load[2], 16)
            for r, a in enumerate((att_src1, att_dst1)):
                act.dma_start(att_bc[:, r, :], a.rearrange("h c -> (h c)").partition_broadcast(P))\
                   .then_inc(wload[f"att{r}"], 16)
            for n in range(3 * DC):
                act.wait_ge(wt_bank, n + 1)
                nc.scalar.activation(WTh["kvq"[n // DC]][:, n % DC, :], banks[n % 2][:, :], ACT.Copy).then_inc(wt_hi, 1)
            for n, h, st in (("W1", W1h, w1_st), ("W2", W2h, w2_st)):
                act.wait_ge(wload[n], 16)
                nc.scalar.activation(h[:, :, :], st[:, :, :], ACT.Copy).then_inc(w_hi, 1)
            act.sem_inc(y_free, SUBS)
            for j in range(2):
                act.sem_inc(y_store[j], 16)
            act.wait_ge(bias_load[2], 16)
            act.wait_ge(w_lo, 1)
            act.wait_ge(w2_lo, 1)
            act.wait_ge(att_sum, 2 * DC)
            with act.Fori(0, MACROS) as m:
                sub0 = act.snap(m * SUBS)
                for s in range(SUBS):
                    act.wait_ge(xt_bank, sub0 + (s + 1))
                    nc.scalar.activation(xTh[:, :, s * ROWS:(s + 1) * ROWS],
                                         groups(banks[s % 2][:, 0:MACRO], DC), ACT.Copy).then_inc(xt_hi, 1)
                for s in range(SUBS):
                    j = s % 2
                    act.wait_ge(kvq_bank, sub0 * 3 + (3 * s + 2))
                    nc.scalar.activation(kvh[:, j, 1, :], banks[2 + (3 * s + 1) % 2][0:ROWS, :], ACT.Copy).then_inc(v_hi, 1)
                    for n, buf in ((0, kbuf), (1, qbuf)):
                        act.wait_ge(ssub, sub0 * 2 + (2 * s + n + 1))
                        nc.scalar.activation(buf[:, j, :], buf[:, j, :], ACT.Exp).then_inc(sexp, 1)
                    for f in (2 * s, 2 * s + 1):
                        act.wait_ge(h_bank, sub0 * 2 + (f + 1))
                        nc.scalar.activation(relu[:, f % 2, :], banks[4 + f % 2][:, 0:MACRO], ACT.Relu,
                                             bias=b1_col[:, f:f + 1])
                        nc.scalar.activation(h1h[:, f, :], banks[4 + f % 2][:, 0:MACRO], ACT.Relu,
                                             bias=b1_col[:, f:f + 1]).then_inc(h_hi, 1)
                    act.wait_ge(snorm_k, sub0 + (s + 1))
                    nc.scalar.activation(kvh[:, j, 0, :], kbuf[:, j, :], ACT.Copy).then_inc(k_hi, 1)
                for s in range(SUBS):
                    j = s % 2
                    act.wait_ge(y_store[j], m * 32 + (16 * (s // 2) + 16))
                    act.wait_ge(y_bank, sub0 + (s + 1))
                    ins = nc.scalar.activation(y2o[:, j, :], banks[2 + j][0:ROWS, :], ACT.Copy)
                    ins.then_inc(y_free, 1)
                    act.wait_ge(y_free, sub0 + (s + 1 + SUBS))
                    act.dma_start(y2_table[bass.ds((m * SUBS + s) * ROWS, ROWS), :], y2o[:, j, :]).then_inc(y_store[j], 16)
            for j in range(2):
                act.wait_ge(y_store[j], 16 * (MACROS * SUBS // 2 + 1))

            phase_end(act, 1)
            act.sem_inc(e_src_out, 1)
            with act.Fori(0, ET) as t:
                act.wait_ge(e_bank, t * 2 + 5)
                nc.scalar.activation(xsT[:, :, bass.ds(t * ROWS, ROWS)], groups(banks[0][:, 0:MACRO], DC), ACT.Copy)\
                  .then_inc(e_src_out, 1)
            for b in range(E // MACRO):
                act.wait_ge(lg_bank, b + 1)
                c = slice(b * MACRO, (b + 1) * MACRO)
                nc.scalar.activation(head_e[:, c], banks[2 + b % 2][0:HEADS, 0:MACRO], ACT.Copy)
                nc.scalar.activation(head_s[:, c], banks[2 + b % 2][32:32 + HEADS, 0:MACRO], ACT.Copy).then_inc(lg_out, 1)
            exp_logits(act, 0)
            take_weights(act, 0)
            act.wait_ge(al_out[0], 2)

            def stage_high(t):
                for r, xT in enumerate((xsT, xdT)):
                    nc.scalar.activation(xsh[:, r, :, :], xT[:, :, bass.ds(t * ROWS, ROWS)], ACT.Copy).then_inc(st_hi, 1)

            def message_high(t):
                for h in range(2):
                    act.wait_ge(m_sum, t * 2 + (h + 1))
                    nc.scalar.activation(msgh[:, h * D:(h + 1) * D], msg[:, h, :], ACT.Copy).then_inc(m_hi, 1)

            def aggregate_out(t, first=False):
                act.wait_ge(ag_out, t + 1)
                nc.scalar.activation(aggh[:, :, :], aggT[:, :, :], ACT.Copy).then_inc(ag_hi, 1)
                act.wait_ge(ye_bank, t + 1)
                if not first:
                    act.wait_ge(ye_store, t * 16)
                nc.scalar.activation(y_edge[:, :], banks[6][0:ROWS, :], ACT.Copy).then_inc(ye_out, 1)

            act.sem_inc(ye_out, 1)
            stage_high(0)
            message_high(0)
            stage_high(1)
            aggregate_out(0, first=True)
            with act.Fori(1, ET - 1) as t:
                message_high(t)
                stage_high(t + 1)
                aggregate_out(t)
            message_high(ET - 1)
            aggregate_out(ET - 1)
            phase_end(act, 2)
            act.sem_inc(g2_copied, 2)
            act.sem_inc(lt_out, 2)
            with act.Fori(0, ET // 2) as i:
                pair = act.snap(i * 2)
                for j in range(2):
                    act.wait_ge(g2_load[j], i * 32 + 32)
                    for r, all_ in enumerate((ys_all, yd_all)):
                        last = nc.scalar.activation(all_[:, bass.ds(i * 2 + j, 1), :].rearrange("p t d -> p (t d)"), g2[:, j, r, :],
                                                    ACT.Copy)
                    last.then_inc(g2_copied, 1)
                    act.wait_ge(lt_bank, pair + (j + 3))
                    col = bass.ds((i * 2 + j) * ROWS, ROWS)
                    nc.scalar.activation(head_e[:, col], banks[j][0:HEADS, 0:ROWS], ACT.Copy)
                    nc.scalar.activation(head_s[:, col], banks[j][0:HEADS, P:P + ROWS], ACT.Copy).then_inc(lt_out, 1)
            exp_logits(act, 1)
            take_weights(act, 1)
            with act.Fori(0, ET // 2) as i:
                pair = act.snap(i * 2)
                for j in range(2):
                    act.wait_ge(m2_set, pair + (j + 3))
                    nc.scalar.activation(m2h[:, j, :], m2[:, j, :], ACT.Copy).then_inc(m2_hi, 1)
                    act.wait_ge(z_bank, pair + (j + 1))
                    nc.scalar.activation(z32[:, j, :], banks[j][0:ROWS, :], ACT.Copy).then_inc(z_hi, 1)
                    nc.scalar.activation(zh[:, j, :], banks[j][0:ROWS, :], ACT.Copy).then_inc(z_hi, 1)
            phase_end(act, 3)
            for n in range(DC):
                act.wait_ge(wp_bank, n + 1)
                nc.scalar.activation(WpTh[:, n, :], banks[n % 2][:, :], ACT.Copy).then_inc(wp_hi, 1)
            act.wait_ge(sw_bank, 1)
            nc.scalar.activation(swT[:, :, :], groups(banks[2][:, 0:DC * EXPERTS], DC), ACT.Copy).then_inc(sw_out, 1)
            act.sem_inc(xft_out, 1)
            NT = MACROS * SUBS

            def q_high(q, r):
                act.wait_ge(qt_bank, q * G + (r + 1))
                nc.scalar.activation(qTh[:, r % 2, :, :], groups(banks[0][:, 0:MACRO], DC), ACT.Copy).then_inc(qt_hi, 1)

            def normalise(q, r):
                act.wait_ge(ln4_set, q * G + (r + 1))
                nc.scalar.activation(xf[:, r, :], x1row[:, r, 0:D], ACT.Identity, bias=x1row[:, r, D + 1:D + 2],
                                     scale=x1row[:, r, D:D + 1]).then_inc(xf_set, 1)

            def o_high(q, r):
                act.wait_ge(ot_bank, q * G + (r + 1))
                nc.scalar.activation(oTh[:, r % 2, :, :], groups(banks[3][:, 0:MACRO], DC), ACT.Copy).then_inc(ot_hi, 1)

            def exp_router(q, r):
                act.wait_ge(rt_max, q * G + (r + 1))
                nc.scalar.activation(ex16[:, r % 2, :], lgt[:, r % 2, :], ACT.Exp, bias=lstat[:, r % 2, 0:1],
                                     accum_out=lstat[:, r % 2, 1:2]).then_inc(rt_exp, 1)

            def log_sum(q, r):
                act.wait_ge(y_max, q * G + (r + 1))
                chain.link(nc.scalar.activation(exp_y[:, :], y_in[:, r, :], ACT.Exp, bias=y_stat[:, r % 2, 0:1],
                                                accum_out=y_stat[:, r % 2, 1:2]))
                nc.scalar.activation(y_stat[:, r % 2, 2:3], y_stat[:, r % 2, 1:2], ACT.Ln).then_inc(lse_set, 1)

            def xf_out(q, r):
                act.wait_ge(xft_bank, q * G + (r + 1))
                nc.scalar.activation(xfT[:, r % 2, :, :], groups(banks[5][:, 0:MACRO], DC), ACT.Copy).then_inc(xft_out, 1)

            in_step(act, NT, G, [(q_high, 0), (normalise, 2), (o_high, 1), (exp_router, 3), (log_sum, 1), (xf_out, 2)],
                    chain=chain, links=G)
            phase_end(act, 4)
            def expert_high(q, r):
                if r % SLOTS:
                    return
                e, j = q * 2 + r // SLOTS, r // SLOTS
                for c in range(DC):
                    act.wait_ge(we_bank, e * DC + (c + 1))
                    nc.scalar.activation(WeTh[:, j, c, :], banks[c % 2][:, :], ACT.Copy).then_inc(we_hi, 1)

            def normal_rows(q, r):
                j = r % 2
                act.wait_ge(row5_load[j], q * (16 * SLOTS) + 16 * (r // 2 + 1))
                nc.scalar.activation(xf5[:, j, :], row5[:, j, 0:D], ACT.Identity, bias=row5[:, j, D + 1:D + 2],
                                     scale=row5[:, j, D:D + 1]).then_inc(x5_set, 1)

            def rows_high(q, r):
                act.wait_ge(f_bank, q * (2 * SLOTS) + (r + 1))
                nc.scalar.activation(fTh[:, r % 2, :, :], groups(banks[2 + r % 2][:, :], DC), ACT.Copy).then_inc(f_hi, 1)

            in_step(act, SL, 2 * SLOTS, [(expert_high, 0), (normal_rows, 1), (rows_high, 1)])

        @block.vector
        def _(dve):
            chain = Chain(dve, dve_chain)
            for n in range(3 * DC):
                dve.wait_ge(wt_hi, n + 1)
                nc.vector.tensor_tensor(WTl["kvq"[n // DC]][:, n % DC, :], banks[n % 2][:, :],
                                        WTh["kvq"[n // DC]][:, n % DC, :].bitcast(F32), ALU.subtract).then_inc(wt_lo, 1)
            dve.wait_ge(w_hi, 1)
            nc.vector.tensor_tensor(W1l[:, :, :], w1_st[:, :, :], W1h[:, :, :].bitcast(F32), ALU.subtract).then_inc(w_lo, 1)
            for r in range(2):
                dve.wait_ge(wload[f"att{r}"], 16)
            dve.wait_ge(const_done, CONSTS)
            for c in range(DC):
                for r in range(2):
                    chain.link(nc.vector.tensor_tensor(att_tmp[:, r, :], w1_st[:, c, :], att_bc[:, r, :], ALU.mult))
                    nc.vector.tensor_reduce(att1[:, c, 40 * r:40 * r + 8], groups(att_tmp[:, r, :], HEADS),
                                            AX.X, ALU.add).then_inc(att_sum, 1)
                    dve.wait_ge(att_sum, c * 2 + r + 1)
            nc.vector.tensor_tensor(att1[:, :, 72:80], att1[:, :, 0:8], att1[:, :, 40:48], ALU.add)
            for n in range(2):
                dve.wait_ge(bias_load[n], 16)
            nc.vector.tensor_copy(ones_r[:, :], ones_f[:, :]).then_inc(ones_done, 1)
            dve.sem_inc(ctx_free, 2)
            dve.wait_ge(w2_lo, 1)
            with dve.Fori(0, MACROS) as m:
                sub0 = dve.snap(m * SUBS)
                chain.enter(m, DVE_LINKS)
                dve.wait_ge(x_load, m * 16 + 16)
                for s in range(SUBS):
                    last = nc.vector.bn_stats(stats[:, s, :], xn[:, s, :])
                chain.link(last, dve_settled)
                for s in range(SUBS):
                    last = nc.vector.bn_aggr(mv[:, s, :], stats[:, s, :])
                chain.link(last)
                nc.vector.tensor_scalar(veps[:, :], mv[:, :, 1], EPS, None, ALU.add).then_inc(var_ready, 1)
                dve.wait_ge(rstd0, m + 1)
                refine(dve, chain, rstd[:, :], veps[:, :], newt)
                for s in range(SUBS):
                    nc.vector.tensor_scalar(xn[:, s, :], xn[:, s, :], mv[:, s, 0:1], rstd[:, s:s + 1],
                                            ALU.subtract, ALU.mult).then_inc(xn_ready, 1)
                for s in range(SUBS):
                    dve.wait_ge(xt_hi, sub0 + (s + 1))
                    nc.vector.tensor_tensor(xTl[:, :, s * ROWS:(s + 1) * ROWS], groups(banks[s % 2][:, 0:MACRO], DC),
                                            xTh[:, :, s * ROWS:(s + 1) * ROWS].bitcast(F32), ALU.subtract).then_inc(xt_lo, 1)
                for s in range(SUBS):
                    j = s % 2
                    for n, buf, bias in ((0, kbuf, bk_bc), (1, qbuf, bq_bc)):
                        dve.wait_ge(kvq_bank, sub0 * 3 + (3 * s + 2 * n + 1))
                        if n:
                            dve.wait_ge(q_store[j], m * 32 + (16 * (s // 2) + 16))
                        nc.vector.tensor_tensor(buf[:, j, :], banks[2 + (3 * s + 2 * n) % 2][0:ROWS, :], bias[:, :],
                                                ALU.add).then_inc(kvq_free, 1)
                        dve.wait_ge(kvq_free, sub0 * 3 + (3 * s + 2 * n + 1))
                        nc.vector.tensor_reduce(kq_max[:, j, n, :], groups(buf[:, j, :], HEADS), AX.X, ALU.max).then_inc(smax, 1)
                        if n == 0:
                            dve.wait_ge(v_hi, sub0 + (s + 1))
                            nc.vector.tensor_tensor(kvl[:, j, 1, :], banks[2 + (3 * s + 1) % 2][0:ROWS, :],
                                                    kvh[:, j, 1, :].bitcast(F32), ALU.subtract).then_inc(kvq_free, 1)
                    for n, buf in ((0, kbuf), (1, qbuf)):
                        dve.wait_ge(sexp, sub0 * 2 + (2 * s + n + 1))
                        chain.link(nc.vector.tensor_reduce(kq_rec[:, j, n, :], groups(buf[:, j, :], HEADS), AX.X, ALU.add))
                        nc.vector.reciprocal(kq_rec[:, j, n, :], kq_rec[:, j, n, :]).then_inc(srec, 1)
                    dve.wait_ge(k_hi, sub0 + (s + 1))
                    nc.vector.tensor_tensor(kvl[:, j, 0, :], kbuf[:, j, :], kvh[:, j, 0, :].bitcast(F32),
                                            ALU.subtract).then_inc(k_lo, 1)
                    if s:
                        add_context(dve, chain, sub0, s - 1)
                add_context(dve, chain, sub0, SUBS - 1)
            chain.leave(MACROS)

            phase_end(dve, 1)
            dve.wait_ge(edge_load["dst"], 16)
            dve.wait_ge(edge_load["next"], 32)
            nc.vector.tensor_copy(dst_f[:, :], dst_i[:, :])
            chain.link(nc.vector.tensor_copy(next_f[:, :], next_i[:, :]))
            chain.link(nc.vector.tensor_tensor(next_f[:, :], dst_f[:, :], next_f[:, :], ALU.is_equal))
            nc.vector.scalar_tensor_tensor(out=scat_i[:, :], in0=next_f[:, :], scalar=float(FAR), in1=dst_f[:, :],
                                           op0=ALU.mult, op1=ALU.add).then_inc(edge_f, 1)
            nc.vector.memset(dst_bc[:, 0:1], -1.0)
            nc.vector.memset(dst_bc[:, E + 1:E + 2], -1.0)
            dve.wait_ge(edge_load["all"], 16)
            chain.link(nc.vector.tensor_copy(dst_bc[:, 1:E + 1], dst_bi[:, :]))
            dve.sem_inc(e_dst_out, 1)
            with dve.Fori(0, ET // 2) as i:
                pair = dve.snap(i * 2)
                chain.enter(i, 2 * 6)
                for j in range(2):
                    dve.wait_ge(e_gath[j], i * 32 + 32)
                    for r in range(2):
                        last = nc.vector.bn_stats(e_stats[:, r, :], gath[:, j, r, :])
                    chain.link(last, dve_settled)
                    for r in range(2):
                        last = nc.vector.bn_aggr(e_mv[:, r, :], e_stats[:, r, :])
                    chain.link(last)
                    nc.vector.tensor_scalar(e_veps[:, :], e_mv[:, :, 1], EPS, None, ALU.add).then_inc(e_var, 1)
                    dve.wait_ge(e_rstd0, pair + (j + 1))
                    refine(dve, chain, e_rstd[:, :], e_veps[:, :], e_newt)
                    for r in range(2):
                        last = nc.vector.tensor_scalar(gath[:, j, r, :], gath[:, j, r, :], e_mv[:, r, 0:1],
                                                       e_rstd[:, r:r + 1], ALU.subtract, ALU.mult)
                    last.then_inc(e_xn, 1)
                for j in range(2):
                    dve.wait_ge(e_bank, pair * 2 + (2 * j + 6))
                    nc.vector.tensor_copy(xdT[:, :, bass.ds((i * 2 + j) * ROWS, ROWS)],
                                          groups(banks[1][:, 0:MACRO], DC)).then_inc(e_dst_out, 1)
            chain.leave(ET // 2)
            dve.wait_ge(lg_out, E // MACRO)
            edge_softmax(dve, chain, 0)
            dve.wait_ge(al_out[0], 2)
            nc.vector.memset(carry[:, :], 0.0)
            nc.vector.memset(same_dst[:, ROWS:ROWS + 1].bitcast(F32), 0.0)
            with dve.Fori(0, ET) as t:
                chain.enter(t, 3)
                for h in range(2):
                    dve.wait_ge(hm_bank, t * 2 + (h + 1))
                    hs = slice(h * HEADS // 2, (h + 1) * HEADS // 2)
                    for d, b, a in ((msg, 2 * h, alpha_e), (msg_self, 2 * h + 1, alpha_s)):
                        last = nc.vector.tensor_tensor(groups(d[:, h, :], HEADS // 2), groups(banks[b][0:ROWS, :], HEADS // 2),
                                                       spread(a[:, bass.ds(t, 1), hs].rearrange("p t h -> p (t h)"), HID),
                                                       ALU.mult)
                    last.then_inc(m_self, 1)
                nc.vector.tensor_scalar(same_dst[:, 0:ROWS], dst_bc[0:ROWS, bass.ds(t * ROWS + 1, ROWS)],
                                        dst_f[:, bass.ds(t, 1)], None, ALU.is_equal).then_inc(mask_set, 1)
                chain.link(nc.vector.tensor_scalar(goes_on[:, :], dst_bc[:, bass.ds(t * ROWS + 1, ROWS)],
                                                   dst_bc[:, bass.ds(t * ROWS, 1)], None, ALU.is_equal))
                dve.wait_ge(ag_bank, t + 1)
                for f in range(FC):
                    c = (f % DC) * (ROWS + 1)
                    last = nc.vector.scalar_tensor_tensor(out=aggT[:, f, :], in0=goes_on[:, :], scalar=carry[:, f:f + 1],
                                                          in1=banks[4 + f // DC][:, c:c + ROWS], op0=ALU.mult, op1=ALU.add)
                chain.link(last)
                chain.link(nc.vector.tensor_copy(carry[:, :], aggT[:, :, ROWS - 1]))
                for f in range(FC):
                    last = nc.vector.tensor_scalar(aggT[:, f, :], aggT[:, f, :], b1_col[:, f:f + 1], 0.0, ALU.add, ALU.max)
                last.then_inc(ag_out, 1)
            chain.leave(ET)
            phase_end(dve, 2)
            dve.wait_ge(att2_load, 32)
            dve.sem_inc(logit2_set, 2)
            dve.sem_inc(m2_set, 2)
            with dve.Fori(0, ET // 2) as i:
                pair = dve.snap(i * 2)
                chain.enter(i, 2 * 2)
                for j in range(2):
                    dve.wait_ge(g2_load[j], i * 32 + 32)
                    for r in range(2):
                        last = nc.vector.tensor_tensor(prod2[:, r, :], g2[:, j, r, :], att2_bc[:, 0, :], ALU.mult)
                    chain.link(last)
                    dve.wait_ge(p2_pool, pair + (j + 1))
                    chain.link(nc.vector.tensor_reduce(dots[:, :, :].rearrange("p r h -> p (r h)"),
                                                       prod2[:, :, :].rearrange("p r (h c) -> p (r h) c", h=HEADS), AX.X, ALU.add))
                    dve.wait_ge(lt_bank, pair + (j + 1))
                    nc.vector.tensor_tensor(logit2[:, j, :].rearrange("p (r h) -> p r h", r=2), dots[:, 0:2, :],
                                            dots[:, 2, :].unsqueeze(1).to_broadcast([ROWS, 2, HEADS]), ALU.add).then_inc(logit2_set, 1)
            chain.leave(ET // 2)
            dve.wait_ge(lt_out, ET + 2)
            edge_softmax(dve, chain, 1)
            dve.wait_ge(al_out[1], 2)
            nc.vector.memset(zh[:, 1, :].bitcast(F32), 0.0)
            nc.vector.memset(zl[:, 1, :].bitcast(F32), 0.0).then_inc(z_lo, 1)
            with dve.Fori(0, ET // 2) as i:
                pair = dve.snap(i * 2)
                chain.enter(i, 2)
                for j in range(2):
                    t = i * 2 + j
                    chain.link(nc.vector.tensor_tensor(groups(m2[:, j, :], HEADS),
                                                       groups(ys_all[:, bass.ds(t, 1), :].rearrange("p t d -> p (t d)"), HEADS),
                                                       spread(alpha_e[:, bass.ds(t, 1), :].rearrange("p t h -> p (t h)"), CLS),
                                                       ALU.mult))
                    dve.wait_ge(m2s_set, pair + (j + 1))
                    nc.vector.tensor_tensor(m2[:, j, :], m2[:, j, :], m2s[:, j, :], ALU.add).then_inc(m2_set, 1)
                    tgt = dst_bc[0:ROWS, bass.ds(t * ROWS + 1, ROWS)]
                    nc.vector.tensor_scalar(same2[:, j, :], tgt, dst_f[:, bass.ds(t, 1)], None, ALU.is_equal)
                    nc.vector.tensor_scalar(goes2[:, j, :], tgt, dst_bc[0:ROWS, bass.ds(t * ROWS, 1)], last_row[:, :],
                                            ALU.is_equal, ALU.mult).then_inc(mask2_set, 1)
                    dve.wait_ge(z_hi, pair * 2 + (2 * j + 2))
                    nc.vector.tensor_tensor(zl[:, j, :], banks[j][0:ROWS, :], zh[:, j, :].bitcast(F32), ALU.subtract).then_inc(z_lo, 1)
            chain.leave(ET // 2)
            phase_end(dve, 3)
            for n in range(DC):
                dve.wait_ge(wp_hi, n + 1)
                nc.vector.tensor_tensor(WpTl[:, n, :], banks[n % 2][:, :], WpTh[:, n, :].bitcast(F32), ALU.subtract).then_inc(wp_lo, 1)
            dve.wait_ge(p4_bv, 16)
            for p in range(DC):
                last = nc.vector.scalar_tensor_tensor(out=ctx_acc[:, p, :], in0=bv_bc[:, p * P:(p + 1) * P],
                                                      scalar=ksum_acc[:, p, 0:1], in1=ctx_acc[:, p, :],
                                                      op0=ALU.mult, op1=ALU.add)
            chain.link(last)
            H = P // 2
            chain.link(nc.vector.memset(ksum2[:, :, :], 0.0))
            for k in range(2):
                nc.vector.memset(ctx_acc[k * H:(k + 1) * H, :, (1 - k) * H:(2 - k) * H], 0.0)
                last = nc.vector.tensor_copy(ksum2[k * H:(k + 1) * H, :, k:k + 1], ksum_acc[k * H:(k + 1) * H, :, 0:1])
            chain.link(last)
            nc.vector.tensor_copy(ctxh[:, :, :], ctx_acc[:, :, :])
            chain.link(nc.vector.tensor_copy(ksh[:, :, :], ksum2[:, :, :]))
            nc.vector.tensor_tensor(ctxl[:, :, :], ctx_acc[:, :, :], ctxh[:, :, :].bitcast(F32), ALU.subtract)
            nc.vector.tensor_tensor(ksl[:, :, :], ksum2[:, :, :], ksh[:, :, :].bitcast(F32), ALU.subtract).then_inc(ctx_ready, 1)
            dve.wait_ge(const4, 3)
            nc.vector.tensor_copy(iota16[:, :], iota_f[:, :])
            nc.vector.tensor_copy(steps128[:, :], steps_i[:, :])
            nc.vector.memset(used[:, :], 0.0)
            chain.link(nc.vector.tensor_copy(rowid[0:ROWS, 0:1], row_0[:, :]))
            dve.wait_ge(p4_sb, 16)
            for s_ in (qt_lo, num_out, ot_lo, x1_set, row_free):
                dve.sem_inc(s_, 1)
            NT = MACROS * SUBS

            def q_low(q, r):
                dve.wait_ge(qt_hi, q * G + (r + 1))
                nc.vector.tensor_tensor(qTl[:, r % 2, :, :], groups(banks[0][:, 0:MACRO], DC), qTh[:, r % 2, :, :].bitcast(F32),
                                        ALU.subtract).then_inc(qt_lo, 1)

            def finish_rstd(q, r):
                dve.wait_ge(r4_set, q * G + (r + 1))
                j = r % 2
                refine(dve, chain, r4[:, j, :], veps4[:, j, :], newt4[:, :, :])
                nc.vector.tensor_copy(x1row[:, r, D:D + 1], r4[:, j, :])
                nc.vector.scalar_tensor_tensor(out=x1row[:, r, D + 1:D + 2], in0=mv4[:, j, 0:1], scalar=-1.0, in1=r4[:, j, :],
                                               op0=ALU.mult, op1=ALU.mult).then_inc(ln4_set, 1)

            def o_low(q, r):
                dve.wait_ge(ot_hi, q * G + (r + 1))
                nc.vector.tensor_tensor(oTl[:, r % 2, :, :], groups(banks[3][:, 0:MACRO], DC), oTh[:, r % 2, :, :].bitcast(F32),
                                        ALU.subtract).then_inc(ot_lo, 1)
                dve.wait_ge(b_added, q * (2 * G) + (2 * r + 1))
                nc.vector.tensor_reduce(y_stat[:, r % 2, 0:1], y_in[:, r, :], AX.X, ALU.max, negate=True).then_inc(y_max, 1)

            def route_max(q, r):
                dve.wait_ge(rt_bank, q * G + (r + 1))
                j = r % 2
                chain.link(nc.vector.tensor_tensor(lgt[:, j, :], banks[6][0:ROWS, 16 * j:16 * j + 16], sb_bc[:, :], ALU.add))
                nc.vector.tensor_reduce(lstat[:, j, 0:1], lgt[:, j, :], AX.X, ALU.max, negate=True).then_inc(rt_max, 1)

            def residual(q, r):
                j = r % 2
                dve.wait_ge(lse_set, q * G + (r + 1))
                chain.link(nc.vector.tensor_tensor(y_stat[:, j, 3:4], y_stat[:, j, 0:1], y_stat[:, j, 2:3], ALU.subtract))
                dve.wait_ge(x1_store[r], q * 16 + 16)
                dve.wait_ge(b_added, q * (2 * G) + (2 * r + 2))
                chain.link(nc.vector.scalar_tensor_tensor(out=x1row[:, r, 0:D], in0=y_in[:, r, :], scalar=y_stat[:, j, 3:4],
                                                          in1=x_in[:, r, :], op0=ALU.add, op1=ALU.add))
                dve.wait_ge(mix_bank, q * G + (r + 1))
                nc.vector.tensor_tensor(x1row[:, r, 0:D], banks[4][0:ROWS, :], x1row[:, r, 0:D], ALU.add).then_inc(x1_set, 1)
                dve.wait_ge(x1_set, q * G + (r + 2))
                dve.sem_inc(dve_settled, 1)
                chain.link(nc.vector.bn_stats(stats4[:, :], x1row[:, r, 0:D]), dve_settled)
                chain.link(nc.vector.bn_aggr(mv4[:, j, :], stats4[:, :]))
                nc.vector.tensor_scalar(veps4[:, j, :], mv4[:, j, 1:2], EPS, None, ALU.add).then_inc(v4_set, 1)

            def route_choose(q, r):
                j = r % 2
                dve.wait_ge(rt_exp, q * G + (r + 1))
                dve.sem_inc(dve_settled, 1)
                chain.link(nc.vector.max(top8[:, :], ex16[:, j, :]), dve_settled)
                chain.link(nc.vector.max_index(arg8[:, :], top8[:, :], ex16[:, j, :]))
                nc.vector.reciprocal(lstat[:, j, 2:3], lstat[:, j, 1:2])
                chain.link(nc.vector.tensor_copy(argf[:, j, :], arg8[:, 0:1]))
                nc.vector.tensor_tensor(x1row[:, r, D + 2:D + 3], top8[:, 0:1], lstat[:, j, 2:3], ALU.mult)
                nc.vector.tensor_scalar(onehot[:, j, :], iota16[0:ROWS, :], argf[:, j, :], None, ALU.is_equal).then_inc(oh_set, 1)

            def attend(q, r):
                j = r % 2
                dve.wait_ge(num_bank, q * G + (r + 1))
                chain.link(nc.vector.reciprocal(den[:, j, :], banks[2][0:ROWS, 0:HEADS]))
                nc.vector.tensor_tensor(groups(attn[:, j, :], HEADS), groups(banks[1][0:ROWS, :], HEADS),
                                        spread(den[:, j, :], HD), ALU.mult).then_inc(num_out, 1)

            def route_place(q, r):
                j = r % 2
                t = q * G + r
                dve.wait_ge(pf_bank, t + 1)
                chain.link(nc.vector.tensor_tensor(rank[:, :], banks[7][0:ROWS, 0:16], used[:, :], ALU.add))
                nc.vector.scalar_tensor_tensor(out=rank[:, :], in0=rank[:, :], scalar=1.0, in1=onehot[:, j, :],
                                               op0=ALU.mult, op1=ALU.mult, accum_out=small[:, 0:1]).then_inc(rank_set, 1)
                chain.link(nc.vector.tensor_tensor(used[:, :], banks[7][0:ROWS, 16:32], used[:, :], ALU.add))
                dve.wait_ge(rank_set, t + 1)
                nc.vector.tensor_scalar(steps_tmp[:, :], steps128[:, :], small[:, 0:1], None, ALU.is_le, ALU.add,
                                        accum_out=small[:, 1:2])
                nc.vector.tensor_scalar(small[:, 2:3], small[:, 0:1], float(SL), None, ALU.mult)
                nc.vector.tensor_scalar(small[:, 3:4], small[:, 0:1], float(CAP), float(FAR), ALU.is_ge, ALU.mult)
                chain.link(nc.vector.tensor_scalar(small[:, 4:5], small[:, 0:1], float(CAP), float(FAR), ALU.is_lt, ALU.mult))
                chain.link(nc.vector.scalar_tensor_tensor(out=small[:, 5:6], in0=small[:, 1:2], scalar=float(1 - P * SL),
                                                          in1=small[:, 2:3], op0=ALU.mult, op1=ALU.add))
                chain.link(nc.vector.scalar_tensor_tensor(out=small[:, 6:7], in0=argf[:, j, :], scalar=float(SLOTS),
                                                          in1=small[:, 5:6], op0=ALU.mult, op1=ALU.add))
                dve.wait_ge(row_free, t + 1)
                nc.vector.tensor_tensor(slot_i[:, j:j + 1], small[:, 6:7], small[:, 3:4], ALU.add)
                nc.vector.tensor_tensor(row_i[:, j:j + 1], rowid[0:ROWS, 0:1], small[:, 4:5], ALU.add)
                chain.link(nc.vector.tensor_copy(token_i[:, j:j + 1], rowid[0:ROWS, 0:1]))
                nc.vector.tensor_scalar(rowid[0:ROWS, 0:1], rowid[0:ROWS, 0:1], float(ROWS), None, ALU.add)
                nc.vector.scalar_tensor_tensor(out=orow[:, j, :], in0=xf[:, r, :], scalar=x1row[:, r, D + 2:D + 3],
                                               in1=x1row[:, r, 0:D], op0=ALU.mult, op1=ALU.add).then_inc(row_set, 1)

            nc.vector.memset(x1row[:, :, D + 3:D + 4], 0.0)
            in_step(dve, NT, G, [(q_low, 0), (finish_rstd, 2), (o_low, 1), (route_max, 3), (residual, 1), (route_choose, 3),
                                 (attend, 0), (route_place, 3)], chain=chain, links=G * LINKS4)
            phase_end(dve, 4)
            dve.wait_ge(tok_load, 16)
            chain.link(nc.vector.tensor_copy(tok_f[:, :], tok_i[:, :]))
            nc.vector.tensor_scalar(from_i[:, :], tok_f[:, :], float(N - 1), None, ALU.min).then_inc(tok_set, 1)
            dve.sem_inc(y5_out, 2)
            dve.sem_inc(f_lo, 2)

            def expert_low(q, r):
                if r % SLOTS:
                    return
                e, j = q * 2 + r // SLOTS, r // SLOTS
                for c in range(DC):
                    dve.wait_ge(we_hi, e * DC + (c + 1))
                    nc.vector.tensor_tensor(WeTl[:, j, c, :], banks[c % 2][:, :], WeTh[:, j, c, :].bitcast(F32),
                                            ALU.subtract).then_inc(we_lo, 1)

            def rows_low(q, r):
                dve.wait_ge(f_hi, q * (2 * SLOTS) + (r + 1))
                nc.vector.tensor_tensor(fTl[:, r % 2, :, :], groups(banks[2 + r % 2][:, :], DC),
                                        fTh[:, r % 2, :, :].bitcast(F32), ALU.subtract).then_inc(f_lo, 1)

            def finish_rows(q, r):
                u, j = q * (2 * SLOTS) + r, r % 2
                if r % SLOTS == 0:
                    dve.wait_ge(eb_load[r // SLOTS], q * 16 + 16)
                dve.wait_ge(y5_bank, u + 1)
                nc.vector.tensor_tensor(yb5[:, j, :], banks[4 + j][:, :], eb_bc[:, r // SLOTS, :], ALU.add).then_inc(y5_out, 1)
                dve.wait_ge(y5_out, u + 3)
                if not isinstance(u, int) or u >= 2:
                    dve.wait_ge(res_store[j], q * (16 * SLOTS) + 16 * (r // 2))
                nc.vector.scalar_tensor_tensor(out=res5[:, j, :], in0=yb5[:, j, :], scalar=row5[:, j, D + 2:D + 3],
                                               in1=row5[:, j, 0:D], op0=ALU.mult, op1=ALU.add).then_inc(res_set, 1)

            in_step(dve, SL, 2 * SLOTS, [(expert_low, 0), (rows_low, 1), (finish_rows, 2)])

        @block.tensor
        def _(pe):
            pe.wait_ge(const_done, 1)
            for n in range(3 * DC):
                if n % DC == 0:
                    pe.wait_ge(wload["kvq"[n // DC]], 16)
                if n >= 2:
                    pe.wait_ge(wt_lo, n - 1)
                st = (wk_st, wv_st, wq_st)[n // DC]
                for c in range(DC):
                    last = nc.tensor.transpose(banks[n % 2][:, c * P:(c + 1) * P],
                                               st[:, c, (n % DC) * P:(n % DC + 1) * P], ident[:, :])
                last.then_inc(wt_bank, 1)
            pe.wait_ge(wt_lo, 3 * DC)
            pe.wait_ge(w_lo, 1)
            pe.wait_ge(w2_lo, 1)
            pe.wait_ge(ones_done, 1)
            with pe.Fori(0, MACROS) as m:
                sub0 = pe.snap(m * SUBS)
                sub3 = pe.snap(m * (3 * SUBS))

                def context(s):
                    j = s % 2
                    pe.wait_ge(k_lo, sub0 + (s + 1))
                    pe.wait_ge(ctx_free, sub0 * 2 + (2 * s + 2))
                    for p in range(DC):
                        c = slice(p * P, (p + 1) * P)
                        products(banks[6][:, c], [(kvh[:, j, 0, c], kvl[:, j, 0, c], kvh[:, j, 1, c], kvl[:, j, 1, c])])
                    for p in range(DC):
                        c = slice(p * P, (p + 1) * P)
                        nc.tensor.matmul(banks[7][:, 2 * p:2 * p + 2], kvh[:, j, 0, c], ones_r[:, :], start=True, stop=False)
                        last = nc.tensor.matmul(banks[7][:, 2 * p:2 * p + 2], kvl[:, j, 0, c], ones_r[:, :], start=False, stop=True)
                    last.then_inc(ctx_bank, 1)

                for s in range(SUBS):
                    if s == 0:
                        pe.wait_ge(xn_ready, sub0 + SUBS)
                    if s >= 2:
                        pe.wait_ge(xt_lo, sub0 + (s - 1))
                    for c in range(DC):
                        last = nc.tensor.transpose(banks[s % 2][:, c * ROWS:(c + 1) * ROWS], xn[:, s, c * P:(c + 1) * P],
                                                   ident[0:ROWS, 0:ROWS])
                    last.then_inc(xt_bank, 1)
                for s in range(SUBS):
                    pe.wait_ge(xt_lo, sub0 + (s + 1) if s else sub0 + 1)
                    r = slice(s * ROWS, (s + 1) * ROWS)
                    for n, w in enumerate("kvq"):
                        u = 3 * s + n
                        if u >= 2:
                            pe.wait_ge(kvq_free, sub3 + (u - 1))
                        else:
                            pe.wait_ge(y_free, sub0 + (SUBS - 1 + u))
                        products(banks[2 + u % 2][0:ROWS, :], [(xTh[:, c, r], xTl[:, c, r], WTh[w][:, c, :], WTl[w][:, c, :])
                                                               for c in range(DC)]).then_inc(kvq_bank, 1)
                    if s == 0:
                        pe.wait_ge(xt_lo, sub0 + SUBS)
                    for f in (2 * s, 2 * s + 1):
                        if f >= 2:
                            pe.wait_ge(h_hi, sub0 * 2 + (f - 1))
                        fs = slice(f * P, (f + 1) * P)
                        products(banks[4 + f % 2][:, 0:MACRO], [(W1h[:, c, fs], W1l[:, c, fs], xTh[:, c, :], xTl[:, c, :])
                                                                for c in range(DC)]).then_inc(h_bank, 1)
                    if s:
                        context(s - 1)
                pe.wait_ge(h_lo, sub0 * 2 + FC)
                for s in range(SUBS):
                    r = slice(s * ROWS, (s + 1) * ROWS)
                    if s < 2:
                        pe.wait_ge(kvq_free, sub3 + (3 * SUBS - 1 + s))
                    else:
                        pe.wait_ge(y_free, sub0 + (SUBS + s - 1))
                    products(banks[2 + s % 2][0:ROWS, :], [(h1h[:, f, r], h1l[:, f, r], W2h[:, f, :], W2l[:, f, :])
                                                           for f in range(FC)]).then_inc(y_bank, 1)
                    if s == 0:
                        context(SUBS - 1)
            phase_end(pe, 1)
            pe.sem_inc(e_bank, 4)
            with pe.Fori(0, ET // 2) as i:
                pair = pe.snap(i * 2)
                for j in range(2):
                    pe.wait_ge(e_xn, pair + (j + 1))
                    for r, out_done in ((0, e_src_out), (1, e_dst_out)):
                        pe.wait_ge(out_done, pair + (j + 1))
                        for c in range(DC):
                            last = nc.tensor.transpose(banks[r][:, c * ROWS:(c + 1) * ROWS], gath[:, j, r, c * P:(c + 1) * P],
                                                       ident[0:ROWS, 0:ROWS])
                        last.then_inc(e_bank, 1)
            pe.wait_ge(e_src_out, ET + 1)
            pe.wait_ge(e_dst_out, ET + 1)
            for b in range(E // MACRO):
                if b >= 2:
                    pe.wait_ge(lg_out, b - 1)
                e = slice(b * MACRO, (b + 1) * MACRO)
                for n, (xT, a) in enumerate(((xsT, 0), (xdT, 40))):
                    for c in range(DC):
                        last = nc.tensor.matmul(banks[2 + b % 2][0:40, 0:MACRO], att1[:, c, a:a + 40], xT[:, c, e],
                                                start=n + c == 0, stop=n == 1 and c == DC - 1)
                last.then_inc(lg_bank, 1)
            weights_by_edge(pe, 0)
            pe.wait_ge(al_out[0], 2)
            pe.wait_ge(lg_out, E // MACRO)

            def hidden_rows(t, first=False):
                pe.wait_ge(st_lo, t * 2 + 2)
                for h in range(2):
                    if not first:
                        pe.wait_ge(m_self, t * 2 + (h - 1))
                    for r in range(2):
                        last = products(banks[2 * h + r][0:ROWS, :],
                                        [(xsh[:, r, c, :], xsl[:, r, c, :], W1h[:, c, h * D:(h + 1) * D], W1l[:, c, h * D:(h + 1) * D])
                                         for c in range(DC)])
                    last.then_inc(hm_bank, 1)

            def aggregate(t):
                pe.wait_ge(mask_set, t + 1)
                pe.wait_ge(m_lo, t * 2 + 2)
                for f in range(FC):
                    c = (f % DC) * (ROWS + 1)
                    o = banks[4 + f // DC][:, c:c + ROWS + 1]
                    nc.tensor.matmul(o, msgh[:, f * P:(f + 1) * P], same_dst[:, :], start=True, stop=False)
                    last = nc.tensor.matmul(o, msgl[:, f * P:(f + 1) * P], same_dst[:, :], start=False, stop=True)
                last.then_inc(ag_bank, 1)

            def edge_rows(t):
                pe.wait_ge(ag_lo, t + 1)
                pe.wait_ge(ye_out, t + 1)
                products(banks[6][0:ROWS, :], [(aggh[:, f, :], aggl[:, f, :], W2h[:, f, :], W2l[:, f, :])
                                               for f in range(FC)]).then_inc(ye_bank, 1)

            hidden_rows(0, first=True)
            aggregate(0)
            with pe.Fori(0, ET - 1) as t:
                hidden_rows(t + 1)
                edge_rows(t)
                aggregate(t + 1)
            edge_rows(ET - 1)
            phase_end(pe, 2)
            pe.sem_inc(lt_bank, 2)
            with pe.Fori(0, ET // 2) as i:
                pair = pe.snap(i * 2)
                for j in range(2):
                    pe.wait_ge(logit2_set, pair + (j + 3))
                    pe.wait_ge(lt_out, pair + (j + 1))
                    nc.tensor.transpose(banks[j][0:HEADS, 0:ROWS], logit2[:, j, 0:HEADS], ident[0:ROWS, 0:ROWS])
                    nc.tensor.transpose(banks[j][0:HEADS, P:P + ROWS], logit2[:, j, HEADS:2 * HEADS],
                                        ident[0:ROWS, 0:ROWS]).then_inc(lt_bank, 1)
            pe.wait_ge(lt_out, ET + 2)
            weights_by_edge(pe, 1)
            pe.wait_ge(al_out[1], 2)
            with pe.Fori(0, ET // 2) as i:
                pair = pe.snap(i * 2)
                for j in range(2):
                    pe.wait_ge(mask2_set, pair + (j + 1))
                    pe.wait_ge(m2_lo, pair + (j + 1))
                    pe.wait_ge(z_lo, pair + (j + 1))
                    z = banks[j][0:ROWS, :]
                    nc.tensor.matmul(z, same2[:, j, :], m2h[:, j, :], start=True, stop=False)
                    nc.tensor.matmul(z, same2[:, j, :], m2l[:, j, :], start=False, stop=False)
                    nc.tensor.matmul(z, goes2[:, j, :], zh[:, 1 - j, :], start=False, stop=False)
                    nc.tensor.matmul(z, goes2[:, j, :], zl[:, 1 - j, :], start=False, stop=True).then_inc(z_bank, 1)
            phase_end(pe, 3)
            pe.wait_ge(p4_load, 16)
            for n in range(DC):
                if n >= 2:
                    pe.wait_ge(wp_lo, n - 1)
                for c in range(DC):
                    last = nc.tensor.transpose(banks[n % 2][:, c * P:(c + 1) * P], wp_st[:, c, n * P:(n + 1) * P], ident[:, :])
                last.then_inc(wp_bank, 1)
            pe.wait_ge(p4_sw, 16)
            for c in range(DC):
                last = nc.tensor.transpose(banks[2][:, c * EXPERTS:(c + 1) * EXPERTS], sw_st[:, c * P:(c + 1) * P],
                                           ident[0:EXPERTS, 0:EXPERTS])
            last.then_inc(sw_bank, 1)
            pe.wait_ge(sw_out, 1)
            pe.wait_ge(wp_lo, DC)
            pe.wait_ge(ctx_ready, 1)

            def q_turn(q, r):
                t = q * G + r
                pe.wait_ge(q4_load[r], q * 16 + 16)
                pe.wait_ge(qt_lo, t + 1)
                for c in range(DC):
                    last = nc.tensor.transpose(banks[0][:, c * ROWS:(c + 1) * ROWS], q_in[:, r, c * P:(c + 1) * P],
                                               ident[0:ROWS, 0:ROWS])
                last.then_inc(qt_bank, 1)

            def o_turn(q, r):
                t = q * G + r
                pe.wait_ge(o_set, t + 1)
                pe.wait_ge(ot_lo, t + 1)
                for c in range(DC):
                    last = nc.tensor.transpose(banks[3][:, c * ROWS:(c + 1) * ROWS], attn[:, r % 2, c * P:(c + 1) * P],
                                               ident[0:ROWS, 0:ROWS])
                last.then_inc(ot_bank, 1)

            def attention(q, r):
                t, j = q * G + r, r % 2
                pe.wait_ge(qt_lo, t + 2)
                pe.wait_ge(num_out, t + 1)
                for p in range(DC):
                    products(banks[1][0:ROWS, p * P:(p + 1) * P], [(qTh[:, j, p, :], qTl[:, j, p, :], ctxh[:, p, :], ctxl[:, p, :])])
                for p in range(DC):
                    last = products(banks[2][0:ROWS, 2 * p:2 * p + 2], [(qTh[:, j, p, :], qTl[:, j, p, :], ksh[:, p, :], ksl[:, p, :])])
                last.then_inc(num_bank, 1)

            def xf_turn(q, r):
                t = q * G + r
                pe.wait_ge(xf_set, t + 1)
                pe.wait_ge(xft_out, t + 1)
                for c in range(DC):
                    last = nc.tensor.transpose(banks[5][:, c * ROWS:(c + 1) * ROWS], xf[:, r, c * P:(c + 1) * P],
                                               ident[0:ROWS, 0:ROWS])
                last.then_inc(xft_bank, 1)

            def mix(q, r):
                t, j = q * G + r, r % 2
                pe.wait_ge(ot_lo, t + 2)
                pe.wait_ge(x1_set, t + 1)
                products(banks[4][0:ROWS, :], [(oTh[:, j, c, :], oTl[:, j, c, :], WpTh[:, c, :], WpTl[:, c, :])
                                               for c in range(DC)]).then_inc(mix_bank, 1)

            def route(q, r):
                t, j = q * G + r, r % 2
                pe.wait_ge(xft_out, t + 2)
                for c in range(DC):
                    last = nc.tensor.matmul(banks[6][0:ROWS, 16 * j:16 * j + 16], xfT[:, j, c, :], swT[:, c, :],
                                            start=c == 0, stop=c == DC - 1)
                last.then_inc(rt_bank, 1)

            def count_before(q, r):
                t, j = q * G + r, r % 2
                pe.wait_ge(oh_set, t + 1)
                nc.tensor.matmul(banks[7][0:ROWS, 0:16], before[:, :], onehot[:, j, :], start=True, stop=True)
                nc.tensor.matmul(banks[7][0:ROWS, 16:32], ones_bf[:, :], onehot[:, j, :], start=True, stop=True).then_inc(pf_bank, 1)

            in_step(pe, MACROS * SUBS, G, [(q_turn, 0), (o_turn, 1), (attention, 0), (xf_turn, 2), (mix, 1), (route, 2),
                                           (count_before, 3)])
            phase_end(pe, 4)
            def expert_turn(q, r):
                if r % SLOTS:
                    return
                e, j = q * 2 + r // SLOTS, r // SLOTS
                pe.wait_ge(we_load[j], q * 16 + 16)
                for n in range(DC):
                    if n >= 2 or not isinstance(e, int) or e:
                        pe.wait_ge(we_lo, e * DC + (n - 1))
                    for c in range(DC):
                        last = nc.tensor.transpose(banks[n % 2][:, c * P:(c + 1) * P], we_st[:, j, c, n * P:(n + 1) * P], ident[:, :])
                    last.then_inc(we_bank, 1)

            def rows_turn(q, r):
                u, j = q * (2 * SLOTS) + r, r % 2
                pe.wait_ge(x5_set, u + 1)
                pe.wait_ge(f_lo, u + 1)
                for c in range(DC):
                    last = nc.tensor.transpose(banks[2 + j][:, c * P:(c + 1) * P], xf5[:, j, c * P:(c + 1) * P], ident[:, :])
                last.then_inc(f_bank, 1)

            def expert_rows(q, r):
                u, j, k = q * (2 * SLOTS) + r, r % 2, r // SLOTS
                if r % SLOTS == 0:
                    pe.wait_ge(we_lo, q * (2 * DC) + (k * DC + DC))
                pe.wait_ge(f_lo, u + 3)
                pe.wait_ge(y5_out, u + 1)
                products(banks[4 + j][:, :], [(fTh[:, j, c, :], fTl[:, j, c, :], WeTh[:, k, c, :], WeTl[:, k, c, :])
                                              for c in range(DC)]).then_inc(y5_bank, 1)

            in_step(pe, SL, 2 * SLOTS, [(expert_turn, 0), (rows_turn, 1), (expert_rows, 2)])


_INPUTS = ["x", "src", "dst"] + ["L0_" + n for n in (
    "gnn_W1", "gnn_att_src1", "gnn_att_dst1", "gnn_b1", "gnn_W2", "gnn_att_src2", "gnn_att_dst2", "gnn_b2",
    "mix_Wq", "mix_bq", "mix_Wk", "mix_bk", "mix_Wv", "mix_bv", "mix_Wp", "mix_bp",
    "ffn_switch_w", "ffn_switch_b", "ffn_expert_w", "ffn_expert_b")]


def kernel(**inputs):
    import numpy as np
    import concourse.bacc as bacc
    from concourse import mybir as ir
    from concourse.bass_utils import run_bass_kernel_spmd

    nc = bacc.Bacc("TRN2", target_bir_lowering=False, num_devices=1)
    arrays, args = {}, []
    for name in _INPUTS:
        a = np.ascontiguousarray(inputs[name])
        arrays[f"in_{name}"] = a
        args.append(nc.dram_tensor(f"in_{name}", a.shape, ir.dt.from_np(a.dtype), kind="ExternalInput").ap())
    n, d = arrays["in_x"].shape
    args.append(nc.dram_tensor("out", (n, d), ir.dt.float32, kind="ExternalOutput").ap())
    for name, shape, dt in scratch_tables(n, d, arrays["in_L0_ffn_switch_w"].shape[0]):
        args.append(nc.dram_tensor(name, shape, dt, kind="Internal").ap())
    gps_layer(nc, *args)
    r = run_bass_kernel_spmd(nc, [arrays], core_ids=[0])
    return r.results[0]["out"]
```

```python
from contextlib import ExitStack

import concourse.bass as bass
from concourse import mybir

F32 = mybir.dt.float32
F32R = mybir.dt.float32r
BF16 = mybir.dt.bfloat16
I32 = mybir.dt.int32
U32 = mybir.dt.uint32
ALU = mybir.AluOpType
ACT = mybir.ActivationFunctionType
AX = mybir.AxisListType

P = 128
ROWS = 125
SUBS = 4
FAR = 1 << 20
EPS = 1e-5


SEM_BASE = (190, 130)


class Chain:

    def __init__(self, eng, sem):
        self.eng, self.sem, self.done, self.base, self.k, self.marks = eng, sem, 0, None, 0, {}

    def enter(self, trip, per_trip):
        self.per, self.k = per_trip, 0
        self.base = self.eng.snap(trip * per_trip + self.done)

    def leave(self, trips):
        assert self.k == self.per, f"the loop links {self.k} instructions, not {self.per}"
        self.done, self.base, self.k = self.done + trips * self.per, None, 0

    def mark(self, name, ins):
        ins.then_inc(self.sem, 1)
        if self.base is None:
            self.done += 1
            self.marks[name] = self.done
        else:
            self.k += 1
            self.marks[name] = self.k

    def need(self, name, settle=None):
        self.eng.wait_ge(self.sem, self.marks[name] if self.base is None else self.base + self.marks[name])
        if settle is not None:
            self.eng.sem_inc(settle, 1)

    def link(self, ins, settle=None):
        ins.then_inc(self.sem, 1)
        if self.base is None:
            self.done += 1
            self.eng.wait_ge(self.sem, self.done)
        else:
            self.k += 1
            self.eng.wait_ge(self.sem, self.base + self.k)
            if settle is not None:
                self.eng.sem_inc(settle, 1)


def in_step(eng, count, unroll, stages, before_loop=None, chain=None, links=0):
    assert max(lag for _, lag in stages) <= unroll

    def step(q, r, known):
        for work, lag in stages:
            if known is None:
                dq, rr = divmod(r - lag, unroll)
                work(q + dq if dq else q, rr)
            elif 0 <= known - lag < count:
                work((known - lag) // unroll, (known - lag) % unroll)

    for n in range(unroll):
        step(0, n, n)
    trips = count // unroll - 1
    with eng.Fori(0, trips) as i:
        if chain is not None:
            chain.enter(i, links)
        for r in range(unroll):
            step(i + 1, r, None)
    if chain is not None:
        chain.leave(trips)
    for n in range(count, count + max(lag for _, lag in stages)):
        step(0, 0, n)


def scratch_tables(n, d, experts):
    capacity = int(1.2 * n / experts)
    return [("y2_table", (n, d), F32), ("q_table", (n, d), F32), ("x1_table", (n, d + 4), F32),
            ("token_of_slot", (P * experts * -(-capacity // P), 1), I32)]


def gps_layer(nc, x, src, dst, W1, att_src1, att_dst1, b1, W2, att_src2, att_dst2, b2,
              Wq, bq, Wk, bk, Wv, bv, Wp, bp, switch_w, switch_b, expert_w, expert_b, out,
              y2_table, q_table, x1_table, token_of_slot):
    N, D = x.shape
    E = src.shape[0]
    HEADS, HID = att_src1.shape
    CLS = att_src2.shape[1]
    HD = D // HEADS
    DH = HEADS * HID
    EXPERTS = switch_w.shape[0]
    CAP = int(1.2 * N / EXPERTS)
    SLOTS = -(-CAP // P)
    DC = D // P
    FC = DH // P
    MACRO = ROWS * SUBS
    MACROS = N // MACRO
    ET = E // ROWS
    META = 4
    assert N % MACRO == 0 and E % (2 * ROWS) == 0 and D == 512 and HEADS * CLS == D and HID == P
    assert EXPERTS == 16 and HD == 64 and CLS == HD

    with ExitStack() as ctx:
        shared = [[], []]
        now = [None]
        given = []

        def for_phase(n):
            for handle in given:
                nc.release_semaphore(handle)
            given.clear()
            now[0] = n

        def sem(name):
            if now[0] is None:
                return ctx.enter_context(nc.semaphore(name))
            numbers = shared[now[0] % 2]
            if len(given) < len(numbers):
                handle = nc.alloc_semaphore(name=name, num=numbers[len(given)])
            else:
                handle = nc.alloc_semaphore(name=name, num=SEM_BASE[now[0] % 2] + len(given))
                numbers.append(SEM_BASE[now[0] % 2] + len(given))
            given.append(handle)
            return handle

        cursor = [nc.sbuf_base + (-nc.sbuf_base) % 32]

        def place(name, shape, dt=F32):
            size = 2 if dt == BF16 else 4
            for n in shape[1:]:
                size *= n
            at = cursor[0] + (-cursor[0]) % 32
            cursor[0] = at + size
            return nc.alloc_sbuf_tensor_at(name, list(shape), dt, offset=at)

        ident = place("ident", [P, P])
        before = place("before", [ROWS, ROWS], BF16)
        ones_bf = place("ones_bf", [ROWS, ROWS], BF16)
        iota16 = place("iota16", [P, 16])
        rowid = place("rowid", [P, 2])
        last_row = place("last_row", [ROWS, 1])
        minus_half = place("minus_half", [ROWS, SUBS])
        ctx_acc = place("ctx_acc", [P, DC, P + 2])
        b1_col = place("b1_col", [P, FC])
        LOW = cursor[0]

        W1h = place("W1h", [P, DC, DH], F32R)
        W1l = place("W1l", [P, DC, DH], F32R)
        W2h = place("W2h", [P, FC, D], F32R)
        W2l = place("W2l", [P, FC, D], F32R)
        att1 = place("att1", [P, DC, 2 * 40])
        AFTER_GNN_WEIGHTS = cursor[0]

        WTh, WTl = {}, {}
        for n in "kvq":
            WTh[n] = place(f"W{n}Th", [P, DC, D], F32R)
            WTl[n] = place(f"W{n}Tl", [P, DC, D], F32R)
        bk_bc = place("bk_bc", [ROWS, D])
        bq_bc = place("bq_bc", [ROWS, D])
        xn = place("xn", [ROWS, SUBS, D])
        SCRATCH = cursor[0]
        xTh = place("xTh", [P, DC, MACRO], F32R)
        xTl = place("xTl", [P, DC, MACRO], F32R)
        kh = place("kh", [ROWS, 2, D], F32R)
        kl = place("kl", [ROWS, 2, D], F32R)
        vh = place("vh", [ROWS, 2, DC, P + 2], F32R)
        vl = place("vl", [ROWS, 2, DC, P + 2], F32R)
        kbuf = place("kbuf", [ROWS, 2, D])
        qbuf = place("qbuf", [ROWS, 2, D])
        y2o = place("y2o", [ROWS, 2, D])
        relu = place("relu", [P, 2, MACRO])
        h1h = place("h1h", [P, FC, MACRO], F32R)
        h1l = place("h1l", [P, FC, MACRO], F32R)
        stats = place("stats", [ROWS, SUBS, 6])
        mv = place("mv", [ROWS, SUBS, 2])
        veps = place("veps", [ROWS, SUBS])
        rstd = place("rstd", [ROWS, SUBS])
        newt = place("newt", [ROWS, 2, SUBS])
        kq_max = place("kq_max", [ROWS, 2, 2, HEADS])
        kq_rec = place("kq_rec", [ROWS, 2, 2, HEADS])
        cursor[0] = SCRATCH
        wk_st = place("wk_st", [P, DC, D])
        wv_st = place("wv_st", [P, DC, D])
        wq_st = place("wq_st", [P, DC, D])
        att_bc = place("att_bc", [P, 2, DH])
        att_tmp = place("att_tmp", [P, 2, DH])
        w1_st = place("w1_st", [P, DC, DH])
        w2_st = place("w2_st", [P, FC, D])

        cursor[0] = AFTER_GNN_WEIGHTS
        src_i = place("src_i", [ROWS, ET], I32)
        dst_i = place("dst_i", [ROWS, ET], I32)
        next_i = place("next_i", [ROWS, ET], I32)
        dst_f = place("dst_f", [ROWS, ET])
        next_f = place("next_f", [ROWS, ET])
        scat_i = place("scat_i", [ROWS, ET], I32)
        SL = EXPERTS * SLOTS
        dst_bc = place("dst_bc", [P, E + 2])
        at = cursor[0]
        xsT = place("xsT", [P, DC, E])
        xdT = place("xdT", [P, DC, E])
        cursor[0] = at
        ys_all = place("ys_all", [ROWS, ET, D])
        yd_all = place("yd_all", [ROWS, ET, D])
        EDGE_SCRATCH = cursor[0] = max(cursor[0], at + 2 * (DC * E * 4 + 32))
        run = place("run", [HEADS, E])
        head_e = place("head_e", [HEADS, E])
        head_s = place("head_s", [HEADS, E])
        same = place("same", [HEADS, E + 1])
        wall = place("wall", [HEADS, E + 1])
        cursor[0] = EDGE_SCRATCH
        dst_bi = place("dst_bi", [P, E], I32)
        gath = place("gath", [ROWS, 2, 2, D])
        e_idx = place("e_idx", [ROWS, 2, 2], I32)
        e_stats = place("e_stats", [ROWS, 2, 6])
        e_mv = place("e_mv", [ROWS, 2, 2])
        e_veps = place("e_veps", [ROWS, 2])
        e_rstd = place("e_rstd", [ROWS, 2])
        e_newt = place("e_newt", [ROWS, 2, 2])
        cursor[0] = EDGE_SCRATCH
        xsh = place("xsh", [P, 2, DC, ROWS], F32R)
        xsl = place("xsl", [P, 2, DC, ROWS], F32R)
        msg = place("msg", [ROWS, 2, D])
        msg_self = place("msg_self", [ROWS, 2, D])
        msgh = place("msgh", [ROWS, DH], F32R)
        msgl = place("msgl", [ROWS, DH], F32R)
        same_dst = place("same_dst", [ROWS, ROWS + 1], F32R)
        goes_on = place("goes_on", [P, ROWS])
        aggT = place("aggT", [P, FC, ROWS])
        aggh = place("aggh", [P, FC, ROWS], F32R)
        aggl = place("aggl", [P, FC, ROWS], F32R)
        carry = place("carry", [P, FC])
        y_edge = place("y_edge", [ROWS, D])
        scat_st = place("scat_st", [ROWS, 2], I32)
        alpha_e = place("alpha_e", [ROWS, ET, HEADS])
        alpha_s = place("alpha_s", [ROWS, ET, HEADS])
        no_token = place("no_token", [P, SL], I32)
        cursor[0] = LOW
        att2_bc = place("att2_bc", [ROWS, 2, D])
        g2 = place("g2", [ROWS, 2, 2, D])
        prod2 = place("prod2", [ROWS, 3, D])
        dots = place("dots", [ROWS, 3, HEADS])
        logit2 = place("logit2", [ROWS, 2, 2 * HEADS])
        idx2 = place("idx2", [ROWS, 2, 2], I32)
        m2 = place("m2", [ROWS, 2, D])
        m2s = place("m2s", [ROWS, 2, D])
        m2h = place("m2h", [ROWS, 2, D], F32R)
        m2l = place("m2l", [ROWS, 2, D], F32R)
        same2 = place("same2", [ROWS, 2, ROWS], F32R)
        goes2 = place("goes2", [ROWS, 2, ROWS], F32R)
        z32 = place("z32", [ROWS, 2, D])
        zh = place("zh", [ROWS, 2, D], F32R)
        zl = place("zl", [ROWS, 2, D], F32R)
        scat2 = place("scat2", [ROWS, 2], I32)

        G = 4
        cursor[0] = LOW
        wp_st = place("wp_st", [P, DC, D])
        WpTh = place("WpTh", [P, DC, D], F32R)
        WpTl = place("WpTl", [P, DC, D], F32R)
        sw_st = place("sw_st", [EXPERTS, D])
        swT = place("swT", [P, DC, EXPERTS])
        sb_bc = place("sb_bc", [ROWS, EXPERTS])
        bv_bc = place("bv_bc", [P, D])
        bp_bc = place("bp_bc", [ROWS, D])
        b2_bc = place("b2_bc", [ROWS, D])
        pairs = place("pairs", [P, DC, 2, HD + 1])
        pairs_h = place("pairs_h", [P, DC, 2 * (HD + 1)], F32R)
        pairs_l = place("pairs_l", [P, DC, 2 * (HD + 1)], F32R)
        ones_row = place("ones_row", [1, ROWS], F32R)
        ones_row32 = place("ones_row32", [1, ROWS])
        bp_h = place("bp_h", [1, D], F32R)
        bp_l = place("bp_l", [1, D], F32R)
        iota_f = place("iota_f", [P, 16], I32)
        row_0 = place("row_0", [ROWS, 1], I32)
        steps_i = place("steps_i", [ROWS, max(SLOTS - 1, 1)], I32)
        used = place("used", [ROWS, EXPERTS])
        steps128 = place("steps128", [ROWS, max(SLOTS - 1, 1)])
        x_in = place("x_in", [ROWS, G, D])
        y_in = place("y_in", [ROWS, G, D])
        q_in = place("q_in", [ROWS, G, D])
        qTh = place("qTh", [P, 2, DC, ROWS], F32R)
        qTl = place("qTl", [P, 2, DC, ROWS], F32R)
        den = place("den", [ROWS, 2, HEADS])
        attn = place("attn", [ROWS, 2, D])
        oTh = place("oTh", [P, 2, DC, ROWS], F32R)
        oTl = place("oTl", [P, 2, DC, ROWS], F32R)
        exp_y = place("exp_y", [ROWS, D])
        y_stat = place("y_stat", [ROWS, 2, 4])
        x1row = place("x1row", [ROWS, G, D + META])
        stats4 = place("stats4", [ROWS, 6])
        mv4 = place("mv4", [ROWS, 2, 2])
        veps4 = place("veps4", [ROWS, 2, 1])
        r4 = place("r4", [ROWS, 2, 1])
        newt4 = place("newt4", [ROWS, 1])
        xf = place("xf", [ROWS, G, D])
        xfT = place("xfT", [P, 2, DC, ROWS])
        lstat = place("lstat", [ROWS, 2, 4])
        ex16 = place("ex16", [ROWS, 2, EXPERTS])
        top8 = place("top8", [ROWS, 8])
        arg8 = place("arg8", [ROWS, 8], U32)
        argf = place("argf", [ROWS, 2, 1])
        onehot = place("onehot", [ROWS, 2, EXPERTS], BF16)
        rank = place("rank", [ROWS, EXPERTS])
        small = place("small", [ROWS, 8])
        slot_i = place("slot_i", [ROWS, 2], I32)
        row_i = place("row_i", [ROWS, 2], I32)
        steps_tmp = place("steps_tmp", [ROWS, max(SLOTS - 1, 1)])
        token_i = place("token_i", [ROWS, 2], I32)
        orow = place("orow", [ROWS, 2, D])
        drop_line = place("drop_line", [ROWS, 2, 2])

        SL = EXPERTS * SLOTS
        cursor[0] = LOW
        ROW5 = 4
        tok_i = place("tok_i", [P, SL], I32)
        tok_f = place("tok_f", [P, SL])
        from_i = place("from_i", [P, SL], I32)
        we_st = place("we_st", [P, 2, DC, D])
        WeTh = place("WeTh", [P, 2, DC, D], F32R)
        WeTl = place("WeTl", [P, 2, DC, D], F32R)
        eb_bc = place("eb_bc", [P, 2, D])
        row5 = place("row5", [P, ROW5, D + META])
        xf5 = place("xf5", [P, 2, D])
        fTh = place("fTh", [P, 2, DC, P], F32R)
        fTl = place("fTl", [P, 2, DC, P], F32R)
        yb5 = place("yb5", [P, 2, D])
        res5 = place("res5", [P, 2, D])
        from_st = place("from_st", [P, ROW5], I32)
        to_st = place("to_st", [P, 2], I32)

        banks = [nc.alloc_psum_tensor(f"bank{i}", [P, 512], F32) for i in range(8)]

        def groups(ap, n):
            return ap.rearrange("p (h c) -> p h c", h=n)

        def spread(ap, n):
            return ap.unsqueeze(2).to_broadcast([ap.shape[0], ap.shape[1], n])

        def products(out_, terms, first=True, more=False):
            last = None
            for n, (ah, al, bh, bl) in enumerate(terms):
                nc.tensor.matmul(out_, ah, bh, start=first and n == 0, stop=False)
                nc.tensor.matmul(out_, ah, bl, start=False, stop=False)
                last = nc.tensor.matmul(out_, al, bh, start=False, stop=not more and n == len(terms) - 1)
            return last


        const_done = sem("const_done")
        pool_chain = sem("pool_chain")
        dve_chain = sem("dve_chain")
        act_chain = sem("act_chain")
        pool_settled = sem("pool_settled")
        dve_settled = sem("dve_settled")
        sp_settled = sem("sp_settled")
        phase_done = sem("phase_done")
        e_gath = [sem(f"e_gath{j}") for j in range(2)]
        ye_store = sem("ye_store")
        g2_load = [sem(f"g2_load{j}") for j in range(2)]
        z_store = [sem(f"z_store{j}") for j in range(2)]
        tok_store = [sem(f"tok_store{j}") for j in range(2)]
        orow_store = [sem(f"orow_store{j}") for j in range(2)]
        row5_load = [sem(f"row5_load{j}") for j in range(4)]
        res_store = [sem(f"res_store{j}") for j in range(2)]
        for_phase(1)
        wload = {n: sem(f"wload_{n}") for n in ("k", "v", "q", "W1", "W2", "att0", "att1")}
        bias_load = [sem(f"bias_load{n}") for n in range(3)]
        ones_done = sem("ones_done")
        wt_bank = sem("wt_bank")
        wt_hi = sem("wt_hi")
        wt_lo = sem("wt_lo")
        w_hi = sem("w_hi")
        w_lo = sem("w_lo")
        w2_lo = sem("w2_lo")
        att_sum = sem("att_sum")
        x_load = sem("x_load")
        var_ready = sem("var_ready")
        rstd0 = sem("rstd0")
        xn_ready = sem("xn_ready")
        xt_bank = sem("xt_bank")
        xt_hi = sem("xt_hi")
        xt_lo = sem("xt_lo")
        kvq_bank = sem("kvq_bank")
        kvq_free = sem("kvq_free")
        smax = sem("smax")
        ssub = sem("ssub")
        sexp = sem("sexp")
        srec = sem("srec")
        snorm_k = sem("snorm_k")
        snorm_q = sem("snorm_q")
        v_hi = sem("v_hi")
        k_hi = sem("k_hi")
        k_lo = sem("k_lo")
        ctx_bank = sem("ctx_bank")
        ctx_free = sem("ctx_free")
        h_bank = sem("h_bank")
        h_hi = sem("h_hi")
        h_lo = sem("h_lo")
        y_bank = sem("y_bank")
        y_free = sem("y_free")
        q_store = [sem(f"q_store{j}") for j in range(2)]
        y_store = [sem(f"y_store{j}") for j in range(2)]
        for_phase(2)
        edge_load = {n: sem(f"edge_load_{n}") for n in ("src", "dst", "next", "all")}
        next_clear = sem("next_clear")
        edge_f = sem("edge_f")
        e_staged = sem("e_staged")
        e_var = sem("e_var")
        e_rstd0 = sem("e_rstd0")
        e_xn = sem("e_xn")
        e_bank = sem("e_bank")
        e_src_out = sem("e_src_out")
        e_dst_out = sem("e_dst_out")
        lg_bank = sem("lg_bank")
        lg_out = sem("lg_out")
        st_hi = sem("st_hi")
        st_lo = sem("st_lo")
        hm_bank = sem("hm_bank")
        m_self = sem("m_self")
        m_sum = sem("m_sum")
        m_hi = sem("m_hi")
        m_lo = sem("m_lo")
        mask_set = sem("mask_set")
        ag_bank = sem("ag_bank")
        ag_out = sem("ag_out")
        ag_hi = sem("ag_hi")
        ag_lo = sem("ag_lo")
        ye_bank = sem("ye_bank")
        ye_out = sem("ye_out")
        pool_scat = sem("pool_scat")
        tok_init = sem("tok_init")
        no_tok = sem("no_tok")
        sc_sub_1 = sem("sc_sub_1")
        sc_exp_1 = sem("sc_exp_1")
        sc_done_1 = sem("sc_done_1")
        al_bank_1 = sem("al_bank_1")
        al_out_1 = sem("al_out_1")
        for_phase(3)
        att2_load = sem("att2_load")
        g2_staged = sem("g2_staged")
        g2_copied = sem("g2_copied")
        p2_pool = sem("p2_pool")
        logit2_set = sem("logit2_set")
        lt_bank = sem("lt_bank")
        lt_out = sem("lt_out")
        m2s_set = sem("m2s_set")
        m2_set = sem("m2_set")
        m2_hi = sem("m2_hi")
        m2_lo = sem("m2_lo")
        z_bank = sem("z_bank")
        mask2_set = sem("mask2_set")
        z_hi = sem("z_hi")
        z_lo = sem("z_lo")
        z_staged = sem("z_staged")
        sc_sub_2 = sem("sc_sub_2")
        sc_exp_2 = sem("sc_exp_2")
        sc_done_2 = sem("sc_done_2")
        al_bank_2 = sem("al_bank_2")
        al_out_2 = sem("al_out_2")
        sc_sub = (sc_sub_1, sc_sub_2)
        sc_exp = (sc_exp_1, sc_exp_2)
        sc_done = (sc_done_1, sc_done_2)
        al_bank = (al_bank_1, al_bank_2)
        al_out = (al_out_1, al_out_2)
        for_phase(4)
        p4_load = sem("p4_load")
        p4_bias = sem("p4_bias")
        p4_sw = sem("p4_sw")
        p4_sb = sem("p4_sb")
        p4_bv = sem("p4_bv")
        wp_bank = sem("wp_bank")
        wp_hi = sem("wp_hi")
        wp_lo = sem("wp_lo")
        sw_bank = sem("sw_bank")
        sw_out = sem("sw_out")
        ctx_ready = sem("ctx_ready")
        b_added = sem("b_added")
        qt_bank = sem("qt_bank")
        qt_hi = sem("qt_hi")
        qt_lo = sem("qt_lo")
        num_bank = sem("num_bank")
        num_out = sem("num_out")
        o_set = sem("o_set")
        ot_bank = sem("ot_bank")
        ot_hi = sem("ot_hi")
        ot_lo = sem("ot_lo")
        mix_bank = sem("mix_bank")
        x1_set = sem("x1_set")
        y_max = sem("y_max")
        lse_set = sem("lse_set")
        v4_set = sem("v4_set")
        r4_set = sem("r4_set")
        ln4_set = sem("ln4_set")
        xf_set = sem("xf_set")
        xft_bank = sem("xft_bank")
        xft_out = sem("xft_out")
        rt_bank = sem("rt_bank")
        rt_max = sem("rt_max")
        rt_exp = sem("rt_exp")
        oh_set = sem("oh_set")
        pf_bank = sem("pf_bank")
        row_set = sem("row_set")
        row_free = sem("row_free")
        orow_set = sem("orow_set")
        const4 = sem("const4")
        rank_set = sem("rank_set")
        x4_load = [sem(f"x4_load{j}") for j in range(G)]
        y4_load = [sem(f"y4_load{j}") for j in range(G)]
        q4_load = [sem(f"q4_load{j}") for j in range(G)]
        x1_store = [sem(f"x1_store{j}") for j in range(G)]
        for_phase(5)
        tok_load = sem("tok_load")
        tok_set = sem("tok_set")
        we_bank = sem("we_bank")
        we_hi = sem("we_hi")
        we_lo = sem("we_lo")
        x5_set = sem("x5_set")
        f_bank = sem("f_bank")
        f_hi = sem("f_hi")
        f_lo = sem("f_lo")
        y5_bank = sem("y5_bank")
        y5_out = sem("y5_out")
        res_set = sem("res_set")
        idx5_set = sem("idx5_set")
        to_set = sem("to_set")
        we_load = [sem(f"we_load{j}") for j in range(2)]
        eb_load = [sem(f"eb_load{j}") for j in range(2)]
        for_phase(None)

        CONSTS = 7
        LINKS4 = 16
        DVE_LINKS = 2 + 4 + 2 * SUBS

        def refine(dve, chain, r, v, tmp):
            chain.link(nc.vector.tensor_tensor(tmp[:, 0, :], r, r, ALU.mult))
            chain.link(nc.vector.tensor_tensor(tmp[:, 0, :], tmp[:, 0, :], v, ALU.mult))
            chain.link(nc.vector.tensor_scalar(tmp[:, 0, :], tmp[:, 0, :], -0.5, 1.5, ALU.mult, ALU.add))
            chain.link(nc.vector.tensor_tensor(r, r, tmp[:, 0, :], ALU.mult))

        def add_context(dve, chain, sub0, s):
            dve.wait_ge(ctx_bank, sub0 + (s + 1))
            dve.wait_ge(ctx_free, sub0 * 2 + (2 * s + 2))
            for b in range(2):
                pairs = slice(b * DC // 2, (b + 1) * DC // 2)
                nc.vector.tensor_tensor(ctx_acc[:, pairs, :], groups(banks[6 + b][:, 0:(P + 2) * DC // 2], DC // 2),
                                        ctx_acc[:, pairs, :], ALU.add).then_inc(ctx_free, 1)

        def phase_end(eng, n):
            eng.drain().then_inc(phase_done, 1)
            eng.wait_ge(phase_done, 5 * n)
            if eng is nc.gpsimd:
                eng.sem_clear(range(shared[n % 2][0], shared[n % 2][-1] + 1))

        def edge_softmax(dve, chain, layer):
            for t in (head_e, head_s):
                chain.link(nc.vector.scalar_tensor_tensor(out=t[:, :], in0=t[:, :], scalar=0.2, in1=t[:, :],
                                                          op0=ALU.mult, op1=ALU.max))
            chain.link(nc.vector.tensor_tensor(same[:, :], dst_bc[0:HEADS, 1:E + 2], dst_bc[0:HEADS, 0:E + 1], ALU.is_equal))
            chain.link(nc.vector.tensor_scalar(wall[:, :], same[:, :], 1e30, -1e30, ALU.mult, ALU.add))
            chain.link(nc.vector.tensor_tensor_scan(run[:, :], wall[:, 0:E], head_e[:, :], -1e30, ALU.add, ALU.max))
            chain.link(nc.vector.tensor_tensor_scan(run[:, ::-1], wall[:, :0:-1], run[:, ::-1], -1e30, ALU.add, ALU.max))
            chain.link(nc.vector.tensor_tensor(run[:, :], run[:, :], head_s[:, :], ALU.max))
            for t in (head_e, head_s):
                last = nc.vector.tensor_tensor(t[:, :], t[:, :], run[:, :], ALU.subtract)
                last.then_inc(sc_sub[layer], 1)
            dve.wait_ge(sc_exp[layer], 2)
            chain.link(nc.vector.tensor_tensor_scan(run[:, :], same[:, 0:E], head_e[:, :], 0.0, ALU.mult, ALU.add))
            chain.link(nc.vector.tensor_scalar(wall[:, :], same[:, :], -1.0, 1.0, ALU.mult, ALU.add))
            chain.link(nc.vector.tensor_tensor(run[:, :], run[:, :], wall[:, 1:E + 1], ALU.mult))
            chain.link(nc.vector.tensor_tensor_scan(run[:, ::-1], same[:, :0:-1], run[:, ::-1], 0.0, ALU.mult, ALU.add))
            chain.link(nc.vector.scalar_tensor_tensor(out=run[:, :], in0=run[:, :], scalar=1e-16, in1=head_s[:, :],
                                                      op0=ALU.add, op1=ALU.add))
            chain.link(nc.vector.reciprocal(run[:, :], run[:, :]))
            chain.link(nc.vector.tensor_tensor(head_s[:, :], head_s[:, :], wall[:, 0:E], ALU.mult))
            nc.vector.tensor_tensor(head_e[:, :], head_e[:, :], run[:, :], ALU.mult).then_inc(sc_done[layer], 1)
            nc.vector.tensor_tensor(head_s[:, :], head_s[:, :], run[:, :], ALU.mult).then_inc(sc_done[layer], 1)

        def exp_logits(act, layer):
            for n, t in enumerate((head_e, head_s)):
                act.wait_ge(sc_sub[layer], n + 1)
                nc.scalar.activation(t[:, :], t[:, :], ACT.Exp).then_inc(sc_exp[layer], 1)

        def weights_by_edge(pe, layer):
            for n, t in enumerate((head_e, head_s)):
                pe.wait_ge(sc_done[layer], n + 1)
                for k in range(ET):
                    last = nc.tensor.transpose(banks[n][0:ROWS, k * HEADS:(k + 1) * HEADS],
                                               t[:, k * ROWS:(k + 1) * ROWS], ident[0:HEADS, 0:HEADS])
                last.then_inc(al_bank[layer], 1)

        def take_weights(act, layer):
            for n, t in enumerate((alpha_e, alpha_s)):
                act.wait_ge(al_bank[layer], n + 1)
                nc.scalar.activation(t[:, :, :], groups(banks[n][0:ROWS, 0:ET * HEADS], ET), ACT.Copy).then_inc(al_out[layer], 1)

        block = ctx.enter_context(nc.Block())

        @block.sync
        def _(sp):
            for n, w, st in (("k", Wk, wk_st), ("v", Wv, wv_st), ("q", Wq, wq_st)):
                sp.dma_start(st[:, :, :], w.rearrange("(c p) i -> p c i", p=P)).then_inc(wload[n], 16)
            sp.dma_start(xn[:, :, :], x[0:MACRO, :].rearrange("(s p) d -> p s d", p=ROWS)).then_inc(x_load, 16)
            sp.dma_start(w1_st[:, :, :], W1.rearrange("(c p) i -> p c i", p=P)).then_inc(wload["W1"], 16)
            sp.dma_start(w2_st[:, :, :], W2.rearrange("(c p) i -> p c i", p=P)).then_inc(wload["W2"], 16)
            for j in range(2):
                sp.sem_inc(q_store[j], 16)

            def store_q(m):
                for s in range(SUBS):
                    sp.wait_ge(snorm_q, m * SUBS + (s + 1))
                    sp.sem_inc(sp_settled, 1)
                    sp.dma_start(q_table[bass.ds((m * SUBS + s) * ROWS, ROWS), :],
                                 qbuf[:, s % 2, :]).then_inc(q_store[s % 2], 16)

            with sp.Fori(0, MACROS - 1) as m:
                store_q(m)
                sp.wait_ge(xt_bank, m * SUBS + SUBS)
                sp.sem_inc(sp_settled, 1)
                sp.dma_start(xn[:, :, :], x[bass.ds(m * MACRO + MACRO, MACRO), :]
                             .rearrange("(s p) d -> p s d", p=ROWS)).then_inc(x_load, 16)
            store_q(MACROS - 1)
            for j in range(2):
                sp.wait_ge(q_store[j], 16 * (MACROS * SUBS // 2 + 1))
            phase_end(sp, 1)
            slow = dict(allow_slow_non_contiguous=True)
            sp.wait_ge(no_tok, 1)
            sp.dma_start(token_of_slot.rearrange("(p s) o -> p (s o)", p=P), no_token[:, :]).then_inc(tok_init, 16)
            sp.wait_ge(tok_init, 16)
            sp.dma_start(src_i[:, :], src.rearrange("(t p) -> p t", p=ROWS), **slow).then_inc(edge_load["src"], 16)
            sp.dma_start(dst_i[:, :], dst.rearrange("(t p) -> p t", p=ROWS), **slow).then_inc(edge_load["dst"], 16)
            sp.dma_start(dst_bi[:, :], dst.partition_broadcast(P)).then_inc(edge_load["all"], 16)
            sp.wait_ge(next_clear, 1)
            sp.dma_start(next_i[:, 0:ET - 1], dst[1:1 + (ET - 1) * ROWS].rearrange("(t p) -> p t", p=ROWS),
                         **slow).then_inc(edge_load["next"], 16)
            sp.dma_start(next_i[0:ROWS - 1, ET - 1:ET], dst[E - ROWS + 1:E].rearrange("(p t) -> p t", t=1),
                         **slow).then_inc(edge_load["next"], 16)
            phase_end(sp, 2)
            for r, a in enumerate((att_src2, att_dst2)):
                sp.dma_start(att2_bc[:, r, :], a.rearrange("h c -> (h c)").partition_broadcast(ROWS)).then_inc(att2_load, 16)
            phase_end(sp, 3)
            sp.dma_start(wp_st[:, :, :], Wp.rearrange("(c p) i -> p c i", p=P)).then_inc(p4_load, 16)
            sp.dma_start(bv_bc[:, :], bv.partition_broadcast(P)).then_inc(p4_bv, 16)
            sp.dma_start(sw_st[:, :], switch_w).then_inc(p4_sw, 16)
            for d, b in ((bp_bc, bp), (b2_bc, b2)):
                sp.dma_start(d[:, :], b.partition_broadcast(ROWS)).then_inc(p4_bias, 16)
            sp.dma_start(sb_bc[:, :], switch_b.partition_broadcast(ROWS)).then_inc(p4_sb, 16)
            for j in range(G):
                sp.sem_inc(x1_store[j], 16)

            def load_nodes(q, r):
                t = q * G + r
                if not isinstance(t, int):
                    sp.wait_ge(o_set, t - (G - 1))
                    sp.sem_inc(sp_settled, 1)
                    sp.wait_ge(x1_set, t - (G - 2))
                    sp.sem_inc(sp_settled, 1)
                rows = bass.ds(t * ROWS, ROWS)
                for d, s_, done in ((q_in, q_table, q4_load), (x_in, x, x4_load), (y_in, y2_table, y4_load)):
                    sp.dma_start(d[:, r, :], s_[rows, :]).then_inc(done[r], 16)

            def store_x1(q, r):
                sp.wait_ge(oh_set, q * G + (r + 1))
                sp.sem_inc(sp_settled, 1)
                sp.dma_start(x1_table[bass.ds((q * G + r) * ROWS, ROWS), :], x1row[:, r, :]).then_inc(x1_store[r], 16)

            in_step(sp, MACROS * SUBS, G, [(load_nodes, 0), (store_x1, 4)])
            for j in range(G):
                sp.wait_ge(x1_store[j], 16 * (MACROS * SUBS // G + 1))
            phase_end(sp, 4)
            sp.dma_start(tok_i[:, :], token_of_slot.rearrange("(p s) o -> p (s o)", p=P)).then_inc(tok_load, 16)

            def load_expert(q, r):
                if r % SLOTS:
                    return
                e, j = q * 2 + r // SLOTS, r // SLOTS
                if not isinstance(e, int):
                    sp.wait_ge(we_bank, e * DC - DC)
                    sp.sem_inc(sp_settled, 1)
                    sp.wait_ge(y5_out, e * SLOTS - SLOTS + 2)
                    sp.sem_inc(sp_settled, 1)
                sp.dma_start(we_st[:, j, :, :], expert_w[bass.ds(e, 1), :, :].rearrange("o (c p) i -> p (o c) i", p=P))\
                  .then_inc(we_load[j], 16)
                sp.dma_start(eb_bc[:, j, :], expert_b[bass.ds(e, 1), :].rearrange("o f -> (o f)").partition_broadcast(P))\
                  .then_inc(eb_load[j], 16)

            in_step(sp, SL, 2 * SLOTS, [(load_expert, 0)])

        @block.gpsimd
        def _(pool):
            chain = Chain(pool, pool_chain)
            settle = lambda: pool.sem_inc(pool_settled, 1)
            chain.link(nc.gpsimd.memset(ident[:, :], 0.0))
            nc.gpsimd.affine_select(out=ident[:, :], in_=ident[:, :], compare_op=ALU.not_equal, fill=1.0, base=0,
                                    pattern=[[-1, P]], channel_multiplier=1).then_inc(const_done, 1)
            nc.gpsimd.memset(ones_bf[:, :], 1.0).then_inc(const_done, 1)
            chain.link(nc.gpsimd.memset(before[:, :], 1.0))
            nc.gpsimd.affine_select(out=before[:, :], in_=before[:, :], compare_op=ALU.is_gt, fill=0.0, base=0,
                                    pattern=[[1, ROWS]], channel_multiplier=-1).then_inc(const_done, 1)
            nc.gpsimd.memset(minus_half[:, :], -0.5).then_inc(const_done, 1)
            chain.link(nc.gpsimd.memset(last_row[:, :], 0.0))
            nc.gpsimd.affine_select(out=last_row[:, :], in_=last_row[:, :], compare_op=ALU.not_equal, fill=1.0,
                                    base=1 - ROWS, pattern=[[0, 1]], channel_multiplier=1).then_inc(const_done, 1)
            nc.gpsimd.memset(ctx_acc[:, :, :], 0.0).then_inc(const_done, 1)
            nc.gpsimd.memset(att1[:, :, :], 0.0).then_inc(const_done, 1)
            pool.wait_ge(const_done, CONSTS)
            pool.wait_ge(w_hi, 2)
            nc.gpsimd.tensor_tensor(W2l[:, :, :], w2_st[:, :, :], W2h[:, :, :].bitcast(F32),
                                    ALU.subtract).then_inc(w2_lo, 1)
            def start_rstds(m):
                pool.wait_ge(var_ready, m + 1)
                settle()
                nc.gpsimd.tensor_tensor(rstd[:, :], veps[:, :], minus_half[:, :], ALU.pow).then_inc(rstd0, 1)

            def softmax_steps(sub0):
                for s in range(SUBS):
                    j = s % 2
                    for n, buf in ((0, kbuf), (1, qbuf)):
                        pool.wait_ge(smax, sub0 * 2 + (2 * s + n + 1))
                        nc.gpsimd.tensor_tensor(groups(buf[:, j, :], HEADS), groups(buf[:, j, :], HEADS),
                                                spread(kq_max[:, j, n, :], HD), ALU.subtract).then_inc(ssub, 1)
                    for n, buf, done in ((0, kbuf, snorm_k), (1, qbuf, snorm_q)):
                        pool.wait_ge(srec, sub0 * 2 + (2 * s + n + 1))
                        nc.gpsimd.tensor_tensor(groups(buf[:, j, :], HEADS), groups(buf[:, j, :], HEADS),
                                                spread(kq_rec[:, j, n, :], HD), ALU.mult).then_inc(done, 1)
                    for f in (2 * s, 2 * s + 1):
                        pool.wait_ge(h_hi, sub0 * 2 + (f + 1))
                        nc.gpsimd.tensor_tensor(h1l[:, f, :], relu[:, f % 2, :], h1h[:, f, :].bitcast(F32),
                                                ALU.subtract).then_inc(h_lo, 1)

            start_rstds(0)
            with pool.Fori(0, MACROS - 1) as m:
                sub0 = pool.snap(m * SUBS)
                softmax_steps(sub0)
                start_rstds(m + 1)
            softmax_steps((MACROS - 1) * SUBS)

            phase_end(pool, 1)
            nc.gpsimd.memset(no_token[:, :], FAR).then_inc(no_tok, 1)
            nc.gpsimd.memset(next_i[:, :], -1).then_inc(next_clear, 1)
            pool.wait_ge(edge_load["src"], 16)
            pool.wait_ge(edge_load["dst"], 16)
            with pool.Fori(0, ET // 2) as i:
                for j in range(2):
                    t = i * 2 + j
                    if j == 0:
                        pair = pool.snap(i * 2)
                    pool.wait_ge(e_bank, pair * 2 + (2 * j + 2))
                    settle()
                    for r, idx in enumerate((src_i, dst_i)):
                        nc.gpsimd.tensor_copy(e_idx[:, j, r:r + 1], idx[:, bass.ds(t, 1)]).then_inc(e_staged, 1)
                    pool.wait_ge(e_staged, pair * 2 + (2 * j + 2))
                    settle()
                    for r in range(2):
                        pool.indirect_dma_start(gath[:, j, r, :], None, x, bass.IndirectOffsetOnAxis(
                            e_idx[:, j, r:r + 1].bitcast(U32), 0)).then_inc(e_gath[j], 16)
                for j in range(2):
                    pool.wait_ge(e_var, pair + (j + 1))
                    settle()
                    nc.gpsimd.tensor_tensor(e_rstd[:, :], e_veps[:, :], minus_half[:, 0:2], ALU.pow).then_inc(e_rstd0, 1)

            def stage_low(t):
                for r, xT in enumerate((xsT, xdT)):
                    pool.wait_ge(st_hi, t * 2 + (r + 1))
                    nc.gpsimd.tensor_tensor(xsl[:, r, :, :], xT[:, :, bass.ds(t * ROWS, ROWS)],
                                            xsh[:, r, :, :].bitcast(F32), ALU.subtract).then_inc(st_lo, 1)

            def message_low(t):
                for h in range(2):
                    pool.wait_ge(m_self, t * 2 + (h + 1))
                    settle()
                    nc.gpsimd.tensor_tensor(msg[:, h, :], msg[:, h, :], msg_self[:, h, :], ALU.add).then_inc(m_sum, 1)
                    pool.wait_ge(m_hi, t * 2 + (h + 1))
                    nc.gpsimd.tensor_tensor(msgl[:, h * D:(h + 1) * D], msg[:, h, :],
                                            msgh[:, h * D:(h + 1) * D].bitcast(F32), ALU.subtract).then_inc(m_lo, 1)

            def aggregate_low(t):
                pool.wait_ge(ag_hi, t + 1)
                nc.gpsimd.tensor_tensor(aggl[:, :, :], aggT[:, :, :], aggh[:, :, :].bitcast(F32), ALU.subtract).then_inc(ag_lo, 1)

            def scatter_rows(t):
                pool.wait_ge(ye_out, t + 2)
                settle()
                nc.gpsimd.tensor_copy(scat_st[:, 0:1], scat_i[:, bass.ds(t, 1)]).then_inc(pool_scat, 1)
                pool.wait_ge(pool_scat, t + 1)
                settle()
                pool.indirect_dma_start(y2_table, bass.IndirectOffsetOnAxis(scat_st[:, 0:1].bitcast(U32), 0), y_edge[:, :],
                                        None, bounds_check=N - 1, oob_is_err=False).then_inc(ye_store, 16)

            stage_low(0)
            message_low(0)
            stage_low(1)
            with pool.Fori(0, ET - 2) as t:
                aggregate_low(t)
                message_low(t + 1)
                stage_low(t + 2)
                scatter_rows(t)
            aggregate_low(ET - 2)
            message_low(ET - 1)
            scatter_rows(ET - 2)
            aggregate_low(ET - 1)
            scatter_rows(ET - 1)
            pool.wait_ge(ye_store, 16 * ET)
            phase_end(pool, 2)
            pool.wait_ge(att2_load, 32)
            with pool.Fori(0, ET // 2) as i:
                pair = pool.snap(i * 2)
                for j in range(2):
                    pool.wait_ge(g2_copied, pair + (j + 1))
                    pool.wait_ge(logit2_set, pair + (j + 1))
                    settle()
                    for r, idx in enumerate((src_i, dst_i)):
                        nc.gpsimd.tensor_copy(idx2[:, j, r:r + 1], idx[:, bass.ds(i * 2 + j, 1)]).then_inc(g2_staged, 1)
                    pool.wait_ge(g2_staged, pair * 2 + (2 * j + 2))
                    settle()
                    for r in range(2):
                        pool.indirect_dma_start(g2[:, j, r, :], None, y2_table, bass.IndirectOffsetOnAxis(
                            idx2[:, j, r:r + 1].bitcast(U32), 0)).then_inc(g2_load[j], 16)
                for j in range(2):
                    pool.wait_ge(g2_load[j], i * 32 + 32)
                    pool.wait_ge(logit2_set, pair + (j + 2))
                    settle()
                    nc.gpsimd.tensor_tensor(prod2[:, 2, :], g2[:, j, 1, :], att2_bc[:, 1, :], ALU.mult).then_inc(p2_pool, 1)
            with pool.Fori(0, ET // 2) as i:
                pair = pool.snap(i * 2)
                for j in range(2):
                    pool.wait_ge(al_out[1], 2)
                    pool.wait_ge(m2_set, pair + (j + 1))
                    settle()
                    nc.gpsimd.tensor_tensor(groups(m2s[:, j, :], HEADS), groups(yd_all[:, bass.ds(i * 2 + j, 1), :]
                                            .rearrange("p t d -> p (t d)"), HEADS),
                                            spread(alpha_s[:, bass.ds(i * 2 + j, 1), :].rearrange("p t h -> p (t h)"), HD),
                                            ALU.mult).then_inc(m2s_set, 1)
                    pool.wait_ge(m2_hi, pair + (j + 1))
                    nc.gpsimd.tensor_tensor(m2l[:, j, :], m2[:, j, :], m2h[:, j, :].bitcast(F32), ALU.subtract).then_inc(m2_lo, 1)
                    pool.wait_ge(z_hi, pair * 2 + (2 * j + 1))
                    settle()
                    nc.gpsimd.tensor_copy(scat2[:, j:j + 1], scat_i[:, bass.ds(i * 2 + j, 1)]).then_inc(z_staged, 1)
                    pool.wait_ge(z_staged, pair + (j + 1))
                    settle()
                    pool.indirect_dma_start(y2_table, bass.IndirectOffsetOnAxis(scat2[:, j:j + 1].bitcast(U32), 0), z32[:, j, :],
                                            None, bounds_check=N - 1, oob_is_err=False).then_inc(z_store[j], 16)
                for j in range(2):
                    pool.wait_ge(z_store[j], i * 16 + 16)
                    settle()
            phase_end(pool, 3)
            nc.gpsimd.iota(iota_f[:, :], pattern=[[1, EXPERTS]], base=0, channel_multiplier=0).then_inc(const4, 1)
            nc.gpsimd.iota(row_0[:, :], pattern=[[0, 1]], base=0, channel_multiplier=1).then_inc(const4, 1)
            nc.gpsimd.iota(steps_i[:, :], pattern=[[P, steps_i.shape[1]]], base=P, channel_multiplier=0).then_inc(const4, 1)
            pool.wait_ge(p4_bias, 32)
            NT = MACROS * SUBS

            def add_biases(q, r):
                pool.wait_ge(y4_load[r], q * 16 + 16)
                settle()
                nc.gpsimd.tensor_tensor(y_in[:, r, :], y_in[:, r, :], b2_bc[:, :], ALU.add).then_inc(b_added, 1)
                pool.wait_ge(x4_load[r], q * 16 + 16)
                settle()
                pool.wait_ge(b_added, q * (2 * G) + (2 * r + 1))
                settle()
                nc.gpsimd.tensor_tensor(x_in[:, r, :], x_in[:, r, :], y_in[:, r, :], ALU.add).then_inc(b_added, 1)

            def start_rstd(q, r):
                pool.wait_ge(v4_set, q * G + (r + 1))
                nc.gpsimd.tensor_tensor(r4[:, r % 2, :], veps4[:, r % 2, :], minus_half[:, 0:1], ALU.pow).then_inc(r4_set, 1)

            def add_q(q, r):
                pool.wait_ge(num_out, q * G + (r + 2))
                nc.gpsimd.tensor_tensor(attn[:, r % 2, :], attn[:, r % 2, :], q_in[:, r, :], ALU.add).then_inc(o_set, 1)

            def send_tokens(q, r):
                t, j = q * G + r, r % 2
                pool.wait_ge(orow_set, t + (G + 1))
                if not isinstance(t, int) or t:
                    for store in (tok_store, orow_store):
                        pool.wait_ge(store[1 - j], q * 32 + 16 * ((r + 1) // 2))
                pool.sem_inc(row_free, 1)
                pool.indirect_dma_start(token_of_slot, bass.IndirectOffsetOnAxis(slot_i[:, j:j + 1].bitcast(U32), 0),
                                        token_i[:, j:j + 1], None, bounds_check=P * SL - 1, oob_is_err=False)\
                    .then_inc(tok_store[j], 16)
                pool.indirect_dma_start(out, bass.IndirectOffsetOnAxis(row_i[:, j:j + 1].bitcast(U32), 0), orow[:, j, :],
                                        None, bounds_check=N - 1, oob_is_err=False).then_inc(orow_store[j], 16)

            in_step(pool, NT, G, [(add_biases, 0), (start_rstd, 2), (send_tokens, 4), (add_q, 0)])
            for j in range(2):
                pool.wait_ge(tok_store[j], 16 * (NT // 2))
                pool.wait_ge(orow_store[j], 16 * (NT // 2))
            phase_end(pool, 4)
            pool.wait_ge(tok_set, 1)

            def gather_rows(q, r):
                u, k = q * (2 * SLOTS) + r, r % ROW5
                if not isinstance(u, int) or u >= ROW5:
                    pool.wait_ge(res_set, u - (ROW5 - 1))
                    settle()
                nc.gpsimd.tensor_copy(from_st[:, k:k + 1], from_i[:, bass.ds(u, 1)]).then_inc(idx5_set, 1)
                pool.wait_ge(idx5_set, u + 1)
                settle()
                pool.indirect_dma_start(row5[:, k, :], None, x1_table, bass.IndirectOffsetOnAxis(
                    from_st[:, k:k + 1].bitcast(U32), 0)).then_inc(row5_load[k], 16)

            def scatter_results(q, r):
                u, j = q * (2 * SLOTS) + r, r % 2
                pool.wait_ge(res_set, u + 1)
                settle()
                nc.gpsimd.tensor_copy(to_st[:, j:j + 1], tok_i[:, bass.ds(u, 1)]).then_inc(to_set, 1)
                pool.wait_ge(to_set, u + 1)
                settle()
                pool.indirect_dma_start(out, bass.IndirectOffsetOnAxis(to_st[:, j:j + 1].bitcast(U32), 0), res5[:, j, :],
                                        None, bounds_check=N - 1, oob_is_err=False).then_inc(res_store[j], 16)

            in_step(pool, SL, 2 * SLOTS, [(gather_rows, 0), (scatter_results, 4)])
            for j in range(2):
                pool.wait_ge(res_store[j], 16 * (SL // 2))

        @block.scalar
        def _(act):
            chain = Chain(act, act_chain)
            nc.scalar.preload_act_table_set("natural_log_exp_and_others")
            for n, d, s in ((0, bk_bc, bk), (1, bq_bc, bq)):
                act.dma_start(d[:, :], s.partition_broadcast(ROWS)).then_inc(bias_load[n], 16)
            act.dma_start(b1_col[:, :], b1.rearrange("(f p) -> p f", p=P), allow_slow_non_contiguous=True)\
               .then_inc(bias_load[2], 16)
            for r, a in enumerate((att_src1, att_dst1)):
                act.dma_start(att_bc[:, r, :], a.rearrange("h c -> (h c)").partition_broadcast(P))\
                   .then_inc(wload[f"att{r}"], 16)
            for n in range(3 * DC):
                act.wait_ge(wt_bank, n + 1)
                nc.scalar.activation(WTh["kvq"[n // DC]][:, n % DC, :], banks[n % 2][:, :], ACT.Copy).then_inc(wt_hi, 1)
            for n, h, st in (("W1", W1h, w1_st), ("W2", W2h, w2_st)):
                act.wait_ge(wload[n], 16)
                nc.scalar.activation(h[:, :, :], st[:, :, :], ACT.Copy).then_inc(w_hi, 1)
            act.sem_inc(y_free, SUBS)
            for j in range(2):
                act.sem_inc(y_store[j], 16)
            act.wait_ge(bias_load[2], 16)
            act.wait_ge(w_lo, 1)
            act.wait_ge(w2_lo, 1)
            act.wait_ge(att_sum, 2 * DC)
            def x_high(m, subs):
                sub0 = m * SUBS
                for s in subs:
                    act.wait_ge(xt_bank, sub0 + (s + 1))
                    nc.scalar.activation(xTh[:, :, s * ROWS:(s + 1) * ROWS],
                                         groups(banks[s % 2][:, 0:MACRO], DC), ACT.Copy).then_inc(xt_hi, 1)

            def keys_queries(sub0):
                for s in range(SUBS):
                    j = s % 2
                    act.wait_ge(kvq_bank, sub0 * 3 + (3 * s + 2))
                    nc.scalar.activation(vh[:, j, :, 0:P], groups(banks[2 + (3 * s + 1) % 2][0:ROWS, :], DC), ACT.Copy).then_inc(v_hi, 1)
                    for n, buf in ((0, kbuf), (1, qbuf)):
                        act.wait_ge(ssub, sub0 * 2 + (2 * s + n + 1))
                        nc.scalar.activation(buf[:, j, :], buf[:, j, :], ACT.Exp).then_inc(sexp, 1)
                    for f in (2 * s, 2 * s + 1):
                        act.wait_ge(h_bank, sub0 * 2 + (f + 1))
                        nc.scalar.activation(relu[:, f % 2, :], banks[4 + f % 2][:, 0:MACRO], ACT.Relu,
                                             bias=b1_col[:, f:f + 1])
                        nc.scalar.activation(h1h[:, f, :], banks[4 + f % 2][:, 0:MACRO], ACT.Relu,
                                             bias=b1_col[:, f:f + 1]).then_inc(h_hi, 1)
                    act.wait_ge(snorm_k, sub0 + (s + 1))
                    nc.scalar.activation(kh[:, j, :], kbuf[:, j, :], ACT.Copy).then_inc(k_hi, 1)

            def y_rows(m, sub0, s):
                j = s % 2
                act.wait_ge(y_store[j], m * 32 + (16 * (s // 2) + 16))
                act.wait_ge(y_bank, sub0 + (s + 1))
                ins = nc.scalar.activation(y2o[:, j, :], banks[2 + j][0:ROWS, :], ACT.Copy)
                ins.then_inc(y_free, 1)
                act.wait_ge(y_free, sub0 + (s + 1 + SUBS))
                act.dma_start(y2_table[bass.ds((m * SUBS + s) * ROWS, ROWS), :], y2o[:, j, :]).then_inc(y_store[j], 16)

            x_high(0, range(SUBS))
            with act.Fori(0, MACROS - 1) as m:
                sub0 = act.snap(m * SUBS)
                keys_queries(sub0)
                y_rows(m, sub0, 0)
                y_rows(m, sub0, 1)
                x_high(m + 1, (0, 1))
                y_rows(m, sub0, 2)
                x_high(m + 1, (2, 3))
                y_rows(m, sub0, 3)
            keys_queries((MACROS - 1) * SUBS)
            for s in range(SUBS):
                y_rows(MACROS - 1, (MACROS - 1) * SUBS, s)
            for j in range(2):
                act.wait_ge(y_store[j], 16 * (MACROS * SUBS // 2 + 1))

            phase_end(act, 1)
            act.sem_inc(e_src_out, 1)
            with act.Fori(0, ET) as t:
                act.wait_ge(e_bank, t * 2 + 5)
                nc.scalar.activation(xsT[:, :, bass.ds(t * ROWS, ROWS)], groups(banks[0][:, 0:MACRO], DC), ACT.Copy)\
                  .then_inc(e_src_out, 1)
            for b in range(E // MACRO):
                act.wait_ge(lg_bank, b + 1)
                c = slice(b * MACRO, (b + 1) * MACRO)
                nc.scalar.activation(head_e[:, c], banks[2 + b % 2][0:HEADS, 0:MACRO], ACT.Copy)
                nc.scalar.activation(head_s[:, c], banks[2 + b % 2][32:32 + HEADS, 0:MACRO], ACT.Copy).then_inc(lg_out, 1)
            exp_logits(act, 0)
            take_weights(act, 0)
            act.wait_ge(al_out[0], 2)

            def stage_high(t):
                for r, xT in enumerate((xsT, xdT)):
                    nc.scalar.activation(xsh[:, r, :, :], xT[:, :, bass.ds(t * ROWS, ROWS)], ACT.Copy).then_inc(st_hi, 1)

            def message_high(t):
                for h in range(2):
                    act.wait_ge(m_sum, t * 2 + (h + 1))
                    nc.scalar.activation(msgh[:, h * D:(h + 1) * D], msg[:, h, :], ACT.Copy).then_inc(m_hi, 1)

            def aggregate_high(t):
                act.wait_ge(ag_out, t + 1)
                nc.scalar.activation(aggh[:, :, :], aggT[:, :, :], ACT.Copy).then_inc(ag_hi, 1)

            def rows_out(t, first=False):
                act.wait_ge(ye_bank, t + 1)
                if not first:
                    act.wait_ge(ye_store, t * 16)
                nc.scalar.activation(y_edge[:, :], banks[6][0:ROWS, :], ACT.Copy).then_inc(ye_out, 1)

            act.sem_inc(ye_out, 1)
            stage_high(0)
            message_high(0)
            stage_high(1)
            aggregate_high(0)
            message_high(1)
            stage_high(2)
            rows_out(0, first=True)
            with act.Fori(1, ET - 2) as t:
                aggregate_high(t)
                message_high(t + 1)
                stage_high(t + 2)
                rows_out(t)
            aggregate_high(ET - 2)
            message_high(ET - 1)
            rows_out(ET - 2)
            aggregate_high(ET - 1)
            rows_out(ET - 1)
            phase_end(act, 2)
            act.sem_inc(g2_copied, 2)
            act.sem_inc(lt_out, 2)
            with act.Fori(0, ET // 2) as i:
                pair = act.snap(i * 2)
                for j in range(2):
                    act.wait_ge(g2_load[j], i * 32 + 32)
                    for r, all_ in enumerate((ys_all, yd_all)):
                        last = nc.scalar.activation(all_[:, bass.ds(i * 2 + j, 1), :].rearrange("p t d -> p (t d)"), g2[:, j, r, :],
                                                    ACT.Copy)
                    last.then_inc(g2_copied, 1)
                    act.wait_ge(lt_bank, pair + (j + 3))
                    col = bass.ds((i * 2 + j) * ROWS, ROWS)
                    nc.scalar.activation(head_e[:, col], banks[j][0:HEADS, 0:ROWS], ACT.Copy)
                    nc.scalar.activation(head_s[:, col], banks[j][0:HEADS, P:P + ROWS], ACT.Copy).then_inc(lt_out, 1)
            exp_logits(act, 1)
            take_weights(act, 1)
            with act.Fori(0, ET // 2) as i:
                pair = act.snap(i * 2)
                for j in range(2):
                    act.wait_ge(m2_set, pair + (j + 3))
                    nc.scalar.activation(m2h[:, j, :], m2[:, j, :], ACT.Copy).then_inc(m2_hi, 1)
                    act.wait_ge(z_bank, pair + (j + 1))
                    nc.scalar.activation(z32[:, j, :], banks[j][0:ROWS, :], ACT.Copy).then_inc(z_hi, 1)
                    nc.scalar.activation(zh[:, j, :], banks[j][0:ROWS, :], ACT.Copy).then_inc(z_hi, 1)
            phase_end(act, 3)
            for n in range(DC):
                act.wait_ge(wp_bank, n + 1)
                nc.scalar.activation(WpTh[:, n, :], banks[n % 2][:, :], ACT.Copy).then_inc(wp_hi, 1)
            act.wait_ge(sw_bank, 1)
            nc.scalar.activation(swT[:, :, :], groups(banks[2][:, 0:DC * EXPERTS], DC), ACT.Copy).then_inc(sw_out, 1)
            act.sem_inc(xft_out, 1)
            NT = MACROS * SUBS

            def q_high(q, r):
                act.wait_ge(qt_bank, q * G + (r + 1))
                nc.scalar.activation(qTh[:, r % 2, :, :], groups(banks[0][:, 0:MACRO], DC), ACT.Copy).then_inc(qt_hi, 1)

            def normalise(q, r):
                act.wait_ge(ln4_set, q * G + (r + 1))
                nc.scalar.activation(xf[:, r, :], x1row[:, r, 0:D], ACT.Identity, bias=x1row[:, r, D + 1:D + 2],
                                     scale=x1row[:, r, D:D + 1]).then_inc(xf_set, 1)

            def o_high(q, r):
                act.wait_ge(ot_bank, q * G + (r + 1))
                nc.scalar.activation(oTh[:, r % 2, :, :], groups(banks[3][:, 0:MACRO], DC), ACT.Copy).then_inc(ot_hi, 1)

            def exp_router(q, r):
                act.wait_ge(rt_max, q * G + (r + 1))
                nc.scalar.activation(ex16[:, r % 2, :], banks[6][0:ROWS, 16 * (r % 2):16 * (r % 2) + 16], ACT.Exp, bias=lstat[:, r % 2, 0:1],
                                     accum_out=lstat[:, r % 2, 1:2]).then_inc(rt_exp, 1)

            def log_sum(q, r):
                act.wait_ge(y_max, q * G + (r + 1))
                chain.link(nc.scalar.activation(exp_y[:, :], y_in[:, r, :], ACT.Exp, bias=y_stat[:, r % 2, 0:1],
                                                accum_out=y_stat[:, r % 2, 1:2]))
                chain.link(nc.scalar.activation(y_stat[:, r % 2, 2:3], y_stat[:, r % 2, 1:2], ACT.Ln))
                nc.scalar.activation(y_stat[:, r % 2, 3:4], y_stat[:, r % 2, 2:3], ACT.Identity, scale=-1.0,
                                     bias=y_stat[:, r % 2, 0:1]).then_inc(lse_set, 1)

            def xf_out(q, r):
                act.wait_ge(xft_bank, q * G + (r + 1))
                nc.scalar.activation(xfT[:, r % 2, :, :], groups(banks[5][:, 0:MACRO], DC), ACT.Copy).then_inc(xft_out, 1)

            def dropped_row(q, r):
                act.wait_ge(row_set, q * G + (r + 1))
                nc.scalar.activation(orow[:, r % 2, :], x1row[:, r, 0:D], ACT.Identity, bias=drop_line[:, r % 2, 1:2],
                                     scale=drop_line[:, r % 2, 0:1]).then_inc(orow_set, 1)

            in_step(act, NT, G, [(q_high, 0), (xf_out, 3), (o_high, 1), (exp_router, 3), (dropped_row, 4), (log_sum, 1), (normalise, 2)],
                    chain=chain, links=2 * G)
            phase_end(act, 4)
            def expert_high(q, r):
                if r % SLOTS:
                    return
                e, j = q * 2 + r // SLOTS, r // SLOTS
                for c in range(DC):
                    act.wait_ge(we_bank, e * DC + (c + 1))
                    nc.scalar.activation(WeTh[:, j, c, :], banks[c % 2][:, :], ACT.Copy).then_inc(we_hi, 1)

            def normal_rows(q, r):
                j, k = r % 2, r % ROW5
                act.wait_ge(row5_load[k], q * (16 * 2 * SLOTS // ROW5) + 16 * (r // ROW5 + 1))
                nc.scalar.activation(xf5[:, j, :], row5[:, k, 0:D], ACT.Identity, bias=row5[:, k, D + 1:D + 2],
                                     scale=row5[:, k, D:D + 1]).then_inc(x5_set, 1)

            def rows_high(q, r):
                act.wait_ge(f_bank, q * (2 * SLOTS) + (r + 1))
                nc.scalar.activation(fTh[:, r % 2, :, :], groups(banks[2 + r % 2][:, :], DC), ACT.Copy).then_inc(f_hi, 1)

            in_step(act, SL, 2 * SLOTS, [(expert_high, 0), (normal_rows, 1), (rows_high, 2)])

        @block.vector
        def _(dve):
            chain = Chain(dve, dve_chain)
            for n in range(3 * DC):
                dve.wait_ge(wt_hi, n + 1)
                nc.vector.tensor_tensor(WTl["kvq"[n // DC]][:, n % DC, :], banks[n % 2][:, :],
                                        WTh["kvq"[n // DC]][:, n % DC, :].bitcast(F32), ALU.subtract).then_inc(wt_lo, 1)
            dve.wait_ge(w_hi, 1)
            nc.vector.tensor_tensor(W1l[:, :, :], w1_st[:, :, :], W1h[:, :, :].bitcast(F32), ALU.subtract).then_inc(w_lo, 1)
            for r in range(2):
                dve.wait_ge(wload[f"att{r}"], 16)
            dve.wait_ge(const_done, CONSTS)
            for c in range(DC):
                for r in range(2):
                    chain.link(nc.vector.tensor_tensor(att_tmp[:, r, :], w1_st[:, c, :], att_bc[:, r, :], ALU.mult))
                    nc.vector.tensor_reduce(att1[:, c, 40 * r:40 * r + 8], groups(att_tmp[:, r, :], HEADS),
                                            AX.X, ALU.add).then_inc(att_sum, 1)
                    dve.wait_ge(att_sum, c * 2 + r + 1)
            nc.vector.tensor_tensor(att1[:, :, 72:80], att1[:, :, 0:8], att1[:, :, 40:48], ALU.add)
            for n in range(2):
                dve.wait_ge(bias_load[n], 16)
            dve.sem_inc(ctx_free, 2)
            dve.wait_ge(w2_lo, 1)
            nc.vector.memset(vl[:, :, :, P:P + 2].bitcast(F32), 0.0)
            nc.vector.memset(vh[:, :, :, P:P + 2].bitcast(F32), 1.0).then_inc(ones_done, 1)
            def layer_norm(m):
                dve.wait_ge(x_load, m * 16 + 16)
                for s in range(SUBS):
                    last = nc.vector.bn_stats(stats[:, s, :], xn[:, s, :])
                chain.link(last, dve_settled)
                for s in range(SUBS):
                    last = nc.vector.bn_aggr(mv[:, s, :], stats[:, s, :])
                chain.link(last)
                nc.vector.tensor_scalar(veps[:, :], mv[:, :, 1], EPS, None, ALU.add).then_inc(var_ready, 1)
                dve.wait_ge(rstd0, m + 1)
                refine(dve, chain, rstd[:, :], veps[:, :], newt)
                for s in range(SUBS):
                    nc.vector.tensor_scalar(xn[:, s, :], xn[:, s, :], mv[:, s, 0:1], rstd[:, s:s + 1],
                                            ALU.subtract, ALU.mult).then_inc(xn_ready, 1)

            def x_low(m):
                sub0 = m * SUBS
                for s in range(SUBS):
                    dve.wait_ge(xt_hi, sub0 + (s + 1))
                    nc.vector.tensor_tensor(xTl[:, :, s * ROWS:(s + 1) * ROWS], groups(banks[s % 2][:, 0:MACRO], DC),
                                            xTh[:, :, s * ROWS:(s + 1) * ROWS].bitcast(F32), ALU.subtract).then_inc(xt_lo, 1)

            def keys_queries(m, sub0):
                for s in range(SUBS):
                    j = s % 2
                    for n, buf, bias in ((0, kbuf, bk_bc), (1, qbuf, bq_bc)):
                        dve.wait_ge(kvq_bank, sub0 * 3 + (3 * s + 2 * n + 1))
                        if n:
                            dve.wait_ge(q_store[j], m * 32 + (16 * (s // 2) + 16))
                        nc.vector.tensor_tensor(buf[:, j, :], banks[2 + (3 * s + 2 * n) % 2][0:ROWS, :], bias[:, :],
                                                ALU.add).then_inc(kvq_free, 1)
                        dve.wait_ge(kvq_free, sub0 * 3 + (3 * s + 2 * n + 1))
                        nc.vector.tensor_reduce(kq_max[:, j, n, :], groups(buf[:, j, :], HEADS), AX.X, ALU.max).then_inc(smax, 1)
                        if n == 0:
                            dve.wait_ge(v_hi, sub0 + (s + 1))
                            nc.vector.tensor_tensor(vl[:, j, :, 0:P], groups(banks[2 + (3 * s + 1) % 2][0:ROWS, :], DC),
                                                    vh[:, j, :, 0:P].bitcast(F32), ALU.subtract).then_inc(kvq_free, 1)
                    for n, buf in ((0, kbuf), (1, qbuf)):
                        dve.wait_ge(sexp, sub0 * 2 + (2 * s + n + 1))
                        chain.link(nc.vector.tensor_reduce(kq_rec[:, j, n, :], groups(buf[:, j, :], HEADS), AX.X, ALU.add))
                        nc.vector.reciprocal(kq_rec[:, j, n, :], kq_rec[:, j, n, :]).then_inc(srec, 1)
                    dve.wait_ge(k_hi, sub0 + (s + 1))
                    nc.vector.tensor_tensor(kl[:, j, :], kbuf[:, j, :], kh[:, j, :].bitcast(F32),
                                            ALU.subtract).then_inc(k_lo, 1)
                    if s:
                        add_context(dve, chain, sub0, s - 1)

            layer_norm(0)
            x_low(0)
            with dve.Fori(0, MACROS - 1) as m:
                sub0 = dve.snap(m * SUBS)
                chain.enter(m, DVE_LINKS)
                keys_queries(m, sub0)
                layer_norm(m + 1)
                add_context(dve, chain, sub0, SUBS - 1)
                x_low(m + 1)
            chain.leave(MACROS - 1)
            keys_queries(MACROS - 1, (MACROS - 1) * SUBS)
            add_context(dve, chain, (MACROS - 1) * SUBS, SUBS - 1)
            phase_end(dve, 1)
            dve.wait_ge(edge_load["dst"], 16)
            dve.wait_ge(edge_load["next"], 32)
            nc.vector.tensor_copy(dst_f[:, :], dst_i[:, :])
            chain.link(nc.vector.tensor_copy(next_f[:, :], next_i[:, :]))
            chain.link(nc.vector.tensor_tensor(next_f[:, :], dst_f[:, :], next_f[:, :], ALU.is_equal))
            nc.vector.scalar_tensor_tensor(out=scat_i[:, :], in0=next_f[:, :], scalar=float(FAR), in1=dst_f[:, :],
                                           op0=ALU.mult, op1=ALU.add).then_inc(edge_f, 1)
            nc.vector.memset(dst_bc[:, 0:1], -1.0)
            nc.vector.memset(dst_bc[:, E + 1:E + 2], -1.0)
            dve.wait_ge(edge_load["all"], 16)
            chain.link(nc.vector.tensor_copy(dst_bc[:, 1:E + 1], dst_bi[:, :]))
            dve.sem_inc(e_dst_out, 1)
            with dve.Fori(0, ET // 2) as i:
                pair = dve.snap(i * 2)
                chain.enter(i, 2 * 6)
                for j in range(2):
                    dve.wait_ge(e_gath[j], i * 32 + 32)
                    for r in range(2):
                        last = nc.vector.bn_stats(e_stats[:, r, :], gath[:, j, r, :])
                    chain.link(last, dve_settled)
                    for r in range(2):
                        last = nc.vector.bn_aggr(e_mv[:, r, :], e_stats[:, r, :])
                    chain.link(last)
                    nc.vector.tensor_scalar(e_veps[:, :], e_mv[:, :, 1], EPS, None, ALU.add).then_inc(e_var, 1)
                    dve.wait_ge(e_rstd0, pair + (j + 1))
                    refine(dve, chain, e_rstd[:, :], e_veps[:, :], e_newt)
                    for r in range(2):
                        last = nc.vector.tensor_scalar(gath[:, j, r, :], gath[:, j, r, :], e_mv[:, r, 0:1],
                                                       e_rstd[:, r:r + 1], ALU.subtract, ALU.mult)
                    last.then_inc(e_xn, 1)
                for j in range(2):
                    dve.wait_ge(e_bank, pair * 2 + (2 * j + 6))
                    nc.vector.tensor_copy(xdT[:, :, bass.ds((i * 2 + j) * ROWS, ROWS)],
                                          groups(banks[1][:, 0:MACRO], DC)).then_inc(e_dst_out, 1)
            chain.leave(ET // 2)
            dve.wait_ge(lg_out, E // MACRO)
            edge_softmax(dve, chain, 0)
            dve.wait_ge(al_out[0], 2)
            nc.vector.memset(carry[:, :], 0.0)
            nc.vector.memset(same_dst[:, ROWS:ROWS + 1].bitcast(F32), 0.0)
            with dve.Fori(0, ET) as t:
                chain.enter(t, 3)
                for h in range(2):
                    dve.wait_ge(hm_bank, t * 2 + (h + 1))
                    hs = slice(h * HEADS // 2, (h + 1) * HEADS // 2)
                    for d, b, a in ((msg, 2 * h, alpha_e), (msg_self, 2 * h + 1, alpha_s)):
                        last = nc.vector.tensor_tensor(groups(d[:, h, :], HEADS // 2), groups(banks[b][0:ROWS, :], HEADS // 2),
                                                       spread(a[:, bass.ds(t, 1), hs].rearrange("p t h -> p (t h)"), HID),
                                                       ALU.mult)
                    last.then_inc(m_self, 1)
                nc.vector.tensor_scalar(same_dst[:, 0:ROWS], dst_bc[0:ROWS, bass.ds(t * ROWS + 1, ROWS)],
                                        dst_f[:, bass.ds(t, 1)], None, ALU.is_equal).then_inc(mask_set, 1)
                chain.link(nc.vector.tensor_scalar(goes_on[:, :], dst_bc[:, bass.ds(t * ROWS + 1, ROWS)],
                                                   dst_bc[:, bass.ds(t * ROWS, 1)], None, ALU.is_equal))
                dve.wait_ge(ag_bank, t + 1)
                for f in range(FC):
                    c = (f % DC) * (ROWS + 1)
                    last = nc.vector.scalar_tensor_tensor(out=aggT[:, f, :], in0=goes_on[:, :], scalar=carry[:, f:f + 1],
                                                          in1=banks[4 + f // DC][:, c:c + ROWS], op0=ALU.mult, op1=ALU.add)
                chain.link(last)
                chain.link(nc.vector.tensor_copy(carry[:, :], aggT[:, :, ROWS - 1]))
                for f in range(FC):
                    last = nc.vector.tensor_scalar(aggT[:, f, :], aggT[:, f, :], b1_col[:, f:f + 1], 0.0, ALU.add, ALU.max)
                last.then_inc(ag_out, 1)
            chain.leave(ET)
            phase_end(dve, 2)
            dve.wait_ge(att2_load, 32)
            dve.sem_inc(logit2_set, 2)
            dve.sem_inc(m2_set, 2)
            with dve.Fori(0, ET // 2) as i:
                pair = dve.snap(i * 2)
                chain.enter(i, 2 * 2)
                for j in range(2):
                    dve.wait_ge(g2_load[j], i * 32 + 32)
                    for r in range(2):
                        last = nc.vector.tensor_tensor(prod2[:, r, :], g2[:, j, r, :], att2_bc[:, 0, :], ALU.mult)
                    chain.link(last)
                    dve.wait_ge(p2_pool, pair + (j + 1))
                    chain.link(nc.vector.tensor_reduce(dots[:, :, :].rearrange("p r h -> p (r h)"),
                                                       prod2[:, :, :].rearrange("p r (h c) -> p (r h) c", h=HEADS), AX.X, ALU.add))
                    dve.wait_ge(lt_bank, pair + (j + 1))
                    nc.vector.tensor_tensor(logit2[:, j, :].rearrange("p (r h) -> p r h", r=2), dots[:, 0:2, :],
                                            dots[:, 2, :].unsqueeze(1).to_broadcast([ROWS, 2, HEADS]), ALU.add).then_inc(logit2_set, 1)
            chain.leave(ET // 2)
            dve.wait_ge(lt_out, ET + 2)
            edge_softmax(dve, chain, 1)
            dve.wait_ge(al_out[1], 2)
            nc.vector.memset(zh[:, 1, :].bitcast(F32), 0.0)
            nc.vector.memset(zl[:, 1, :].bitcast(F32), 0.0).then_inc(z_lo, 1)
            with dve.Fori(0, ET // 2) as i:
                pair = dve.snap(i * 2)
                chain.enter(i, 2)
                for j in range(2):
                    t = i * 2 + j
                    chain.link(nc.vector.tensor_tensor(groups(m2[:, j, :], HEADS),
                                                       groups(ys_all[:, bass.ds(t, 1), :].rearrange("p t d -> p (t d)"), HEADS),
                                                       spread(alpha_e[:, bass.ds(t, 1), :].rearrange("p t h -> p (t h)"), CLS),
                                                       ALU.mult))
                    dve.wait_ge(m2s_set, pair + (j + 1))
                    nc.vector.tensor_tensor(m2[:, j, :], m2[:, j, :], m2s[:, j, :], ALU.add).then_inc(m2_set, 1)
                    tgt = dst_bc[0:ROWS, bass.ds(t * ROWS + 1, ROWS)]
                    nc.vector.tensor_scalar(same2[:, j, :], tgt, dst_f[:, bass.ds(t, 1)], None, ALU.is_equal)
                    nc.vector.tensor_scalar(goes2[:, j, :], tgt, dst_bc[0:ROWS, bass.ds(t * ROWS, 1)], last_row[:, :],
                                            ALU.is_equal, ALU.mult).then_inc(mask2_set, 1)
                    dve.wait_ge(z_hi, pair * 2 + (2 * j + 2))
                    nc.vector.tensor_tensor(zl[:, j, :], banks[j][0:ROWS, :], zh[:, j, :].bitcast(F32), ALU.subtract).then_inc(z_lo, 1)
            chain.leave(ET // 2)
            phase_end(dve, 3)
            for n in range(DC):
                dve.wait_ge(wp_hi, n + 1)
                nc.vector.tensor_tensor(WpTl[:, n, :], banks[n % 2][:, :], WpTh[:, n, :].bitcast(F32), ALU.subtract).then_inc(wp_lo, 1)
            dve.wait_ge(p4_bv, 16)
            dve.wait_ge(p4_bias, 32)
            chain.link(nc.vector.memset(pairs[:, :, :, :], 0.0))
            H = P // 2
            for p in range(DC):
                for k in range(2):
                    c = slice(p * P + k * H, p * P + (k + 1) * H)
                    nc.vector.scalar_tensor_tensor(out=pairs[k * H:(k + 1) * H, p, k, 0:HD], in0=bv_bc[k * H:(k + 1) * H, c],
                                                   scalar=ctx_acc[k * H:(k + 1) * H, p, P:P + 1],
                                                   in1=ctx_acc[k * H:(k + 1) * H, p, k * H:(k + 1) * H],
                                                   op0=ALU.mult, op1=ALU.add)
            for k in range(2):
                last = nc.vector.tensor_copy(pairs[k * H:(k + 1) * H, :, k, HD:HD + 1], ctx_acc[k * H:(k + 1) * H, :, P:P + 1])
            chain.link(last)
            pair_cols = pairs[:, :, :, :].rearrange("p d k c -> p d (k c)")
            nc.vector.memset(ones_row[:, :].bitcast(F32), 1.0)
            nc.vector.memset(ones_row32[:, :], 1.0)
            nc.vector.tensor_copy(bp_h[:, :], bp_bc[0:1, :])
            chain.link(nc.vector.tensor_copy(pairs_h[:, :, :], pair_cols))
            nc.vector.tensor_tensor(bp_l[:, :], bp_bc[0:1, :], bp_h[:, :].bitcast(F32), ALU.subtract)
            nc.vector.tensor_tensor(pairs_l[:, :, :], pair_cols, pairs_h[:, :, :].bitcast(F32), ALU.subtract).then_inc(ctx_ready, 1)
            dve.wait_ge(const4, 3)
            nc.vector.tensor_copy(iota16[:, :], iota_f[:, :])
            nc.vector.tensor_copy(steps128[:, :], steps_i[:, :])
            nc.vector.memset(used[:, :], 0.0)
            chain.link(nc.vector.tensor_copy(rowid[0:ROWS, 0:1], row_0[:, :]))
            dve.wait_ge(p4_sb, 16)
            dve.sem_inc(orow_set, G)
            for s_ in (qt_lo, num_out, ot_lo, x1_set, row_free, rank_set):
                dve.sem_inc(s_, 1)
            NT = MACROS * SUBS

            def q_low(q, r):
                dve.wait_ge(qt_hi, q * G + (r + 1))
                nc.vector.tensor_tensor(qTl[:, r % 2, :, :], groups(banks[0][:, 0:MACRO], DC), qTh[:, r % 2, :, :].bitcast(F32),
                                        ALU.subtract).then_inc(qt_lo, 1)

            def o_low(q, r):
                dve.wait_ge(ot_hi, q * G + (r + 1))
                nc.vector.tensor_tensor(oTl[:, r % 2, :, :], groups(banks[3][:, 0:MACRO], DC), oTh[:, r % 2, :, :].bitcast(F32),
                                        ALU.subtract).then_inc(ot_lo, 1)

            def largest_y(q, r):
                dve.wait_ge(b_added, q * (2 * G) + (2 * r + 1))
                nc.vector.tensor_reduce(y_stat[:, r % 2, 0:1], y_in[:, r, :], AX.X, ALU.max, negate=True).then_inc(y_max, 1)

            def route_max(q, r):
                dve.wait_ge(rt_bank, q * G + (r + 1))
                nc.vector.tensor_reduce(lstat[:, r % 2, 0:1], banks[6][0:ROWS, 16 * (r % 2):16 * (r % 2) + 16], AX.X, ALU.max,
                                        negate=True).then_inc(rt_max, 1)

            def residual(q, r):
                j = r % 2
                dve.wait_ge(lse_set, q * G + (r + 1))
                dve.wait_ge(x1_store[r], q * 16 + 16)
                dve.wait_ge(orow_set, q * G + (r + 1))
                dve.wait_ge(b_added, q * (2 * G) + (2 * r + 2))
                dve.wait_ge(mix_bank, q * G + (r + 1))
                nc.vector.scalar_tensor_tensor(out=x1row[:, r, 0:D], in0=banks[4][0:ROWS, :], scalar=y_stat[:, j, 3:4],
                                               in1=x_in[:, r, :], op0=ALU.add, op1=ALU.add).then_inc(x1_set, 1)

            def x1_stats(q, r):
                dve.wait_ge(x1_set, q * G + (r + 2))
                dve.sem_inc(dve_settled, 1)
                chain.mark("stats", nc.vector.bn_stats(stats4[:, :], x1row[:, r, 0:D]))

            def x1_mean(q, r):
                chain.need("stats", dve_settled)
                chain.mark("mean", nc.vector.bn_aggr(mv4[:, r % 2, :], stats4[:, :]))

            def x1_var(q, r):
                chain.need("mean")
                nc.vector.tensor_scalar(veps4[:, r % 2, :], mv4[:, r % 2, 1:2], EPS, None, ALU.add).then_inc(v4_set, 1)

            def square(q, r):
                dve.wait_ge(r4_set, q * G + (r + 1))
                chain.mark("square", nc.vector.tensor_tensor(newt4[:, :], r4[:, r % 2, :], r4[:, r % 2, :], ALU.mult))

            def square_by_var(q, r):
                chain.need("square")
                chain.mark("by_var", nc.vector.tensor_tensor(newt4[:, :], newt4[:, :], veps4[:, r % 2, :], ALU.mult))

            def newton_factor(q, r):
                chain.need("by_var")
                chain.mark("factor", nc.vector.tensor_scalar(newt4[:, :], newt4[:, :], -0.5, 1.5, ALU.mult, ALU.add))

            def newton_rstd(q, r):
                chain.need("factor")
                chain.mark("rstd", nc.vector.tensor_tensor(x1row[:, r, D:D + 1], r4[:, r % 2, :], newt4[:, :], ALU.mult))

            def newton_shift(q, r):
                chain.need("rstd")
                nc.vector.scalar_tensor_tensor(out=x1row[:, r, D + 1:D + 2], in0=mv4[:, r % 2, 0:1], scalar=-1.0,
                                               in1=x1row[:, r, D:D + 1], op0=ALU.mult, op1=ALU.mult).then_inc(ln4_set, 1)

            def largest_prob(q, r):
                dve.wait_ge(rt_exp, q * G + (r + 1))
                dve.sem_inc(dve_settled, 1)
                chain.mark("top", nc.vector.max(top8[:, :], ex16[:, r % 2, :]))
                nc.vector.reciprocal(lstat[:, r % 2, 2:3], lstat[:, r % 2, 1:2])

            def its_expert(q, r):
                chain.need("top", dve_settled)
                chain.mark("arg", nc.vector.max_index(arg8[:, :], top8[:, :], ex16[:, r % 2, :]))

            def expert_number(q, r):
                chain.need("arg")
                chain.mark("argf", nc.vector.tensor_copy(argf[:, r % 2, :], arg8[:, 0:1]))
                nc.vector.tensor_tensor(x1row[:, r, D + 2:D + 3], top8[:, 0:1], lstat[:, r % 2, 2:3], ALU.mult)

            def one_hot(q, r):
                chain.need("argf")
                nc.vector.tensor_scalar(onehot[:, r % 2, :], iota16[0:ROWS, :], argf[:, r % 2, :], None, ALU.is_equal).then_inc(oh_set, 1)

            half = HEADS // 2
            heads = [groups(banks[1 + b][0:ROWS, 0:half * (HD + 1)], half) for b in range(2)]

            def attend_sums(q, r):
                dve.wait_ge(num_bank, q * G + (r + 1))
                for b in range(2):
                    last = nc.vector.reciprocal(den[:, r % 2, b * half:(b + 1) * half], heads[b][:, :, HD])
                chain.mark("den", last)

            def attend(q, r):
                j = r % 2
                chain.need("den")
                for b in range(2):
                    last = nc.vector.tensor_tensor(groups(attn[:, j, b * D // 2:(b + 1) * D // 2], half), heads[b][:, :, 0:HD],
                                                   spread(den[:, j, b * half:(b + 1) * half], HD), ALU.mult)
                last.then_inc(num_out, 1)

            def queue(q, r):
                dve.wait_ge(pf_bank, q * G + (r + 1))
                chain.mark("rank", nc.vector.tensor_tensor(rank[:, :], banks[7][0:ROWS, 0:16], used[:, :], ALU.add))

            def queue_ends(q, r):
                chain.need("rank")
                chain.mark("used", nc.vector.tensor_tensor(used[:, :], banks[7][0:ROWS, 16:32], used[:, :], ALU.add))
                nc.vector.scalar_tensor_tensor(out=rank[:, :], in0=rank[:, :], scalar=1.0, in1=onehot[:, r % 2, :],
                                               op0=ALU.mult, op1=ALU.mult, accum_out=small[:, 0:1]).then_inc(rank_set, 1)

            def slot_terms(q, r):
                dve.wait_ge(rank_set, q * G + (r + 2))
                nc.vector.tensor_scalar(steps_tmp[:, :], steps128[:, :], small[:, 0:1], None, ALU.is_le, ALU.add,
                                        accum_out=small[:, 1:2])
                nc.vector.tensor_scalar(small[:, 2:3], small[:, 0:1], float(SL), None, ALU.mult)
                nc.vector.tensor_scalar(small[:, 3:4], small[:, 0:1], float(CAP), float(FAR), ALU.is_ge, ALU.mult)
                chain.mark("terms", nc.vector.tensor_scalar(small[:, 4:5], small[:, 0:1], float(CAP), float(FAR),
                                                            ALU.is_lt, ALU.mult))

            def slot_place(q, r):
                chain.need("terms")
                chain.mark("slot", nc.vector.scalar_tensor_tensor(out=small[:, 5:6], in0=small[:, 1:2], scalar=float(1 - P * SL),
                                                                  in1=small[:, 2:3], op0=ALU.mult, op1=ALU.add))

            def slot_full(q, r):
                chain.need("slot")
                chain.mark("full", nc.vector.scalar_tensor_tensor(out=small[:, 6:7], in0=argf[:, r % 2, :], scalar=float(SLOTS),
                                                                  in1=small[:, 5:6], op0=ALU.mult, op1=ALU.add))

            def slot_rows(q, r):
                j = r % 2
                dve.wait_ge(row_free, q * G + (r + 1))
                nc.vector.tensor_tensor(row_i[:, j:j + 1], rowid[0:ROWS, 0:1], small[:, 4:5], ALU.add)
                nc.vector.tensor_scalar(drop_line[:, j, 0:1], x1row[:, r, D:D + 1], x1row[:, r, D + 2:D + 3], 1.0,
                                        ALU.mult, ALU.add)
                nc.vector.tensor_tensor(drop_line[:, j, 1:2], x1row[:, r, D + 1:D + 2], x1row[:, r, D + 2:D + 3], ALU.mult)
                chain.mark("token", nc.vector.tensor_copy(token_i[:, j:j + 1], rowid[0:ROWS, 0:1]))

            def slot_done(q, r):
                chain.need("token")
                chain.need("full")
                nc.vector.tensor_tensor(slot_i[:, r % 2:r % 2 + 1], small[:, 6:7], small[:, 3:4], ALU.add)
                nc.vector.tensor_scalar(rowid[0:ROWS, 0:1], rowid[0:ROWS, 0:1], float(ROWS), None, ALU.add).then_inc(row_set, 1)

            nc.vector.memset(x1row[:, :, D + 3:D + 4], 0.0)
            in_step(dve, NT, G, [(queue, 4), (q_low, 0), (queue_ends, 4), (residual, 2), (slot_terms, 4), (o_low, 1), (slot_place, 4), (x1_stats, 2), (slot_full, 4), (slot_rows, 4), (route_max, 3), (x1_mean, 2), (x1_var, 2), (slot_done, 4), (largest_y, 1), (square, 2), (largest_prob, 3), (square_by_var, 2), (its_expert, 3), (newton_factor, 2), (expert_number, 3), (newton_rstd, 2), (attend_sums, 0), (newton_shift, 2), (one_hot, 3), (attend, 0)],
                chain=chain, links=G * LINKS4)
            phase_end(dve, 4)
            dve.wait_ge(tok_load, 16)
            chain.link(nc.vector.tensor_copy(tok_f[:, :], tok_i[:, :]))
            nc.vector.tensor_scalar(from_i[:, :], tok_f[:, :], float(N - 1), None, ALU.min).then_inc(tok_set, 1)
            dve.sem_inc(y5_out, 2)
            dve.sem_inc(f_lo, 2)

            def expert_low(q, r):
                if r % SLOTS:
                    return
                e, j = q * 2 + r // SLOTS, r // SLOTS
                for c in range(DC):
                    dve.wait_ge(we_hi, e * DC + (c + 1))
                    nc.vector.tensor_tensor(WeTl[:, j, c, :], banks[c % 2][:, :], WeTh[:, j, c, :].bitcast(F32),
                                            ALU.subtract).then_inc(we_lo, 1)

            def rows_low(q, r):
                dve.wait_ge(f_hi, q * (2 * SLOTS) + (r + 1))
                nc.vector.tensor_tensor(fTl[:, r % 2, :, :], groups(banks[2 + r % 2][:, :], DC),
                                        fTh[:, r % 2, :, :].bitcast(F32), ALU.subtract).then_inc(f_lo, 1)

            def finish_rows(q, r):
                u, j, k = q * (2 * SLOTS) + r, r % 2, r % ROW5
                if r % SLOTS == 0:
                    dve.wait_ge(eb_load[r // SLOTS], q * 16 + 16)
                dve.wait_ge(y5_bank, u + 1)
                nc.vector.tensor_tensor(yb5[:, j, :], banks[4 + j][:, :], eb_bc[:, r // SLOTS, :], ALU.add).then_inc(y5_out, 1)
                dve.wait_ge(y5_out, u + 3)
                if not isinstance(u, int) or u >= 2:
                    dve.wait_ge(res_store[j], q * (16 * SLOTS) + 16 * (r // 2))
                nc.vector.scalar_tensor_tensor(out=res5[:, j, :], in0=yb5[:, j, :], scalar=row5[:, k, D + 2:D + 3],
                                               in1=row5[:, k, 0:D], op0=ALU.mult, op1=ALU.add).then_inc(res_set, 1)

            in_step(dve, SL, 2 * SLOTS, [(expert_low, 0), (rows_low, 2), (finish_rows, 3)])

        @block.tensor
        def _(pe):
            pe.wait_ge(const_done, 1)
            for n in range(3 * DC):
                if n % DC == 0:
                    pe.wait_ge(wload["kvq"[n // DC]], 16)
                if n >= 2:
                    pe.wait_ge(wt_lo, n - 1)
                st = (wk_st, wv_st, wq_st)[n // DC]
                for c in range(DC):
                    last = nc.tensor.transpose(banks[n % 2][:, c * P:(c + 1) * P],
                                               st[:, c, (n % DC) * P:(n % DC + 1) * P], ident[:, :])
                last.then_inc(wt_bank, 1)
            pe.wait_ge(wt_lo, 3 * DC)
            pe.wait_ge(w_lo, 1)
            pe.wait_ge(w2_lo, 1)
            pe.wait_ge(ones_done, 1)
            def turn(m, subs):
                sub0 = m * SUBS
                for s in subs:
                    if s == 0:
                        pe.wait_ge(xn_ready, sub0 + SUBS)
                    if s >= 2:
                        pe.wait_ge(xt_lo, sub0 + (s - 1))
                    for c in range(DC):
                        last = nc.tensor.transpose(banks[s % 2][:, c * ROWS:(c + 1) * ROWS], xn[:, s, c * P:(c + 1) * P],
                                                   ident[0:ROWS, 0:ROWS])
                    last.then_inc(xt_bank, 1)

            def macro_tile(m, sub0, sub3, more):
                def context(s):
                    j = s % 2
                    pe.wait_ge(k_lo, sub0 + (s + 1))
                    pe.wait_ge(ctx_free, sub0 * 2 + (2 * s + 2))
                    for p in range(DC):
                        c = slice(p * P, (p + 1) * P)
                        last = products(banks[6 + p // 2][:, p % 2 * (P + 2):(p % 2 + 1) * (P + 2)],
                                        [(kh[:, j, c], kl[:, j, c], vh[:, j, p, :], vl[:, j, p, :])])
                    last.then_inc(ctx_bank, 1)

                for s in range(SUBS):
                    pe.wait_ge(xt_lo, sub0 + (s + 1) if s else sub0 + 1)
                    r = slice(s * ROWS, (s + 1) * ROWS)
                    for n, w in enumerate("kvq"):
                        u = 3 * s + n
                        if u >= 2:
                            pe.wait_ge(kvq_free, sub3 + (u - 1))
                        else:
                            pe.wait_ge(y_free, sub0 + (SUBS - 1 + u))
                        products(banks[2 + u % 2][0:ROWS, :], [(xTh[:, c, r], xTl[:, c, r], WTh[w][:, c, :], WTl[w][:, c, :])
                                                               for c in range(DC)]).then_inc(kvq_bank, 1)
                    if s == 0:
                        pe.wait_ge(xt_lo, sub0 + SUBS)
                    for f in (2 * s, 2 * s + 1):
                        if f >= 2:
                            pe.wait_ge(h_hi, sub0 * 2 + (f - 1))
                        fs = slice(f * P, (f + 1) * P)
                        products(banks[4 + f % 2][:, 0:MACRO], [(W1h[:, c, fs], W1l[:, c, fs], xTh[:, c, :], xTl[:, c, :])
                                                                for c in range(DC)]).then_inc(h_bank, 1)
                    if s:
                        context(s - 1)
                for s in range(SUBS):
                    r = slice(s * ROWS, (s + 1) * ROWS)
                    if s < 2:
                        pe.wait_ge(kvq_free, sub3 + (3 * SUBS - 1 + s))
                    else:
                        pe.wait_ge(y_free, sub0 + (SUBS + s - 1))
                    for f in range(FC):
                        if s == 0:
                            pe.wait_ge(h_lo, sub0 * 2 + (f + 1))
                        last = products(banks[2 + s % 2][0:ROWS, :], [(h1h[:, f, r], h1l[:, f, r], W2h[:, f, :], W2l[:, f, :])],
                                        first=f == 0, more=f < FC - 1)
                    last.then_inc(y_bank, 1)
                    if s == 0:
                        context(SUBS - 1)
                    elif s < 3 and more:
                        turn(m + 1, (2 * s - 2, 2 * s - 1))
            turn(0, range(SUBS))
            with pe.Fori(0, MACROS - 1) as m:
                macro_tile(m, pe.snap(m * SUBS), pe.snap(m * (3 * SUBS)), more=True)
            macro_tile(MACROS - 1, (MACROS - 1) * SUBS, (MACROS - 1) * (3 * SUBS), more=False)
            phase_end(pe, 1)
            pe.sem_inc(e_bank, 4)
            with pe.Fori(0, ET // 2) as i:
                pair = pe.snap(i * 2)
                for j in range(2):
                    pe.wait_ge(e_xn, pair + (j + 1))
                    for r, out_done in ((0, e_src_out), (1, e_dst_out)):
                        pe.wait_ge(out_done, pair + (j + 1))
                        for c in range(DC):
                            last = nc.tensor.transpose(banks[r][:, c * ROWS:(c + 1) * ROWS], gath[:, j, r, c * P:(c + 1) * P],
                                                       ident[0:ROWS, 0:ROWS])
                        last.then_inc(e_bank, 1)
            pe.wait_ge(e_src_out, ET + 1)
            pe.wait_ge(e_dst_out, ET + 1)
            for b in range(E // MACRO):
                if b >= 2:
                    pe.wait_ge(lg_out, b - 1)
                e = slice(b * MACRO, (b + 1) * MACRO)
                for n, (xT, a) in enumerate(((xsT, 0), (xdT, 40))):
                    for c in range(DC):
                        last = nc.tensor.matmul(banks[2 + b % 2][0:40, 0:MACRO], att1[:, c, a:a + 40], xT[:, c, e],
                                                start=n + c == 0, stop=n == 1 and c == DC - 1)
                last.then_inc(lg_bank, 1)
            weights_by_edge(pe, 0)
            pe.wait_ge(al_out[0], 2)
            pe.wait_ge(lg_out, E // MACRO)

            def hidden_rows(t, first=False):
                pe.wait_ge(st_lo, t * 2 + 2)
                for h in range(2):
                    if not first:
                        pe.wait_ge(m_self, t * 2 + (h - 1))
                    for r in range(2):
                        last = products(banks[2 * h + r][0:ROWS, :],
                                        [(xsh[:, r, c, :], xsl[:, r, c, :], W1h[:, c, h * D:(h + 1) * D], W1l[:, c, h * D:(h + 1) * D])
                                         for c in range(DC)])
                    last.then_inc(hm_bank, 1)

            def aggregate(t):
                pe.wait_ge(mask_set, t + 1)
                pe.wait_ge(m_lo, t * 2 + 2)
                for f in range(FC):
                    c = (f % DC) * (ROWS + 1)
                    o = banks[4 + f // DC][:, c:c + ROWS + 1]
                    nc.tensor.matmul(o, msgh[:, f * P:(f + 1) * P], same_dst[:, :], start=True, stop=False)
                    last = nc.tensor.matmul(o, msgl[:, f * P:(f + 1) * P], same_dst[:, :], start=False, stop=True)
                last.then_inc(ag_bank, 1)

            def edge_rows(t):
                pe.wait_ge(ag_lo, t + 1)
                pe.wait_ge(ye_out, t + 1)
                products(banks[6][0:ROWS, :], [(aggh[:, f, :], aggl[:, f, :], W2h[:, f, :], W2l[:, f, :])
                                               for f in range(FC)]).then_inc(ye_bank, 1)

            hidden_rows(0, first=True)
            aggregate(0)
            with pe.Fori(0, ET - 1) as t:
                hidden_rows(t + 1)
                edge_rows(t)
                aggregate(t + 1)
            edge_rows(ET - 1)
            phase_end(pe, 2)
            pe.sem_inc(lt_bank, 2)
            with pe.Fori(0, ET // 2) as i:
                pair = pe.snap(i * 2)
                for j in range(2):
                    pe.wait_ge(logit2_set, pair + (j + 3))
                    pe.wait_ge(lt_out, pair + (j + 1))
                    nc.tensor.transpose(banks[j][0:HEADS, 0:ROWS], logit2[:, j, 0:HEADS], ident[0:ROWS, 0:ROWS])
                    nc.tensor.transpose(banks[j][0:HEADS, P:P + ROWS], logit2[:, j, HEADS:2 * HEADS],
                                        ident[0:ROWS, 0:ROWS]).then_inc(lt_bank, 1)
            pe.wait_ge(lt_out, ET + 2)
            weights_by_edge(pe, 1)
            pe.wait_ge(al_out[1], 2)
            with pe.Fori(0, ET // 2) as i:
                pair = pe.snap(i * 2)
                for j in range(2):
                    pe.wait_ge(mask2_set, pair + (j + 1))
                    pe.wait_ge(m2_lo, pair + (j + 1))
                    pe.wait_ge(z_lo, pair + (j + 1))
                    z = banks[j][0:ROWS, :]
                    nc.tensor.matmul(z, same2[:, j, :], m2h[:, j, :], start=True, stop=False)
                    nc.tensor.matmul(z, same2[:, j, :], m2l[:, j, :], start=False, stop=False)
                    nc.tensor.matmul(z, goes2[:, j, :], zh[:, 1 - j, :], start=False, stop=False)
                    nc.tensor.matmul(z, goes2[:, j, :], zl[:, 1 - j, :], start=False, stop=True).then_inc(z_bank, 1)
            phase_end(pe, 3)
            pe.wait_ge(p4_load, 16)
            for n in range(DC):
                if n >= 2:
                    pe.wait_ge(wp_lo, n - 1)
                for c in range(DC):
                    last = nc.tensor.transpose(banks[n % 2][:, c * P:(c + 1) * P], wp_st[:, c, n * P:(n + 1) * P], ident[:, :])
                last.then_inc(wp_bank, 1)
            pe.wait_ge(p4_sw, 16)
            for c in range(DC):
                last = nc.tensor.transpose(banks[2][:, c * EXPERTS:(c + 1) * EXPERTS], sw_st[:, c * P:(c + 1) * P],
                                           ident[0:EXPERTS, 0:EXPERTS])
            last.then_inc(sw_bank, 1)
            pe.wait_ge(sw_out, 1)
            pe.wait_ge(wp_lo, DC)
            pe.wait_ge(ctx_ready, 1)
            pe.wait_ge(p4_sb, 16)

            def q_turn(q, r):
                t = q * G + r
                pe.wait_ge(q4_load[r], q * 16 + 16)
                pe.wait_ge(qt_lo, t + 1)
                for c in range(DC):
                    last = nc.tensor.transpose(banks[0][:, c * ROWS:(c + 1) * ROWS], q_in[:, r, c * P:(c + 1) * P],
                                               ident[0:ROWS, 0:ROWS])
                last.then_inc(qt_bank, 1)

            def o_turn(q, r):
                t = q * G + r
                pe.wait_ge(o_set, t + 1)
                pe.wait_ge(ot_lo, t + 1)
                for c in range(DC):
                    last = nc.tensor.transpose(banks[3][:, c * ROWS:(c + 1) * ROWS], attn[:, r % 2, c * P:(c + 1) * P],
                                               ident[0:ROWS, 0:ROWS])
                last.then_inc(ot_bank, 1)

            def attention(q, r):
                t, j = q * G + r, r % 2
                pe.wait_ge(qt_lo, t + 2)
                pe.wait_ge(num_out, t + 1)
                W = 2 * (HD + 1)
                for p in range(DC):
                    last = products(banks[1 + p // 2][0:ROWS, p % 2 * W:(p % 2 + 1) * W],
                                    [(qTh[:, j, p, :], qTl[:, j, p, :], pairs_h[:, p, :], pairs_l[:, p, :])])
                last.then_inc(num_bank, 1)

            def xf_turn(q, r):
                t = q * G + r
                pe.wait_ge(xf_set, t + 1)
                pe.wait_ge(xft_out, t + 1)
                for c in range(DC):
                    last = nc.tensor.transpose(banks[5][:, c * ROWS:(c + 1) * ROWS], xf[:, r, c * P:(c + 1) * P],
                                               ident[0:ROWS, 0:ROWS])
                last.then_inc(xft_bank, 1)

            def mix(q, r):
                t, j = q * G + r, r % 2
                pe.wait_ge(ot_lo, t + 2)
                pe.wait_ge(x1_set, t + 1)
                products(banks[4][0:ROWS, :], [(oTh[:, j, c, :], oTl[:, j, c, :], WpTh[:, c, :], WpTl[:, c, :])
                                               for c in range(DC)], more=True)
                nc.tensor.matmul(banks[4][0:ROWS, :], ones_row[:, :], bp_h[:, :], start=False, stop=False)
                nc.tensor.matmul(banks[4][0:ROWS, :], ones_row[:, :], bp_l[:, :], start=False, stop=True).then_inc(mix_bank, 1)

            def route(q, r):
                t, j = q * G + r, r % 2
                pe.wait_ge(xft_out, t + 2)
                for c in range(DC):
                    nc.tensor.matmul(banks[6][0:ROWS, 16 * j:16 * j + 16], xfT[:, j, c, :], swT[:, c, :],
                                     start=c == 0, stop=False)
                last = nc.tensor.matmul(banks[6][0:ROWS, 16 * j:16 * j + 16], ones_row32[:, :], sb_bc[0:1, :],
                                        start=False, stop=True)
                last.then_inc(rt_bank, 1)

            def count_before(q, r):
                t, j = q * G + r, r % 2
                pe.wait_ge(oh_set, t + 1)
                pe.wait_ge(rank_set, t + 1)
                nc.tensor.matmul(banks[7][0:ROWS, 0:16], before[:, :], onehot[:, j, :], start=True, stop=True)
                nc.tensor.matmul(banks[7][0:ROWS, 16:32], ones_bf[:, :], onehot[:, j, :], start=True, stop=True).then_inc(pf_bank, 1)

            in_step(pe, MACROS * SUBS, G, [(count_before, 4), (q_turn, 0), (xf_turn, 3), (o_turn, 1), (route, 3), (attention, 0), (mix, 1)])
            phase_end(pe, 4)
            def expert_turn(q, r):
                if r % SLOTS:
                    return
                e, j = q * 2 + r // SLOTS, r // SLOTS
                pe.wait_ge(we_load[j], q * 16 + 16)
                for n in range(DC):
                    if n >= 2 or not isinstance(e, int) or e:
                        pe.wait_ge(we_lo, e * DC + (n - 1))
                    for c in range(DC):
                        last = nc.tensor.transpose(banks[n % 2][:, c * P:(c + 1) * P], we_st[:, j, c, n * P:(n + 1) * P], ident[:, :])
                    last.then_inc(we_bank, 1)

            def rows_turn(q, r):
                u, j = q * (2 * SLOTS) + r, r % 2
                pe.wait_ge(x5_set, u + 1)
                pe.wait_ge(f_lo, u + 1)
                for c in range(DC):
                    last = nc.tensor.transpose(banks[2 + j][:, c * P:(c + 1) * P], xf5[:, j, c * P:(c + 1) * P], ident[:, :])
                last.then_inc(f_bank, 1)

            def expert_rows(q, r):
                u, j, k = q * (2 * SLOTS) + r, r % 2, r // SLOTS
                if r % SLOTS == 0:
                    pe.wait_ge(we_lo, q * (2 * DC) + (k * DC + DC))
                pe.wait_ge(f_lo, u + 3)
                pe.wait_ge(y5_out, u + 1)
                products(banks[4 + j][:, :], [(fTh[:, j, c, :], fTl[:, j, c, :], WeTh[:, k, c, :], WeTl[:, k, c, :])
                                              for c in range(DC)]).then_inc(y5_bank, 1)

            in_step(pe, SL, 2 * SLOTS, [(expert_turn, 0), (rows_turn, 2), (expert_rows, 3)])


_INPUTS = ["x", "src", "dst"] + ["L0_" + n for n in (
    "gnn_W1", "gnn_att_src1", "gnn_att_dst1", "gnn_b1", "gnn_W2", "gnn_att_src2", "gnn_att_dst2", "gnn_b2",
    "mix_Wq", "mix_bq", "mix_Wk", "mix_bk", "mix_Wv", "mix_bv", "mix_Wp", "mix_bp",
    "ffn_switch_w", "ffn_switch_b", "ffn_expert_w", "ffn_expert_b")]


def kernel(**inputs):
    import numpy as np
    import concourse.bacc as bacc
    from concourse import mybir as ir
    from concourse.bass_utils import run_bass_kernel_spmd

    nc = bacc.Bacc("TRN2", target_bir_lowering=False, num_devices=1)
    arrays, args = {}, []
    for name in _INPUTS:
        a = np.ascontiguousarray(inputs[name])
        arrays[f"in_{name}"] = a
        args.append(nc.dram_tensor(f"in_{name}", a.shape, ir.dt.from_np(a.dtype), kind="ExternalInput").ap())
    n, d = arrays["in_x"].shape
    args.append(nc.dram_tensor("out", (n, d), ir.dt.float32, kind="ExternalOutput").ap())
    for name, shape, dt in scratch_tables(n, d, arrays["in_L0_ffn_switch_w"].shape[0]):
        args.append(nc.dram_tensor(name, shape, dt, kind="Internal").ap())
    gps_layer(nc, *args)
    r = run_bass_kernel_spmd(nc, [arrays], core_ids=[0])
    return r.results[0]["out"]
```

```python
from contextlib import ExitStack

import concourse.bass as bass
from concourse import mybir

F32 = mybir.dt.float32
F32R = mybir.dt.float32r
BF16 = mybir.dt.bfloat16
I32 = mybir.dt.int32
U32 = mybir.dt.uint32
ALU = mybir.AluOpType
ACT = mybir.ActivationFunctionType
AX = mybir.AxisListType

P = 128
ROWS = 125
SUBS = 4
FAR = 1 << 20
EPS = 1e-5


SEM_BASE = (190, 130)


class Chain:

    def __init__(self, eng, sem):
        self.eng, self.sem, self.done, self.base, self.k, self.marks = eng, sem, 0, None, 0, {}

    def enter(self, trip, per_trip):
        self.per, self.k = per_trip, 0
        self.base = self.eng.snap(trip * per_trip + self.done)

    def leave(self, trips):
        assert self.k == self.per, f"the loop links {self.k} instructions, not {self.per}"
        self.done, self.base, self.k = self.done + trips * self.per, None, 0

    def mark(self, name, ins):
        ins.then_inc(self.sem, 1)
        if self.base is None:
            self.done += 1
            self.marks[name] = self.done
        else:
            self.k += 1
            self.marks[name] = self.k

    def need(self, name, settle=None):
        self.eng.wait_ge(self.sem, self.marks[name] if self.base is None else self.base + self.marks[name])
        if settle is not None:
            self.eng.sem_inc(settle, 1)

    def link(self, ins, settle=None):
        ins.then_inc(self.sem, 1)
        if self.base is None:
            self.done += 1
            self.eng.wait_ge(self.sem, self.done)
        else:
            self.k += 1
            self.eng.wait_ge(self.sem, self.base + self.k)
            if settle is not None:
                self.eng.sem_inc(settle, 1)


def in_step(eng, count, unroll, stages, before_loop=None, chain=None, links=0):
    assert max(lag for _, lag in stages) <= unroll

    def step(q, r, known):
        for work, lag in stages:
            if known is None:
                dq, rr = divmod(r - lag, unroll)
                work(q + dq if dq else q, rr)
            elif 0 <= known - lag < count:
                work((known - lag) // unroll, (known - lag) % unroll)

    for n in range(unroll):
        step(0, n, n)
    trips = count // unroll - 1
    with eng.Fori(0, trips) as i:
        if chain is not None:
            chain.enter(i, links)
        for r in range(unroll):
            step(i + 1, r, None)
    if chain is not None:
        chain.leave(trips)
    for n in range(count, count + max(lag for _, lag in stages)):
        step(0, 0, n)


def scratch_tables(n, d, experts, edges):
    capacity = int(1.2 * n / experts)
    return [("y2_table", (n, d), F32), ("q_table", (n, d), F32), ("x1_table", (n, d + 4), F32),
            ("token_of_slot", (P * experts * -(-capacity // P), 1), I32),
            ("sorted_src", (edges, 1), I32), ("sorted_dst", (edges, 1), I32)]


def gps_layer(nc, x, src, dst, W1, att_src1, att_dst1, b1, W2, att_src2, att_dst2, b2,
              Wq, bq, Wk, bk, Wv, bv, Wp, bp, switch_w, switch_b, expert_w, expert_b, out,
              y2_table, q_table, x1_table, token_of_slot, sorted_src, sorted_dst):
    N, D = x.shape
    E = src.shape[0]
    HEADS, HID = att_src1.shape
    CLS = att_src2.shape[1]
    HD = D // HEADS
    DH = HEADS * HID
    EXPERTS = switch_w.shape[0]
    CAP = int(1.2 * N / EXPERTS)
    SLOTS = -(-CAP // P)
    DC = D // P
    ROW5 = next(n for n in (6, 5, 4) if 2 * SLOTS % n == 0)
    FC = DH // P
    MACRO = ROWS * SUBS
    MACROS = N // MACRO
    ET = E // ROWS
    META = 4
    assert N % MACRO == 0 and E % (2 * ROWS) == 0 and D == 512 and HEADS * CLS == D and HID == P
    assert EXPERTS == 16 and HD == 64 and CLS == HD

    with ExitStack() as ctx:
        shared = [[], []]
        now = [None]
        given = []

        def for_phase(n):
            for handle in given:
                nc.release_semaphore(handle)
            given.clear()
            now[0] = n

        def sem(name):
            if now[0] is None:
                return ctx.enter_context(nc.semaphore(name))
            numbers = shared[now[0] % 2]
            if len(given) < len(numbers):
                handle = nc.alloc_semaphore(name=name, num=numbers[len(given)])
            else:
                handle = nc.alloc_semaphore(name=name, num=SEM_BASE[now[0] % 2] + len(given))
                numbers.append(SEM_BASE[now[0] % 2] + len(given))
            given.append(handle)
            return handle

        cursor = [nc.sbuf_base + (-nc.sbuf_base) % 32]

        def place(name, shape, dt=F32):
            size = 2 if dt == BF16 else 4
            for n in shape[1:]:
                size *= n
            at = cursor[0] + (-cursor[0]) % 32
            cursor[0] = at + size
            return nc.alloc_sbuf_tensor_at(name, list(shape), dt, offset=at)

        ident = place("ident", [P, P])
        before = place("before", [ROWS, ROWS], BF16)
        ones_bf = place("ones_bf", [ROWS, ROWS], BF16)
        iota16 = place("iota16", [P, 16])
        rowid = place("rowid", [P, 2])
        last_row = place("last_row", [ROWS, 1])
        minus_half = place("minus_half", [ROWS, SUBS])
        ctx_acc = place("ctx_acc", [P, DC, P + 2])
        b1_col = place("b1_col", [P, FC])
        LOW = cursor[0]

        W1h = place("W1h", [P, DC, DH], F32R)
        W1l = place("W1l", [P, DC, DH], F32R)
        W2h = place("W2h", [P, FC, D], F32R)
        W2l = place("W2l", [P, FC, D], F32R)
        att1 = place("att1", [P, DC, 2 * 40])
        AFTER_GNN_WEIGHTS = cursor[0]

        WTh, WTl = {}, {}
        for n in "kvq":
            WTh[n] = place(f"W{n}Th", [P, DC, D], F32R)
            WTl[n] = place(f"W{n}Tl", [P, DC, D], F32R)
        bk_bc = place("bk_bc", [ROWS, D])
        bq_bc = place("bq_bc", [ROWS, D])
        xn = place("xn", [ROWS, SUBS, D])
        SCRATCH = cursor[0]
        xTh = place("xTh", [P, DC, MACRO], F32R)
        xTl = place("xTl", [P, DC, MACRO], F32R)
        kh = place("kh", [ROWS, 2, D], F32R)
        kl = place("kl", [ROWS, 2, D], F32R)
        vh = place("vh", [ROWS, 2, DC, P + 2], F32R)
        vl = place("vl", [ROWS, 2, DC, P + 2], F32R)
        kbuf = place("kbuf", [ROWS, 2, D])
        qbuf = place("qbuf", [ROWS, 2, D])
        y2o = place("y2o", [ROWS, 2, D])
        relu = place("relu", [P, 2, MACRO])
        h1h = place("h1h", [P, FC, MACRO], F32R)
        h1l = place("h1l", [P, FC, MACRO], F32R)
        stats = place("stats", [ROWS, SUBS, 6])
        mv = place("mv", [ROWS, SUBS, 2])
        veps = place("veps", [ROWS, SUBS])
        rstd = place("rstd", [ROWS, SUBS])
        newt = place("newt", [ROWS, 2, SUBS])
        kq_max = place("kq_max", [ROWS, 2, 2, HEADS])
        kq_rec = place("kq_rec", [ROWS, 2, 2, HEADS])
        cursor[0] = SCRATCH
        wk_st = place("wk_st", [P, DC, D])
        wv_st = place("wv_st", [P, DC, D])
        wq_st = place("wq_st", [P, DC, D])
        att_bc = place("att_bc", [P, 2, DH])
        att_tmp = place("att_tmp", [P, 2, DH])
        w1_st = place("w1_st", [P, DC, DH])
        w2_st = place("w2_st", [P, FC, D])

        cursor[0] = AFTER_GNN_WEIGHTS
        src_i = place("src_i", [ROWS, ET], I32)
        dst_i = place("dst_i", [ROWS, ET], I32)
        next_i = place("next_i", [ROWS, ET], I32)
        dst_f = place("dst_f", [ROWS, ET])
        next_f = place("next_f", [ROWS, ET])
        scat_i = place("scat_i", [ROWS, ET], I32)
        SL = EXPERTS * SLOTS
        dst_bc = place("dst_bc", [P, E + 2])
        at = cursor[0]
        raw_src = place("raw_src", [ROWS, ET], I32)
        raw_dst = place("raw_dst", [ROWS, ET], I32)
        raw_f = place("raw_f", [ROWS, ET])
        place_f = place("place_f", [ROWS, 2])
        place_st = place("place_st", [ROWS, 2], I32)
        src_st = place("src_st", [ROWS, 2], I32)
        dst_st = place("dst_st", [ROWS, 2], I32)
        earlier = place("earlier", [ROWS, 2 * E], BF16)
        sort_bits = place("sort_bits", [ROWS, E], BF16)
        cursor[0] = at
        xsT = place("xsT", [P, DC, E])
        xdT = place("xdT", [P, DC, E])
        cursor[0] = at
        ys_all = place("ys_all", [ROWS, ET, D])
        yd_all = place("yd_all", [ROWS, ET, D])
        EDGE_SCRATCH = cursor[0] = max(cursor[0], at + 2 * (DC * E * 4 + 32))
        run = place("run", [HEADS, E])
        same = place("same", [HEADS, E + 1])
        cursor[0] = max(cursor[0], EDGE_SCRATCH + 4 * 2 * D * 4 + 512)
        head_e = place("head_e", [HEADS, E])
        head_s = place("head_s", [HEADS, E])
        wall = place("wall", [HEADS, E + 1])
        cursor[0] = EDGE_SCRATCH
        dst_bi = place("dst_bi", [P, E], I32)
        cursor[0] = EDGE_SCRATCH
        gath = place("gath", [ROWS, 4, 2, D])
        e_idx = place("e_idx", [ROWS, 4, 2], I32)
        e_stats = place("e_stats", [ROWS, 2, 6])
        e_mv = place("e_mv", [ROWS, 2, 2, 2])
        e_veps = place("e_veps", [ROWS, 2, 2])
        e_rstd = place("e_rstd", [ROWS, 2, 2])
        e_newt = place("e_newt", [ROWS, 2, 2])
        cursor[0] = EDGE_SCRATCH
        xsh = place("xsh", [P, 2, DC, ROWS], F32R)
        xsl = place("xsl", [P, 2, DC, ROWS], F32R)
        msg = place("msg", [ROWS, 2, D])
        msg_self = place("msg_self", [ROWS, 2, D])
        msgh = place("msgh", [ROWS, DH], F32R)
        msgl = place("msgl", [ROWS, DH], F32R)
        same_dst = place("same_dst", [ROWS, ROWS + 1], F32R)
        goes_on = place("goes_on", [P, ROWS])
        aggT = place("aggT", [P, FC, ROWS])
        aggh = place("aggh", [P, FC, ROWS], F32R)
        aggl = place("aggl", [P, FC, ROWS], F32R)
        carry = place("carry", [P, FC])
        y_edge = place("y_edge", [ROWS, D])
        scat_st = place("scat_st", [ROWS, 2], I32)
        alpha_e = place("alpha_e", [ROWS, ET, HEADS])
        alpha_s = place("alpha_s", [ROWS, ET, HEADS])
        one_over = place("one_over", [ROWS, ET, HEADS])
        no_token = place("no_token", [P, SL], I32)
        cursor[0] = LOW
        att2_bc = place("att2_bc", [ROWS, 2, D])
        g2 = place("g2", [ROWS, 2, 2, D])
        prod2 = place("prod2", [ROWS, 3, D])
        dots = place("dots", [ROWS, 3, HEADS])
        logit2 = place("logit2", [ROWS, 2, 2 * HEADS])
        idx2 = place("idx2", [ROWS, 2, 2], I32)
        m2 = place("m2", [ROWS, 2, D])
        m2s = place("m2s", [ROWS, 2, D])
        m2h = place("m2h", [ROWS, 2, D], F32R)
        m2l = place("m2l", [ROWS, 2, D], F32R)
        same2 = place("same2", [ROWS, 2, ROWS], F32R)
        goes2 = place("goes2", [ROWS, 2, ROWS], F32R)
        z32 = place("z32", [ROWS, 2, D])
        zh = place("zh", [ROWS, 2, D], F32R)
        zl = place("zl", [ROWS, 2, D], F32R)
        scat2 = place("scat2", [ROWS, 2], I32)

        G = 4
        cursor[0] = LOW
        wp_st = place("wp_st", [P, DC, D])
        WpTh = place("WpTh", [P, DC, D], F32R)
        WpTl = place("WpTl", [P, DC, D], F32R)
        sw_st = place("sw_st", [EXPERTS, D])
        swT = place("swT", [P, DC, EXPERTS])
        sb_bc = place("sb_bc", [ROWS, EXPERTS])
        bv_bc = place("bv_bc", [P, D])
        bp_bc = place("bp_bc", [ROWS, D])
        b2_bc = place("b2_bc", [ROWS, D])
        pairs = place("pairs", [P, DC, 2, HD + 1])
        pairs_h = place("pairs_h", [P, DC, 2 * (HD + 1)], F32R)
        pairs_l = place("pairs_l", [P, DC, 2 * (HD + 1)], F32R)
        ones_row = place("ones_row", [1, ROWS], F32R)
        ones_row32 = place("ones_row32", [1, ROWS])
        bp_h = place("bp_h", [1, D], F32R)
        bp_l = place("bp_l", [1, D], F32R)
        iota_f = place("iota_f", [P, 16], I32)
        row_0 = place("row_0", [ROWS, 1], I32)
        steps_i = place("steps_i", [ROWS, max(SLOTS - 1, 1)], I32)
        used = place("used", [ROWS, EXPERTS])
        steps128 = place("steps128", [ROWS, max(SLOTS - 1, 1)])
        x_in = place("x_in", [ROWS, G, D])
        y_in = place("y_in", [ROWS, G, D])
        q_in = place("q_in", [ROWS, G, D])
        qTh = place("qTh", [P, 2, DC, ROWS], F32R)
        qTl = place("qTl", [P, 2, DC, ROWS], F32R)
        den = place("den", [ROWS, 2, HEADS])
        attn = place("attn", [ROWS, 2, D])
        oTh = place("oTh", [P, 2, DC, ROWS], F32R)
        oTl = place("oTl", [P, 2, DC, ROWS], F32R)
        exp_y = place("exp_y", [ROWS, D])
        y_stat = place("y_stat", [ROWS, 2, 4])
        x1row = place("x1row", [ROWS, G, D + META])
        stats4 = place("stats4", [ROWS, 6])
        mv4 = place("mv4", [ROWS, 2, 2])
        veps4 = place("veps4", [ROWS, 2, 1])
        r4 = place("r4", [ROWS, 2, 1])
        newt4 = place("newt4", [ROWS, 1])
        xf = place("xf", [ROWS, G, D])
        xfT = place("xfT", [P, 2, DC, ROWS])
        lstat = place("lstat", [ROWS, 2, 4])
        ex16 = place("ex16", [ROWS, 2, EXPERTS])
        top8 = place("top8", [ROWS, 8])
        arg8 = place("arg8", [ROWS, 8], U32)
        argf = place("argf", [ROWS, 2, 1])
        onehot = place("onehot", [ROWS, 2, EXPERTS], BF16)
        rank = place("rank", [ROWS, EXPERTS])
        small = place("small", [ROWS, 8])
        slot_i = place("slot_i", [ROWS, 2], I32)
        row_i = place("row_i", [ROWS, 2], I32)
        steps_tmp = place("steps_tmp", [ROWS, max(SLOTS - 1, 1)])
        token_i = place("token_i", [ROWS, 2], I32)
        orow = place("orow", [ROWS, 2, D])
        drop_line = place("drop_line", [ROWS, 2, 2])

        SL = EXPERTS * SLOTS
        cursor[0] = LOW
        tok_i = place("tok_i", [P, SL], I32)
        tok_f = place("tok_f", [P, SL])
        from_i = place("from_i", [P, SL], I32)
        we_st = place("we_st", [P, 2, DC, D])
        WeTh = place("WeTh", [P, 2, DC, D], F32R)
        WeTl = place("WeTl", [P, 2, DC, D], F32R)
        eb_bc = place("eb_bc", [P, 2, D])
        row5 = place("row5", [P, ROW5, D + META])
        xf5 = place("xf5", [P, 2, D])
        fTh = place("fTh", [P, 2, DC, P], F32R)
        fTl = place("fTl", [P, 2, DC, P], F32R)
        yb5 = place("yb5", [P, 2, D])
        res5 = place("res5", [P, 2, D])
        from_st = place("from_st", [P, ROW5], I32)
        to_st = place("to_st", [P, 2], I32)

        banks = [nc.alloc_psum_tensor(f"bank{i}", [P, 512], F32) for i in range(8)]

        def groups(ap, n):
            return ap.rearrange("p (h c) -> p h c", h=n)

        def spread(ap, n):
            return ap.unsqueeze(2).to_broadcast([ap.shape[0], ap.shape[1], n])

        def products(out_, terms, first=True, more=False):
            last = None
            for n, (ah, al, bh, bl) in enumerate(terms):
                nc.tensor.matmul(out_, ah, bh, start=first and n == 0, stop=False)
                nc.tensor.matmul(out_, ah, bl, start=False, stop=False)
                last = nc.tensor.matmul(out_, al, bh, start=False, stop=not more and n == len(terms) - 1)
            return last


        const_done = sem("const_done")
        pool_chain = sem("pool_chain")
        dve_chain = sem("dve_chain")
        act_chain = sem("act_chain")
        pool_settled = sem("pool_settled")
        dve_settled = sem("dve_settled")
        sp_settled = sem("sp_settled")
        phase_done = sem("phase_done")
        sort_store = [sem(f"sort_store{j}") for j in range(2)]
        e_gath = [sem(f"e_gath{j}") for j in range(4)]
        ye_store = sem("ye_store")
        g2_load = [sem(f"g2_load{j}") for j in range(2)]
        z_store = [sem(f"z_store{j}") for j in range(2)]
        tok_store = [sem(f"tok_store{j}") for j in range(2)]
        orow_store = [sem(f"orow_store{j}") for j in range(2)]
        row5_load = [sem(f"row5_load{j}") for j in range(ROW5)]
        res_store = [sem(f"res_store{j}") for j in range(2)]
        for_phase(1)
        wload = {n: sem(f"wload_{n}") for n in ("k", "v", "q", "W1", "W2", "att0", "att1")}
        bias_load = [sem(f"bias_load{n}") for n in range(3)]
        ones_done = sem("ones_done")
        wt_bank = sem("wt_bank")
        wt_hi = sem("wt_hi")
        wt_lo = sem("wt_lo")
        w_hi = sem("w_hi")
        w_lo = sem("w_lo")
        w2_lo = sem("w2_lo")
        att_sum = sem("att_sum")
        x_load = sem("x_load")
        var_ready = sem("var_ready")
        rstd0 = sem("rstd0")
        xn_ready = sem("xn_ready")
        xt_bank = sem("xt_bank")
        xt_hi = sem("xt_hi")
        xt_lo = sem("xt_lo")
        kvq_bank = sem("kvq_bank")
        kvq_free = sem("kvq_free")
        smax = sem("smax")
        ssub = sem("ssub")
        sexp = sem("sexp")
        srec = sem("srec")
        snorm_k = sem("snorm_k")
        snorm_q = sem("snorm_q")
        v_hi = sem("v_hi")
        k_hi = sem("k_hi")
        k_lo = sem("k_lo")
        ctx_bank = sem("ctx_bank")
        ctx_free = sem("ctx_free")
        h_bank = sem("h_bank")
        h_hi = sem("h_hi")
        h_lo = sem("h_lo")
        y_bank = sem("y_bank")
        y_free = sem("y_free")
        q_store = [sem(f"q_store{j}") for j in range(2)]
        y_store = [sem(f"y_store{j}") for j in range(2)]
        for_phase(2)
        edge_load = {n: sem(f"edge_load_{n}") for n in ("src", "dst", "next", "all")}
        next_clear = sem("next_clear")
        raw_load = sem("raw_load")
        earlier_set = sem("earlier_set")
        sort_staged = sem("sort_staged")
        edges_sorted = sem("edges_sorted")
        bc_set = sem("bc_set")
        edge_f = sem("edge_f")
        e_staged = sem("e_staged")
        e_var = sem("e_var")
        e_rstd0 = sem("e_rstd0")
        e_xn = sem("e_xn")
        e_bank = sem("e_bank")
        e_src_out = sem("e_src_out")
        e_dst_out = sem("e_dst_out")
        lg_bank = sem("lg_bank")
        lg_out = sem("lg_out")
        st_hi = sem("st_hi")
        st_lo = sem("st_lo")
        hm_bank = sem("hm_bank")
        m_self = sem("m_self")
        m_sum = sem("m_sum")
        m_hi = sem("m_hi")
        m_lo = sem("m_lo")
        mask_set = sem("mask_set")
        ag_bank = sem("ag_bank")
        ag_out = sem("ag_out")
        ag_hi = sem("ag_hi")
        ag_lo = sem("ag_lo")
        ye_bank = sem("ye_bank")
        ye_out = sem("ye_out")
        pool_scat = sem("pool_scat")
        tok_init = sem("tok_init")
        no_tok = sem("no_tok")
        sc_sub_1 = sem("sc_sub_1")
        sc_exp_1 = sem("sc_exp_1")
        sc_done_1 = sem("sc_done_1")
        al_bank_1 = sem("al_bank_1")
        al_out_1 = sem("al_out_1")
        for_phase(3)
        att2_load = sem("att2_load")
        g2_staged = sem("g2_staged")
        g2_copied = sem("g2_copied")
        p2_pool = sem("p2_pool")
        logit2_set = sem("logit2_set")
        lt_bank = sem("lt_bank")
        lt_out = sem("lt_out")
        m2s_set = sem("m2s_set")
        m2_set = sem("m2_set")
        m2_times = sem("m2_times")
        m2_hi = sem("m2_hi")
        m2_lo = sem("m2_lo")
        z_bank = sem("z_bank")
        mask2_set = sem("mask2_set")
        z_hi = sem("z_hi")
        zh_set = sem("zh_set")
        z_lo = sem("z_lo")
        z_staged = sem("z_staged")
        sc_sub_2 = sem("sc_sub_2")
        sc_exp_2 = sem("sc_exp_2")
        sc_done_2 = sem("sc_done_2")
        al_bank_2 = sem("al_bank_2")
        al_out_2 = sem("al_out_2")
        sc_sub = (sc_sub_1, sc_sub_2)
        sc_exp = (sc_exp_1, sc_exp_2)
        sc_done = (sc_done_1, sc_done_2)
        al_bank = (al_bank_1, al_bank_2)
        al_out = (al_out_1, al_out_2)
        for_phase(4)
        p4_load = sem("p4_load")
        p4_bias = sem("p4_bias")
        p4_sw = sem("p4_sw")
        p4_sb = sem("p4_sb")
        p4_bv = sem("p4_bv")
        wp_bank = sem("wp_bank")
        wp_hi = sem("wp_hi")
        wp_lo = sem("wp_lo")
        sw_bank = sem("sw_bank")
        sw_out = sem("sw_out")
        ctx_ready = sem("ctx_ready")
        b_added = sem("b_added")
        qt_bank = sem("qt_bank")
        qt_hi = sem("qt_hi")
        qt_lo = sem("qt_lo")
        num_bank = sem("num_bank")
        num_out = sem("num_out")
        o_set = sem("o_set")
        ot_bank = sem("ot_bank")
        ot_hi = sem("ot_hi")
        ot_lo = sem("ot_lo")
        mix_bank = sem("mix_bank")
        x1_set = sem("x1_set")
        y_max = sem("y_max")
        lse_set = sem("lse_set")
        v4_set = sem("v4_set")
        r4_set = sem("r4_set")
        ln4_set = sem("ln4_set")
        xf_set = sem("xf_set")
        xft_bank = sem("xft_bank")
        xft_out = sem("xft_out")
        rt_bank = sem("rt_bank")
        rt_max = sem("rt_max")
        rt_exp = sem("rt_exp")
        oh_set = sem("oh_set")
        pf_bank = sem("pf_bank")
        row_set = sem("row_set")
        row_free = sem("row_free")
        orow_set = sem("orow_set")
        const4 = sem("const4")
        rank_set = sem("rank_set")
        x4_load = [sem(f"x4_load{j}") for j in range(G)]
        y4_load = [sem(f"y4_load{j}") for j in range(G)]
        q4_load = [sem(f"q4_load{j}") for j in range(G)]
        x1_store = [sem(f"x1_store{j}") for j in range(G)]
        for_phase(5)
        tok_load = sem("tok_load")
        tok_set = sem("tok_set")
        we_bank = sem("we_bank")
        we_hi = sem("we_hi")
        we_lo = sem("we_lo")
        x5_set = sem("x5_set")
        f_bank = sem("f_bank")
        f_hi = sem("f_hi")
        f_lo = sem("f_lo")
        y5_bank = sem("y5_bank")
        y5_out = sem("y5_out")
        res_set = sem("res_set")
        idx5_set = sem("idx5_set")
        to_set = sem("to_set")
        we_load = [sem(f"we_load{j}") for j in range(2)]
        eb_load = [sem(f"eb_load{j}") for j in range(2)]
        for_phase(None)

        CONSTS = 7
        LINKS4 = 16
        DVE_LINKS = 2 + 4 + 2 * SUBS

        def refine(dve, chain, r, v, tmp):
            chain.link(nc.vector.tensor_tensor(tmp[:, 0, :], r, r, ALU.mult))
            chain.link(nc.vector.tensor_tensor(tmp[:, 0, :], tmp[:, 0, :], v, ALU.mult))
            chain.link(nc.vector.tensor_scalar(tmp[:, 0, :], tmp[:, 0, :], -0.5, 1.5, ALU.mult, ALU.add))
            chain.link(nc.vector.tensor_tensor(r, r, tmp[:, 0, :], ALU.mult))

        def add_context(dve, chain, sub0, s):
            dve.wait_ge(ctx_bank, sub0 + (s + 1))
            dve.wait_ge(ctx_free, sub0 * 2 + (2 * s + 2))
            for b in range(2):
                pairs = slice(b * DC // 2, (b + 1) * DC // 2)
                nc.vector.tensor_tensor(ctx_acc[:, pairs, :], groups(banks[6 + b][:, 0:(P + 2) * DC // 2], DC // 2),
                                        ctx_acc[:, pairs, :], ALU.add).then_inc(ctx_free, 1)

        def phase_end(eng, n):
            eng.drain().then_inc(phase_done, 1)
            eng.wait_ge(phase_done, 5 * n)
            if eng is nc.gpsimd:
                eng.sem_clear(range(shared[n % 2][0], shared[n % 2][-1] + 1))

        def find_walls(dve, chain):
            chain.link(nc.vector.tensor_tensor(same[:, :], dst_bc[0:HEADS, 1:E + 2], dst_bc[0:HEADS, 0:E + 1], ALU.is_equal))
            chain.link(nc.vector.tensor_scalar(wall[:, :], same[:, :], 1e30, -1e30, ALU.mult, ALU.add))

        def edge_softmax(dve, chain, layer):
            for t in (head_e, head_s):
                chain.link(nc.vector.scalar_tensor_tensor(out=t[:, :], in0=t[:, :], scalar=0.2, in1=t[:, :],
                                                          op0=ALU.mult, op1=ALU.max))
            chain.link(nc.vector.tensor_tensor_scan(run[:, :], wall[:, 0:E], head_e[:, :], -1e30, ALU.add, ALU.max))
            chain.link(nc.vector.tensor_tensor_scan(run[:, ::-1], wall[:, :0:-1], run[:, ::-1], -1e30, ALU.add, ALU.max))
            chain.link(nc.vector.tensor_tensor(run[:, :], run[:, :], head_s[:, :], ALU.max))
            for t in (head_e, head_s):
                last = nc.vector.tensor_tensor(t[:, :], t[:, :], run[:, :], ALU.subtract)
                last.then_inc(sc_sub[layer], 1)
            dve.wait_ge(sc_exp[layer], 2)
            chain.link(nc.vector.tensor_tensor_scan(run[:, :], same[:, 0:E], head_e[:, :], 0.0, ALU.mult, ALU.add))
            chain.link(nc.vector.tensor_scalar(wall[:, :], same[:, :], -1.0, 1.0, ALU.mult, ALU.add))
            chain.link(nc.vector.tensor_tensor(run[:, :], run[:, :], wall[:, 1:E + 1], ALU.mult))
            chain.link(nc.vector.tensor_tensor_scan(run[:, ::-1], same[:, :0:-1], run[:, ::-1], 0.0, ALU.mult, ALU.add))
            nc.vector.scalar_tensor_tensor(out=run[:, :], in0=run[:, :], scalar=1e-16, in1=head_s[:, :],
                                           op0=ALU.add, op1=ALU.add).then_inc(sc_done[layer], 1)
            nc.vector.tensor_tensor(head_s[:, :], head_s[:, :], wall[:, 0:E], ALU.mult).then_inc(sc_done[layer], 1)
            dve.wait_ge(sc_done[layer], 2)
            dve.wait_ge(al_bank[layer], 3)
            chain.link(nc.vector.reciprocal(one_over[:, :, :], groups(banks[1][0:ROWS, 0:ET * HEADS], ET)))
            nc.vector.tensor_tensor(alpha_e[:, :, :], groups(banks[0][0:ROWS, 0:ET * HEADS], ET), one_over[:, :, :], ALU.mult)
            nc.vector.tensor_tensor(alpha_s[:, :, :], groups(banks[2][0:ROWS, 0:ET * HEADS], ET), one_over[:, :, :],
                                    ALU.mult).then_inc(al_out[layer], 1)

        def exp_logits(act, layer):
            for n, t in enumerate((head_e, head_s)):
                act.wait_ge(sc_sub[layer], n + 1)
                nc.scalar.activation(t[:, :], t[:, :], ACT.Exp).then_inc(sc_exp[layer], 1)

        def weights_by_edge(pe, layer):
            for n, (t, done, count) in enumerate(((head_e, sc_exp, 1), (run, sc_done, 1), (head_s, sc_done, 2))):
                pe.wait_ge(done[layer], count)
                for k in range(ET):
                    last = nc.tensor.transpose(banks[n][0:ROWS, k * HEADS:(k + 1) * HEADS],
                                               t[:, k * ROWS:(k + 1) * ROWS], ident[0:HEADS, 0:HEADS])
                last.then_inc(al_bank[layer], 1)

        block = ctx.enter_context(nc.Block())

        @block.sync
        def _(sp):
            for n, w, st in (("k", Wk, wk_st), ("v", Wv, wv_st), ("q", Wq, wq_st)):
                sp.dma_start(st[:, :, :], w.rearrange("(c p) i -> p c i", p=P)).then_inc(wload[n], 16)
            sp.dma_start(xn[:, :, :], x[0:MACRO, :].rearrange("(s p) d -> p s d", p=ROWS)).then_inc(x_load, 16)
            sp.dma_start(w1_st[:, :, :], W1.rearrange("(c p) i -> p c i", p=P)).then_inc(wload["W1"], 16)
            sp.dma_start(w2_st[:, :, :], W2.rearrange("(c p) i -> p c i", p=P)).then_inc(wload["W2"], 16)
            for j in range(2):
                sp.sem_inc(q_store[j], 16)

            def store_q(m):
                for s in range(SUBS):
                    sp.wait_ge(snorm_q, m * SUBS + (s + 1))
                    sp.sem_inc(sp_settled, 1)
                    sp.dma_start(q_table[bass.ds((m * SUBS + s) * ROWS, ROWS), :],
                                 qbuf[:, s % 2, :]).then_inc(q_store[s % 2], 16)

            with sp.Fori(0, MACROS - 1) as m:
                store_q(m)
                sp.wait_ge(xt_bank, m * SUBS + SUBS)
                sp.sem_inc(sp_settled, 1)
                sp.dma_start(xn[:, :, :], x[bass.ds(m * MACRO + MACRO, MACRO), :]
                             .rearrange("(s p) d -> p s d", p=ROWS)).then_inc(x_load, 16)
            store_q(MACROS - 1)
            for j in range(2):
                sp.wait_ge(q_store[j], 16 * (MACROS * SUBS // 2 + 1))
            phase_end(sp, 1)
            slow = dict(allow_slow_non_contiguous=True)
            for d, s_ in ((raw_src, src), (raw_dst, dst)):
                sp.dma_start(d[:, :], s_.rearrange("(t p) -> p t", p=ROWS), **slow).then_inc(raw_load, 16)
            sp.dma_start(dst_bi[:, :], dst.partition_broadcast(P)).then_inc(raw_load, 16)
            sp.wait_ge(no_tok, 1)
            sp.dma_start(token_of_slot.rearrange("(p s) o -> p (s o)", p=P), no_token[:, :]).then_inc(tok_init, 16)
            sp.wait_ge(tok_init, 16)
            sp.wait_ge(edges_sorted, 1)
            by_src, by_dst = sorted_src.rearrange("e o -> (e o)"), sorted_dst.rearrange("e o -> (e o)")
            sp.dma_start(src_i[:, :], by_src.rearrange("(t p) -> p t", p=ROWS), **slow).then_inc(edge_load["src"], 16)
            sp.dma_start(dst_i[:, :], by_dst.rearrange("(t p) -> p t", p=ROWS), **slow).then_inc(edge_load["dst"], 16)
            sp.dma_start(dst_bi[:, :], by_dst.partition_broadcast(P)).then_inc(edge_load["all"], 16)
            sp.wait_ge(next_clear, 1)
            sp.dma_start(next_i[:, 0:ET - 1], by_dst[1:1 + (ET - 1) * ROWS].rearrange("(t p) -> p t", p=ROWS),
                         **slow).then_inc(edge_load["next"], 16)
            sp.dma_start(next_i[0:ROWS - 1, ET - 1:ET], by_dst[E - ROWS + 1:E].rearrange("(p t) -> p t", t=1),
                         **slow).then_inc(edge_load["next"], 16)
            phase_end(sp, 2)
            for r, a in enumerate((att_src2, att_dst2)):
                sp.dma_start(att2_bc[:, r, :], a.rearrange("h c -> (h c)").partition_broadcast(ROWS)).then_inc(att2_load, 16)
            phase_end(sp, 3)
            sp.dma_start(wp_st[:, :, :], Wp.rearrange("(c p) i -> p c i", p=P)).then_inc(p4_load, 16)
            sp.dma_start(bv_bc[:, :], bv.partition_broadcast(P)).then_inc(p4_bv, 16)
            sp.dma_start(sw_st[:, :], switch_w).then_inc(p4_sw, 16)
            for d, b in ((bp_bc, bp), (b2_bc, b2)):
                sp.dma_start(d[:, :], b.partition_broadcast(ROWS)).then_inc(p4_bias, 16)
            sp.dma_start(sb_bc[:, :], switch_b.partition_broadcast(ROWS)).then_inc(p4_sb, 16)
            for j in range(G):
                sp.sem_inc(x1_store[j], 16)

            def load_nodes(q, r):
                t = q * G + r
                if not isinstance(t, int):
                    sp.wait_ge(o_set, t - (G - 1))
                    sp.sem_inc(sp_settled, 1)
                    sp.wait_ge(x1_set, t - (G - 2))
                    sp.sem_inc(sp_settled, 1)
                rows = bass.ds(t * ROWS, ROWS)
                for d, s_, done in ((q_in, q_table, q4_load), (x_in, x, x4_load), (y_in, y2_table, y4_load)):
                    sp.dma_start(d[:, r, :], s_[rows, :]).then_inc(done[r], 16)

            def store_x1(q, r):
                sp.wait_ge(oh_set, q * G + (r + 1))
                sp.sem_inc(sp_settled, 1)
                sp.dma_start(x1_table[bass.ds((q * G + r) * ROWS, ROWS), :], x1row[:, r, :]).then_inc(x1_store[r], 16)

            in_step(sp, MACROS * SUBS, G, [(load_nodes, 0), (store_x1, 4)])
            for j in range(G):
                sp.wait_ge(x1_store[j], 16 * (MACROS * SUBS // G + 1))
            phase_end(sp, 4)
            sp.dma_start(tok_i[:, :], token_of_slot.rearrange("(p s) o -> p (s o)", p=P)).then_inc(tok_load, 16)

            def load_expert(q, r):
                if r % SLOTS:
                    return
                e, j = q * 2 + r // SLOTS, r // SLOTS
                if not isinstance(e, int):
                    sp.wait_ge(we_bank, e * DC - DC)
                    sp.sem_inc(sp_settled, 1)
                    sp.wait_ge(y5_out, e * SLOTS - SLOTS + 2)
                    sp.sem_inc(sp_settled, 1)
                sp.dma_start(we_st[:, j, :, :], expert_w[bass.ds(e, 1), :, :].rearrange("o (c p) i -> p (o c) i", p=P))\
                  .then_inc(we_load[j], 16)
                sp.dma_start(eb_bc[:, j, :], expert_b[bass.ds(e, 1), :].rearrange("o f -> (o f)").partition_broadcast(P))\
                  .then_inc(eb_load[j], 16)

            in_step(sp, SL, 2 * SLOTS, [(load_expert, 0)])

        @block.gpsimd
        def _(pool):
            chain = Chain(pool, pool_chain)
            settle = lambda: pool.sem_inc(pool_settled, 1)
            chain.link(nc.gpsimd.memset(ident[:, :], 0.0))
            nc.gpsimd.affine_select(out=ident[:, :], in_=ident[:, :], compare_op=ALU.not_equal, fill=1.0, base=0,
                                    pattern=[[-1, P]], channel_multiplier=1).then_inc(const_done, 1)
            nc.gpsimd.memset(ones_bf[:, :], 1.0).then_inc(const_done, 1)
            chain.link(nc.gpsimd.memset(before[:, :], 1.0))
            nc.gpsimd.affine_select(out=before[:, :], in_=before[:, :], compare_op=ALU.is_gt, fill=0.0, base=0,
                                    pattern=[[1, ROWS]], channel_multiplier=-1).then_inc(const_done, 1)
            nc.gpsimd.memset(minus_half[:, :], -0.5).then_inc(const_done, 1)
            chain.link(nc.gpsimd.memset(last_row[:, :], 0.0))
            nc.gpsimd.affine_select(out=last_row[:, :], in_=last_row[:, :], compare_op=ALU.not_equal, fill=1.0,
                                    base=1 - ROWS, pattern=[[0, 1]], channel_multiplier=1).then_inc(const_done, 1)
            nc.gpsimd.memset(ctx_acc[:, :, :], 0.0).then_inc(const_done, 1)
            nc.gpsimd.memset(att1[:, :, :], 0.0).then_inc(const_done, 1)
            def start_rstds(m):
                pool.wait_ge(var_ready, m + 1)
                settle()
                nc.gpsimd.tensor_tensor(rstd[:, :], veps[:, :], minus_half[:, :], ALU.pow).then_inc(rstd0, 1)

            pool.wait_ge(const_done, CONSTS)
            start_rstds(0)
            pool.wait_ge(w_hi, 2)
            nc.gpsimd.tensor_tensor(W2l[:, :, :], w2_st[:, :, :], W2h[:, :, :].bitcast(F32),
                                    ALU.subtract).then_inc(w2_lo, 1)
            def softmax_steps(sub0):
                for s in range(SUBS):
                    j = s % 2
                    for n, buf in ((0, kbuf), (1, qbuf)):
                        pool.wait_ge(smax, sub0 * 2 + (2 * s + n + 1))
                        nc.gpsimd.tensor_tensor(groups(buf[:, j, :], HEADS), groups(buf[:, j, :], HEADS),
                                                spread(kq_max[:, j, n, :], HD), ALU.subtract).then_inc(ssub, 1)
                    for n, buf, done in ((0, kbuf, snorm_k), (1, qbuf, snorm_q)):
                        pool.wait_ge(srec, sub0 * 2 + (2 * s + n + 1))
                        nc.gpsimd.tensor_tensor(groups(buf[:, j, :], HEADS), groups(buf[:, j, :], HEADS),
                                                spread(kq_rec[:, j, n, :], HD), ALU.mult).then_inc(done, 1)
                    for f in (2 * s, 2 * s + 1):
                        pool.wait_ge(h_hi, sub0 * 2 + (f + 1))
                        nc.gpsimd.tensor_tensor(h1l[:, f, :], relu[:, f % 2, :], h1h[:, f, :].bitcast(F32),
                                                ALU.subtract).then_inc(h_lo, 1)

            with pool.Fori(0, MACROS - 1) as m:
                sub0 = pool.snap(m * SUBS)
                softmax_steps(sub0)
                start_rstds(m + 1)
            softmax_steps((MACROS - 1) * SUBS)

            phase_end(pool, 1)
            nc.gpsimd.memset(no_token[:, :], FAR).then_inc(no_tok, 1)
            nc.gpsimd.memset(next_i[:, :], -1).then_inc(next_clear, 1)
            chain.link(nc.gpsimd.memset(earlier[:, E:E + ROWS], 1.0))
            nc.gpsimd.affine_select(out=earlier[:, E:E + ROWS], in_=earlier[:, E:E + ROWS], compare_op=ALU.is_gt, fill=0.0,
                                    base=0, pattern=[[-1, ROWS]], channel_multiplier=1).then_inc(earlier_set, 1)
            with pool.Fori(0, ET // 2) as i:
                pair = pool.snap(i * 2)
                for j in range(2):
                    pool.wait_ge(sort_staged, pair + (j + 1))
                    settle()
                    for d, s_ in ((sorted_src, src_st), (sorted_dst, dst_st)):
                        pool.indirect_dma_start(d, bass.IndirectOffsetOnAxis(place_st[:, j:j + 1].bitcast(U32), 0), s_[:, j:j + 1],
                                                None, bounds_check=E - 1, oob_is_err=False).then_inc(sort_store[j], 16)
            for j in range(2):
                pool.wait_ge(sort_store[j], 16 * ET)
            pool.sem_inc(edges_sorted, 1)
            pool.wait_ge(edge_load["src"], 16)
            pool.wait_ge(edge_load["dst"], 16)
            pool.wait_ge(bc_set, 1)

            def gather_edges(q, r):
                t = q * 4 + r
                pool.wait_ge(e_bank, t * 2 + 2)
                settle()
                for n, idx in enumerate((src_i, dst_i)):
                    nc.gpsimd.tensor_copy(e_idx[:, r, n:n + 1], idx[:, bass.ds(t, 1)]).then_inc(e_staged, 1)
                pool.wait_ge(e_staged, t * 2 + 2)
                settle()
                for n in range(2):
                    pool.indirect_dma_start(gath[:, r, n, :], None, x, bass.IndirectOffsetOnAxis(
                        e_idx[:, r, n:n + 1].bitcast(U32), 0)).then_inc(e_gath[r], 16)

            def edge_rstd(q, r):
                pool.wait_ge(e_var, q * 4 + (r + 1))
                settle()
                nc.gpsimd.tensor_tensor(e_rstd[:, r % 2, :], e_veps[:, r % 2, :], minus_half[:, 0:2], ALU.pow).then_inc(e_rstd0, 1)

            in_step(pool, ET, 4, [(gather_edges, 0), (edge_rstd, 2)])

            def stage_low(t):
                for r, xT in enumerate((xsT, xdT)):
                    pool.wait_ge(st_hi, t * 2 + (r + 1))
                    nc.gpsimd.tensor_tensor(xsl[:, r, :, :], xT[:, :, bass.ds(t * ROWS, ROWS)],
                                            xsh[:, r, :, :].bitcast(F32), ALU.subtract).then_inc(st_lo, 1)

            def message_low(t):
                for h in range(2):
                    pool.wait_ge(m_self, t * 2 + (h + 1))
                    settle()
                    nc.gpsimd.tensor_tensor(msg[:, h, :], msg[:, h, :], msg_self[:, h, :], ALU.add).then_inc(m_sum, 1)
                    pool.wait_ge(m_hi, t * 2 + (h + 1))
                    nc.gpsimd.tensor_tensor(msgl[:, h * D:(h + 1) * D], msg[:, h, :],
                                            msgh[:, h * D:(h + 1) * D].bitcast(F32), ALU.subtract).then_inc(m_lo, 1)

            def aggregate_low(t):
                pool.wait_ge(ag_hi, t + 1)
                nc.gpsimd.tensor_tensor(aggl[:, :, :], aggT[:, :, :], aggh[:, :, :].bitcast(F32), ALU.subtract).then_inc(ag_lo, 1)

            def scatter_rows(t):
                pool.wait_ge(ye_out, t + 2)
                settle()
                nc.gpsimd.tensor_copy(scat_st[:, 0:1], scat_i[:, bass.ds(t, 1)]).then_inc(pool_scat, 1)
                pool.wait_ge(pool_scat, t + 1)
                settle()
                pool.indirect_dma_start(y2_table, bass.IndirectOffsetOnAxis(scat_st[:, 0:1].bitcast(U32), 0), y_edge[:, :],
                                        None, bounds_check=N - 1, oob_is_err=False).then_inc(ye_store, 16)

            stage_low(0)
            message_low(0)
            stage_low(1)
            with pool.Fori(0, ET - 2) as t:
                aggregate_low(t)
                message_low(t + 1)
                stage_low(t + 2)
                scatter_rows(t)
            aggregate_low(ET - 2)
            message_low(ET - 1)
            scatter_rows(ET - 2)
            aggregate_low(ET - 1)
            scatter_rows(ET - 1)
            pool.wait_ge(ye_store, 16 * ET)
            phase_end(pool, 2)
            pool.wait_ge(att2_load, 32)
            with pool.Fori(0, ET // 2) as i:
                pair = pool.snap(i * 2)
                for j in range(2):
                    pool.wait_ge(g2_copied, pair + (j + 1))
                    pool.wait_ge(logit2_set, pair + (j + 1))
                    settle()
                    for r, idx in enumerate((src_i, dst_i)):
                        nc.gpsimd.tensor_copy(idx2[:, j, r:r + 1], idx[:, bass.ds(i * 2 + j, 1)]).then_inc(g2_staged, 1)
                    pool.wait_ge(g2_staged, pair * 2 + (2 * j + 2))
                    settle()
                    for r in range(2):
                        pool.indirect_dma_start(g2[:, j, r, :], None, y2_table, bass.IndirectOffsetOnAxis(
                            idx2[:, j, r:r + 1].bitcast(U32), 0)).then_inc(g2_load[j], 16)
                for j in range(2):
                    pool.wait_ge(g2_load[j], i * 32 + 32)
                    pool.wait_ge(logit2_set, pair + (j + 2))
                    settle()
                    nc.gpsimd.tensor_tensor(prod2[:, 2, :], g2[:, j, 1, :], att2_bc[:, 1, :], ALU.mult).then_inc(p2_pool, 1)
            pool.wait_ge(al_out[1], 1)

            def own_message(q, r):
                t, j = q * 4 + r, r % 2
                pool.wait_ge(m2_set, t + 1)
                settle()
                nc.gpsimd.tensor_tensor(groups(m2s[:, j, :], HEADS), groups(yd_all[:, bass.ds(t, 1), :]
                                        .rearrange("p t d -> p (t d)"), HEADS),
                                        spread(alpha_s[:, bass.ds(t, 1), :].rearrange("p t h -> p (t h)"), HD),
                                        ALU.mult).then_inc(m2s_set, 1)

            def message2_low(q, r):
                pool.wait_ge(m2_hi, q * 4 + (r + 1))
                nc.gpsimd.tensor_tensor(m2l[:, r % 2, :], m2[:, r % 2, :], m2h[:, r % 2, :].bitcast(F32),
                                        ALU.subtract).then_inc(m2_lo, 1)

            def scatter_z(q, r):
                t, j = q * 4 + r, r % 2
                pool.wait_ge(z_hi, t + 1)
                settle()
                if not isinstance(t, int) or t >= 2:
                    pool.wait_ge(z_store[j], q * 32 + 16 * (r // 2))
                    settle()
                nc.gpsimd.tensor_copy(scat2[:, j:j + 1], scat_i[:, bass.ds(t, 1)]).then_inc(z_staged, 1)
                pool.wait_ge(z_staged, t + 1)
                settle()
                pool.indirect_dma_start(y2_table, bass.IndirectOffsetOnAxis(scat2[:, j:j + 1].bitcast(U32), 0), z32[:, j, :],
                                        None, bounds_check=N - 1, oob_is_err=False).then_inc(z_store[j], 16)

            in_step(pool, ET, 4, [(own_message, 0), (message2_low, 1), (scatter_z, 3)])
            for j in range(2):
                pool.wait_ge(z_store[j], 16 * (ET // 2))
            phase_end(pool, 3)
            nc.gpsimd.iota(iota_f[:, :], pattern=[[1, EXPERTS]], base=0, channel_multiplier=0).then_inc(const4, 1)
            nc.gpsimd.iota(row_0[:, :], pattern=[[0, 1]], base=0, channel_multiplier=1).then_inc(const4, 1)
            nc.gpsimd.iota(steps_i[:, :], pattern=[[P, steps_i.shape[1]]], base=P, channel_multiplier=0).then_inc(const4, 1)
            pool.wait_ge(p4_bias, 32)
            NT = MACROS * SUBS

            def add_biases(q, r):
                pool.wait_ge(y4_load[r], q * 16 + 16)
                settle()
                nc.gpsimd.tensor_tensor(y_in[:, r, :], y_in[:, r, :], b2_bc[:, :], ALU.add).then_inc(b_added, 1)
                pool.wait_ge(x4_load[r], q * 16 + 16)
                settle()
                pool.wait_ge(b_added, q * (2 * G) + (2 * r + 1))
                settle()
                nc.gpsimd.tensor_tensor(x_in[:, r, :], x_in[:, r, :], y_in[:, r, :], ALU.add).then_inc(b_added, 1)

            def start_rstd(q, r):
                pool.wait_ge(v4_set, q * G + (r + 1))
                nc.gpsimd.tensor_tensor(r4[:, r % 2, :], veps4[:, r % 2, :], minus_half[:, 0:1], ALU.pow).then_inc(r4_set, 1)

            def add_q(q, r):
                pool.wait_ge(num_out, q * G + (r + 2))
                nc.gpsimd.tensor_tensor(attn[:, r % 2, :], attn[:, r % 2, :], q_in[:, r, :], ALU.add).then_inc(o_set, 1)

            def send_tokens(q, r):
                t, j = q * G + r, r % 2
                pool.wait_ge(orow_set, t + (G + 1))
                if not isinstance(t, int) or t:
                    for store in (tok_store, orow_store):
                        pool.wait_ge(store[1 - j], q * 32 + 16 * ((r + 1) // 2))
                pool.sem_inc(row_free, 1)
                pool.indirect_dma_start(token_of_slot, bass.IndirectOffsetOnAxis(slot_i[:, j:j + 1].bitcast(U32), 0),
                                        token_i[:, j:j + 1], None, bounds_check=P * SL - 1, oob_is_err=False)\
                    .then_inc(tok_store[j], 16)
                pool.indirect_dma_start(out, bass.IndirectOffsetOnAxis(row_i[:, j:j + 1].bitcast(U32), 0), orow[:, j, :],
                                        None, bounds_check=N - 1, oob_is_err=False).then_inc(orow_store[j], 16)

            in_step(pool, NT, G, [(add_biases, 0), (start_rstd, 2), (send_tokens, 4), (add_q, 0)])
            for j in range(2):
                pool.wait_ge(tok_store[j], 16 * (NT // 2))
                pool.wait_ge(orow_store[j], 16 * (NT // 2))
            phase_end(pool, 4)
            pool.wait_ge(tok_set, 1)

            def gather_rows(q, r):
                u, k = q * (2 * SLOTS) + r, r % ROW5
                if not isinstance(u, int) or u >= ROW5:
                    pool.wait_ge(res_set, u - (ROW5 - 1))
                    settle()
                nc.gpsimd.tensor_copy(from_st[:, k:k + 1], from_i[:, bass.ds(u, 1)]).then_inc(idx5_set, 1)
                pool.wait_ge(idx5_set, u + 1)
                settle()
                pool.indirect_dma_start(row5[:, k, :], None, x1_table, bass.IndirectOffsetOnAxis(
                    from_st[:, k:k + 1].bitcast(U32), 0)).then_inc(row5_load[k], 16)

            def scatter_results(q, r):
                u, j = q * (2 * SLOTS) + r, r % 2
                pool.wait_ge(res_set, u + 1)
                settle()
                nc.gpsimd.tensor_copy(to_st[:, j:j + 1], tok_i[:, bass.ds(u, 1)]).then_inc(to_set, 1)
                pool.wait_ge(to_set, u + 1)
                settle()
                pool.indirect_dma_start(out, bass.IndirectOffsetOnAxis(to_st[:, j:j + 1].bitcast(U32), 0), res5[:, j, :],
                                        None, bounds_check=N - 1, oob_is_err=False).then_inc(res_store[j], 16)

            in_step(pool, SL, 2 * SLOTS, [(gather_rows, 0), (scatter_results, 4)])
            for j in range(2):
                pool.wait_ge(res_store[j], 16 * (SL // 2))

        @block.scalar
        def _(act):
            chain = Chain(act, act_chain)
            nc.scalar.preload_act_table_set("natural_log_exp_and_others")
            for n, d, s in ((0, bk_bc, bk), (1, bq_bc, bq)):
                act.dma_start(d[:, :], s.partition_broadcast(ROWS)).then_inc(bias_load[n], 16)
            act.dma_start(b1_col[:, :], b1.rearrange("(f p) -> p f", p=P), allow_slow_non_contiguous=True)\
               .then_inc(bias_load[2], 16)
            for r, a in enumerate((att_src1, att_dst1)):
                act.dma_start(att_bc[:, r, :], a.rearrange("h c -> (h c)").partition_broadcast(P))\
                   .then_inc(wload[f"att{r}"], 16)
            for n in range(3 * DC):
                act.wait_ge(wt_bank, n + 1)
                nc.scalar.activation(WTh["kvq"[n // DC]][:, n % DC, :], banks[n % 2][:, :], ACT.Copy).then_inc(wt_hi, 1)
            for n, h, st in (("W1", W1h, w1_st), ("W2", W2h, w2_st)):
                act.wait_ge(wload[n], 16)
                nc.scalar.activation(h[:, :, :], st[:, :, :], ACT.Copy).then_inc(w_hi, 1)
            def x_high(m, subs):
                sub0 = m * SUBS
                for s in subs:
                    act.wait_ge(xt_bank, sub0 + (s + 1))
                    nc.scalar.activation(xTh[:, :, s * ROWS:(s + 1) * ROWS],
                                         groups(banks[s % 2][:, 0:MACRO], DC), ACT.Copy).then_inc(xt_hi, 1)

            x_high(0, range(SUBS))
            act.sem_inc(y_free, SUBS)
            for j in range(2):
                act.sem_inc(y_store[j], 16)
            act.wait_ge(bias_load[2], 16)
            act.wait_ge(w_lo, 1)
            act.wait_ge(w2_lo, 1)
            act.wait_ge(att_sum, 2 * DC)
            def keys_queries(sub0):
                for s in range(SUBS):
                    j = s % 2
                    act.wait_ge(kvq_bank, sub0 * 3 + (3 * s + 2))
                    nc.scalar.activation(vh[:, j, :, 0:P], groups(banks[2 + (3 * s + 1) % 2][0:ROWS, :], DC), ACT.Copy).then_inc(v_hi, 1)
                    for n, buf in ((0, kbuf), (1, qbuf)):
                        act.wait_ge(ssub, sub0 * 2 + (2 * s + n + 1))
                        nc.scalar.activation(buf[:, j, :], buf[:, j, :], ACT.Exp).then_inc(sexp, 1)
                    for f in (2 * s, 2 * s + 1):
                        act.wait_ge(h_bank, sub0 * 2 + (f + 1))
                        nc.scalar.activation(relu[:, f % 2, :], banks[4 + f % 2][:, 0:MACRO], ACT.Relu,
                                             bias=b1_col[:, f:f + 1])
                        nc.scalar.activation(h1h[:, f, :], banks[4 + f % 2][:, 0:MACRO], ACT.Relu,
                                             bias=b1_col[:, f:f + 1]).then_inc(h_hi, 1)
                    act.wait_ge(snorm_k, sub0 + (s + 1))
                    nc.scalar.activation(kh[:, j, :], kbuf[:, j, :], ACT.Copy).then_inc(k_hi, 1)

            def y_rows(m, sub0, s):
                j = s % 2
                act.wait_ge(y_store[j], m * 32 + (16 * (s // 2) + 16))
                act.wait_ge(y_bank, sub0 + (s + 1))
                ins = nc.scalar.activation(y2o[:, j, :], banks[2 + j][0:ROWS, :], ACT.Copy)
                ins.then_inc(y_free, 1)
                act.wait_ge(y_free, sub0 + (s + 1 + SUBS))
                act.dma_start(y2_table[bass.ds((m * SUBS + s) * ROWS, ROWS), :], y2o[:, j, :]).then_inc(y_store[j], 16)

            with act.Fori(0, MACROS - 1) as m:
                sub0 = act.snap(m * SUBS)
                keys_queries(sub0)
                y_rows(m, sub0, 0)
                y_rows(m, sub0, 1)
                x_high(m + 1, (0, 1))
                y_rows(m, sub0, 2)
                x_high(m + 1, (2, 3))
                y_rows(m, sub0, 3)
            keys_queries((MACROS - 1) * SUBS)
            for s in range(SUBS):
                y_rows(MACROS - 1, (MACROS - 1) * SUBS, s)
            for j in range(2):
                act.wait_ge(y_store[j], 16 * (MACROS * SUBS // 2 + 1))

            phase_end(act, 1)
            act.sem_inc(e_src_out, 1)
            act.sem_inc(lg_out, 2)

            def sources_out(q, r):
                t = q * 4 + r
                act.wait_ge(e_bank, t * 2 + 9)
                nc.scalar.activation(xsT[:, :, bass.ds(t * ROWS, ROWS)], groups(banks[0][:, 0:MACRO], DC), ACT.Copy)\
                  .then_inc(e_src_out, 1)

            def logits_out(q, r):
                t = q * 4 + r
                act.wait_ge(lg_bank, t + 1)
                c = bass.ds(t * ROWS, ROWS)
                nc.scalar.activation(head_e[:, c], banks[2 + r % 2][0:HEADS, 0:ROWS], ACT.Copy)
                nc.scalar.activation(head_s[:, c], banks[2 + r % 2][32:32 + HEADS, 0:ROWS], ACT.Copy).then_inc(lg_out, 1)

            in_step(act, ET, 4, [(sources_out, 0), (logits_out, 1)])
            exp_logits(act, 0)
            act.wait_ge(al_out[0], 1)

            def stage_high(t):
                for r, xT in enumerate((xsT, xdT)):
                    nc.scalar.activation(xsh[:, r, :, :], xT[:, :, bass.ds(t * ROWS, ROWS)], ACT.Copy).then_inc(st_hi, 1)

            def message_high(t):
                for h in range(2):
                    act.wait_ge(m_sum, t * 2 + (h + 1))
                    nc.scalar.activation(msgh[:, h * D:(h + 1) * D], msg[:, h, :], ACT.Copy).then_inc(m_hi, 1)

            def aggregate_high(t):
                act.wait_ge(ag_out, t + 1)
                nc.scalar.activation(aggh[:, :, :], aggT[:, :, :], ACT.Copy).then_inc(ag_hi, 1)

            def rows_out(t, first=False):
                act.wait_ge(ye_bank, t + 1)
                if not first:
                    act.wait_ge(ye_store, t * 16)
                nc.scalar.activation(y_edge[:, :], banks[6][0:ROWS, :], ACT.Copy).then_inc(ye_out, 1)

            act.sem_inc(ye_out, 1)
            stage_high(0)
            message_high(0)
            stage_high(1)
            aggregate_high(0)
            message_high(1)
            stage_high(2)
            rows_out(0, first=True)
            with act.Fori(1, ET - 2) as t:
                aggregate_high(t)
                message_high(t + 1)
                stage_high(t + 2)
                rows_out(t)
            aggregate_high(ET - 2)
            message_high(ET - 1)
            rows_out(ET - 2)
            aggregate_high(ET - 1)
            rows_out(ET - 1)
            phase_end(act, 2)
            act.sem_inc(g2_copied, 2)
            act.sem_inc(lt_out, 2)
            with act.Fori(0, ET // 2) as i:
                pair = act.snap(i * 2)
                for j in range(2):
                    act.wait_ge(g2_load[j], i * 32 + 32)
                    for r, all_ in enumerate((ys_all, yd_all)):
                        last = nc.scalar.activation(all_[:, bass.ds(i * 2 + j, 1), :].rearrange("p t d -> p (t d)"), g2[:, j, r, :],
                                                    ACT.Copy)
                    last.then_inc(g2_copied, 1)
                    act.wait_ge(lt_bank, pair + (j + 3))
                    col = bass.ds((i * 2 + j) * ROWS, ROWS)
                    nc.scalar.activation(head_e[:, col], banks[j][0:HEADS, 0:ROWS], ACT.Copy)
                    nc.scalar.activation(head_s[:, col], banks[j][0:HEADS, P:P + ROWS], ACT.Copy).then_inc(lt_out, 1)
            exp_logits(act, 1)
            def message2_high(q, r):
                act.wait_ge(m2_set, q * 4 + (r + 3))
                nc.scalar.activation(m2h[:, r % 2, :], m2[:, r % 2, :], ACT.Copy).then_inc(m2_hi, 1)

            def z_out(q, r):
                t, j = q * 4 + r, r % 2
                act.wait_ge(z_bank, t + 1)
                if not isinstance(t, int) or t >= 2:
                    act.wait_ge(z_store[j], q * 32 + 16 * (r // 2))
                nc.scalar.activation(z32[:, j, :], banks[j][0:ROWS, :], ACT.Copy).then_inc(z_hi, 1)
                nc.scalar.activation(zh[:, j, :], banks[j][0:ROWS, :], ACT.Copy).then_inc(zh_set, 1)

            in_step(act, ET, 4, [(z_out, 2), (message2_high, 1)])
            phase_end(act, 3)
            for n in range(DC):
                act.wait_ge(wp_bank, n + 1)
                nc.scalar.activation(WpTh[:, n, :], banks[n % 2][:, :], ACT.Copy).then_inc(wp_hi, 1)
            act.wait_ge(sw_bank, 1)
            nc.scalar.activation(swT[:, :, :], groups(banks[2][:, 0:DC * EXPERTS], DC), ACT.Copy).then_inc(sw_out, 1)
            act.sem_inc(xft_out, 1)
            NT = MACROS * SUBS

            def q_high(q, r):
                act.wait_ge(qt_bank, q * G + (r + 1))
                nc.scalar.activation(qTh[:, r % 2, :, :], groups(banks[0][:, 0:MACRO], DC), ACT.Copy).then_inc(qt_hi, 1)

            def normalise(q, r):
                act.wait_ge(ln4_set, q * G + (r + 1))
                nc.scalar.activation(xf[:, r, :], x1row[:, r, 0:D], ACT.Identity, bias=x1row[:, r, D + 1:D + 2],
                                     scale=x1row[:, r, D:D + 1]).then_inc(xf_set, 1)

            def o_high(q, r):
                act.wait_ge(ot_bank, q * G + (r + 1))
                nc.scalar.activation(oTh[:, r % 2, :, :], groups(banks[3][:, 0:MACRO], DC), ACT.Copy).then_inc(ot_hi, 1)

            def exp_router(q, r):
                act.wait_ge(rt_max, q * G + (r + 1))
                nc.scalar.activation(ex16[:, r % 2, :], banks[6][0:ROWS, 16 * (r % 2):16 * (r % 2) + 16], ACT.Exp,
                                     bias=lstat[:, r % 2, 0:1], accum_out=lstat[:, r % 2, 1:2]).then_inc(rt_exp, 1)

            def log_sum(q, r):
                act.wait_ge(y_max, q * G + (r + 1))
                chain.link(nc.scalar.activation(exp_y[:, :], y_in[:, r, :], ACT.Exp, bias=y_stat[:, r % 2, 0:1],
                                                accum_out=y_stat[:, r % 2, 1:2]))
                chain.link(nc.scalar.activation(y_stat[:, r % 2, 2:3], y_stat[:, r % 2, 1:2], ACT.Ln))
                nc.scalar.activation(y_stat[:, r % 2, 3:4], y_stat[:, r % 2, 2:3], ACT.Identity, scale=-1.0,
                                     bias=y_stat[:, r % 2, 0:1]).then_inc(lse_set, 1)

            def xf_out(q, r):
                act.wait_ge(xft_bank, q * G + (r + 1))
                nc.scalar.activation(xfT[:, r % 2, :, :], groups(banks[5][:, 0:MACRO], DC), ACT.Copy).then_inc(xft_out, 1)

            def dropped_row(q, r):
                act.wait_ge(row_set, q * G + (r + 1))
                nc.scalar.activation(orow[:, r % 2, :], x1row[:, r, 0:D], ACT.Identity, bias=drop_line[:, r % 2, 1:2],
                                     scale=drop_line[:, r % 2, 0:1]).then_inc(orow_set, 1)

            in_step(act, NT, G, [(q_high, 0), (xf_out, 3), (o_high, 1), (exp_router, 3), (dropped_row, 4), (log_sum, 1), (normalise, 2)],
                    chain=chain, links=2 * G)
            phase_end(act, 4)
            def expert_high(q, r):
                if r % SLOTS > 1:
                    return
                e, j = q * 2 + r // SLOTS, r // SLOTS
                for c in range(r % SLOTS * DC // 2, (r % SLOTS + 1) * DC // 2):
                    act.wait_ge(we_bank, e * DC + (c + 1))
                    nc.scalar.activation(WeTh[:, j, c, :], banks[c % 2][:, :], ACT.Copy).then_inc(we_hi, 1)

            def normal_rows(q, r):
                j, k = r % 2, r % ROW5
                act.wait_ge(row5_load[k], q * (16 * 2 * SLOTS // ROW5) + 16 * (r // ROW5 + 1))
                nc.scalar.activation(xf5[:, j, :], row5[:, k, 0:D], ACT.Identity, bias=row5[:, k, D + 1:D + 2],
                                     scale=row5[:, k, D:D + 1]).then_inc(x5_set, 1)

            def rows_high(q, r):
                act.wait_ge(f_bank, q * (2 * SLOTS) + (r + 1))
                nc.scalar.activation(fTh[:, r % 2, :, :], groups(banks[2 + r % 2][:, :], DC), ACT.Copy).then_inc(f_hi, 1)

            in_step(act, SL, 2 * SLOTS, [(expert_high, 0), (normal_rows, 1), (rows_high, 2)])

        @block.vector
        def _(dve):
            chain = Chain(dve, dve_chain)
            for n in range(3 * DC):
                dve.wait_ge(wt_hi, n + 1)
                nc.vector.tensor_tensor(WTl["kvq"[n // DC]][:, n % DC, :], banks[n % 2][:, :],
                                        WTh["kvq"[n // DC]][:, n % DC, :].bitcast(F32), ALU.subtract).then_inc(wt_lo, 1)
            def layer_norm(m):
                dve.wait_ge(x_load, m * 16 + 16)
                for s in range(SUBS):
                    last = nc.vector.bn_stats(stats[:, s, :], xn[:, s, :])
                chain.link(last, dve_settled)
                for s in range(SUBS):
                    last = nc.vector.bn_aggr(mv[:, s, :], stats[:, s, :])
                chain.link(last)
                nc.vector.tensor_scalar(veps[:, :], mv[:, :, 1], EPS, None, ALU.add).then_inc(var_ready, 1)
                dve.wait_ge(rstd0, m + 1)
                refine(dve, chain, rstd[:, :], veps[:, :], newt)
                for s in range(SUBS):
                    nc.vector.tensor_scalar(xn[:, s, :], xn[:, s, :], mv[:, s, 0:1], rstd[:, s:s + 1],
                                            ALU.subtract, ALU.mult).then_inc(xn_ready, 1)

            def x_low(m):
                sub0 = m * SUBS
                for s in range(SUBS):
                    dve.wait_ge(xt_hi, sub0 + (s + 1))
                    nc.vector.tensor_tensor(xTl[:, :, s * ROWS:(s + 1) * ROWS], groups(banks[s % 2][:, 0:MACRO], DC),
                                            xTh[:, :, s * ROWS:(s + 1) * ROWS].bitcast(F32), ALU.subtract).then_inc(xt_lo, 1)

            layer_norm(0)
            dve.wait_ge(w_hi, 1)
            nc.vector.tensor_tensor(W1l[:, :, :], w1_st[:, :, :], W1h[:, :, :].bitcast(F32), ALU.subtract).then_inc(w_lo, 1)
            x_low(0)
            for r in range(2):
                dve.wait_ge(wload[f"att{r}"], 16)
            dve.wait_ge(const_done, CONSTS)
            for c in range(DC):
                for r in range(2):
                    chain.link(nc.vector.tensor_tensor(att_tmp[:, r, :], w1_st[:, c, :], att_bc[:, r, :], ALU.mult))
                    nc.vector.tensor_reduce(att1[:, c, 40 * r:40 * r + 8], groups(att_tmp[:, r, :], HEADS),
                                            AX.X, ALU.add).then_inc(att_sum, 1)
                    dve.wait_ge(att_sum, c * 2 + r + 1)
            nc.vector.tensor_tensor(att1[:, :, 72:80], att1[:, :, 0:8], att1[:, :, 40:48], ALU.add)
            for n in range(2):
                dve.wait_ge(bias_load[n], 16)
            dve.sem_inc(ctx_free, 2)
            dve.wait_ge(w2_lo, 1)
            nc.vector.memset(vl[:, :, :, P:P + 2].bitcast(F32), 0.0)
            nc.vector.memset(vh[:, :, :, P:P + 2].bitcast(F32), 1.0).then_inc(ones_done, 1)
            def keys_queries(m, sub0):
                for s in range(SUBS):
                    j = s % 2
                    for n, buf, bias in ((0, kbuf, bk_bc), (1, qbuf, bq_bc)):
                        dve.wait_ge(kvq_bank, sub0 * 3 + (3 * s + 2 * n + 1))
                        if n:
                            dve.wait_ge(q_store[j], m * 32 + (16 * (s // 2) + 16))
                        nc.vector.tensor_tensor(buf[:, j, :], banks[2 + (3 * s + 2 * n) % 2][0:ROWS, :], bias[:, :],
                                                ALU.add).then_inc(kvq_free, 1)
                        dve.wait_ge(kvq_free, sub0 * 3 + (3 * s + 2 * n + 1))
                        nc.vector.tensor_reduce(kq_max[:, j, n, :], groups(buf[:, j, :], HEADS), AX.X, ALU.max).then_inc(smax, 1)
                        if n == 0:
                            dve.wait_ge(v_hi, sub0 + (s + 1))
                            nc.vector.tensor_tensor(vl[:, j, :, 0:P], groups(banks[2 + (3 * s + 1) % 2][0:ROWS, :], DC),
                                                    vh[:, j, :, 0:P].bitcast(F32), ALU.subtract).then_inc(kvq_free, 1)
                    for n, buf in ((0, kbuf), (1, qbuf)):
                        dve.wait_ge(sexp, sub0 * 2 + (2 * s + n + 1))
                        chain.link(nc.vector.tensor_reduce(kq_rec[:, j, n, :], groups(buf[:, j, :], HEADS), AX.X, ALU.add))
                        nc.vector.reciprocal(kq_rec[:, j, n, :], kq_rec[:, j, n, :]).then_inc(srec, 1)
                    dve.wait_ge(k_hi, sub0 + (s + 1))
                    nc.vector.tensor_tensor(kl[:, j, :], kbuf[:, j, :], kh[:, j, :].bitcast(F32),
                                            ALU.subtract).then_inc(k_lo, 1)
                    if s:
                        add_context(dve, chain, sub0, s - 1)

            with dve.Fori(0, MACROS - 1) as m:
                sub0 = dve.snap(m * SUBS)
                chain.enter(m, DVE_LINKS)
                keys_queries(m, sub0)
                layer_norm(m + 1)
                add_context(dve, chain, sub0, SUBS - 1)
                x_low(m + 1)
            chain.leave(MACROS - 1)
            keys_queries(MACROS - 1, (MACROS - 1) * SUBS)
            add_context(dve, chain, (MACROS - 1) * SUBS, SUBS - 1)
            phase_end(dve, 1)
            dve.wait_ge(raw_load, 48)
            nc.vector.memset(earlier[:, 0:E], 1.0)
            nc.vector.memset(earlier[:, E + ROWS:2 * E], 0.0)
            nc.vector.tensor_copy(raw_f[:, :], raw_dst[:, :])
            chain.link(nc.vector.tensor_copy(dst_bc[:, 1:E + 1], dst_bi[:, :]))
            dve.wait_ge(earlier_set, 1)

            def find_places(i, first=False):
                for j in range(2):
                    t = i * 2 + j
                    chain.link(nc.vector.scalar_tensor_tensor(out=sort_bits[:, :], in0=dst_bc[0:ROWS, 1:E + 1],
                                                              scalar=raw_f[:, bass.ds(t, 1)],
                                                              in1=earlier[:, bass.ds(E - t * ROWS, E)], op0=ALU.subtract,
                                                              op1=ALU.is_lt, accum_out=place_f[:, j:j + 1]))
                    if not first:
                        dve.wait_ge(sort_store[j], i * 32)
                    nc.vector.tensor_copy(place_st[:, j:j + 1], place_f[:, j:j + 1])
                    nc.vector.tensor_copy(src_st[:, j:j + 1], raw_src[:, bass.ds(t, 1)])
                    nc.vector.tensor_copy(dst_st[:, j:j + 1], raw_dst[:, bass.ds(t, 1)]).then_inc(sort_staged, 1)

            find_places(0, first=True)
            with dve.Fori(1, ET // 2) as i:
                chain.enter(i - 1, 2)
                find_places(i)
            chain.leave(ET // 2 - 1)
            dve.wait_ge(edge_load["dst"], 16)
            dve.wait_ge(edge_load["next"], 32)
            nc.vector.tensor_copy(dst_f[:, :], dst_i[:, :])
            chain.link(nc.vector.tensor_copy(next_f[:, :], next_i[:, :]))
            chain.link(nc.vector.tensor_tensor(next_f[:, :], dst_f[:, :], next_f[:, :], ALU.is_equal))
            nc.vector.scalar_tensor_tensor(out=scat_i[:, :], in0=next_f[:, :], scalar=float(FAR), in1=dst_f[:, :],
                                           op0=ALU.mult, op1=ALU.add).then_inc(edge_f, 1)
            nc.vector.memset(dst_bc[:, 0:1], -1.0)
            nc.vector.memset(dst_bc[:, E + 1:E + 2], -1.0)
            dve.wait_ge(edge_load["all"], 16)
            chain.link(nc.vector.tensor_copy(dst_bc[:, 1:E + 1], dst_bi[:, :]))
            dve.sem_inc(e_dst_out, 1)
            dve.sem_inc(bc_set, 1)

            def edge_stats(q, r):
                j = r % 2
                dve.wait_ge(e_gath[r], q * 32 + 32)
                for n in range(2):
                    last = nc.vector.bn_stats(e_stats[:, n, :], gath[:, r, n, :])
                chain.link(last, dve_settled)
                for n in range(2):
                    last = nc.vector.bn_aggr(e_mv[:, j, n, :], e_stats[:, n, :])
                chain.link(last)
                nc.vector.tensor_scalar(e_veps[:, j, :], e_mv[:, j, :, 1], EPS, None, ALU.add).then_inc(e_var, 1)

            def edge_normal(q, r):
                j = r % 2
                dve.wait_ge(e_rstd0, q * 4 + (r + 1))
                refine(dve, chain, e_rstd[:, j, :], e_veps[:, j, :], e_newt)
                for n in range(2):
                    last = nc.vector.tensor_scalar(gath[:, r, n, :], gath[:, r, n, :], e_mv[:, j, n, 0:1],
                                                   e_rstd[:, j, n:n + 1], ALU.subtract, ALU.mult)
                last.then_inc(e_xn, 1)

            def targets_out(q, r):
                t = q * 4 + r
                dve.wait_ge(e_bank, t * 2 + 10)
                nc.vector.tensor_copy(xdT[:, :, bass.ds(t * ROWS, ROWS)],
                                      groups(banks[1][:, 0:MACRO], DC)).then_inc(e_dst_out, 1)

            in_step(dve, ET, 4, [(edge_stats, 0), (targets_out, 2), (edge_normal, 1)], chain=chain, links=4 * 6)
            find_walls(dve, chain)
            dve.wait_ge(lg_out, ET + 2)
            edge_softmax(dve, chain, 0)
            dve.wait_ge(al_out[0], 1)
            nc.vector.memset(carry[:, :], 0.0)
            nc.vector.memset(same_dst[:, ROWS:ROWS + 1].bitcast(F32), 0.0)
            with dve.Fori(0, ET) as t:
                chain.enter(t, 3)
                for h in range(2):
                    dve.wait_ge(hm_bank, t * 2 + (h + 1))
                    hs = slice(h * HEADS // 2, (h + 1) * HEADS // 2)
                    for d, b, a in ((msg, 2 * h, alpha_e), (msg_self, 2 * h + 1, alpha_s)):
                        last = nc.vector.tensor_tensor(groups(d[:, h, :], HEADS // 2), groups(banks[b][0:ROWS, :], HEADS // 2),
                                                       spread(a[:, bass.ds(t, 1), hs].rearrange("p t h -> p (t h)"), HID),
                                                       ALU.mult)
                    last.then_inc(m_self, 1)
                nc.vector.tensor_scalar(same_dst[:, 0:ROWS], dst_bc[0:ROWS, bass.ds(t * ROWS + 1, ROWS)],
                                        dst_f[:, bass.ds(t, 1)], None, ALU.is_equal).then_inc(mask_set, 1)
                chain.link(nc.vector.tensor_scalar(goes_on[:, :], dst_bc[:, bass.ds(t * ROWS + 1, ROWS)],
                                                   dst_bc[:, bass.ds(t * ROWS, 1)], None, ALU.is_equal))
                dve.wait_ge(ag_bank, t + 1)
                for f in range(FC):
                    c = (f % DC) * (ROWS + 1)
                    last = nc.vector.scalar_tensor_tensor(out=aggT[:, f, :], in0=goes_on[:, :], scalar=carry[:, f:f + 1],
                                                          in1=banks[4 + f // DC][:, c:c + ROWS], op0=ALU.mult, op1=ALU.add)
                chain.link(last)
                chain.link(nc.vector.tensor_copy(carry[:, :], aggT[:, :, ROWS - 1]))
                for f in range(FC):
                    last = nc.vector.tensor_scalar(aggT[:, f, :], aggT[:, f, :], b1_col[:, f:f + 1], 0.0, ALU.add, ALU.max)
                last.then_inc(ag_out, 1)
            chain.leave(ET)
            phase_end(dve, 2)
            dve.wait_ge(att2_load, 32)
            dve.sem_inc(logit2_set, 2)
            dve.sem_inc(m2_set, 2)
            find_walls(dve, chain)
            with dve.Fori(0, ET // 2) as i:
                pair = dve.snap(i * 2)
                chain.enter(i, 2 * 2)
                for j in range(2):
                    dve.wait_ge(g2_load[j], i * 32 + 32)
                    for r in range(2):
                        last = nc.vector.tensor_tensor(prod2[:, r, :], g2[:, j, r, :], att2_bc[:, 0, :], ALU.mult)
                    chain.link(last)
                    dve.wait_ge(p2_pool, pair + (j + 1))
                    chain.link(nc.vector.tensor_reduce(dots[:, :, :].rearrange("p r h -> p (r h)"),
                                                       prod2[:, :, :].rearrange("p r (h c) -> p (r h) c", h=HEADS), AX.X, ALU.add))
                    dve.wait_ge(lt_bank, pair + (j + 1))
                    nc.vector.tensor_tensor(logit2[:, j, :].rearrange("p (r h) -> p r h", r=2), dots[:, 0:2, :],
                                            dots[:, 2, :].unsqueeze(1).to_broadcast([ROWS, 2, HEADS]), ALU.add).then_inc(logit2_set, 1)
            chain.leave(ET // 2)
            dve.wait_ge(lt_out, ET + 2)
            edge_softmax(dve, chain, 1)
            dve.wait_ge(al_out[1], 1)
            nc.vector.memset(zh[:, 1, :].bitcast(F32), 0.0)
            nc.vector.memset(zl[:, 1, :].bitcast(F32), 0.0).then_inc(z_lo, 1)
            def message2(q, r):
                t, j = q * 4 + r, r % 2
                if not isinstance(t, int) or t >= 2:
                    dve.wait_ge(m2_lo, t - 1)
                nc.vector.tensor_tensor(groups(m2[:, j, :], HEADS),
                                        groups(ys_all[:, bass.ds(t, 1), :].rearrange("p t d -> p (t d)"), HEADS),
                                        spread(alpha_e[:, bass.ds(t, 1), :].rearrange("p t h -> p (t h)"), CLS),
                                        ALU.mult).then_inc(m2_times, 1)

            def add_own(q, r):
                t, j = q * 4 + r, r % 2
                dve.wait_ge(m2_times, t + 1)
                dve.wait_ge(m2s_set, t + 1)
                nc.vector.tensor_tensor(m2[:, j, :], m2[:, j, :], m2s[:, j, :], ALU.add).then_inc(m2_set, 1)
                tgt = dst_bc[0:ROWS, bass.ds(t * ROWS + 1, ROWS)]
                nc.vector.tensor_scalar(same2[:, j, :], tgt, dst_f[:, bass.ds(t, 1)], None, ALU.is_equal)
                nc.vector.tensor_scalar(goes2[:, j, :], tgt, dst_bc[0:ROWS, bass.ds(t * ROWS, 1)], last_row[:, :],
                                        ALU.is_equal, ALU.mult).then_inc(mask2_set, 1)

            def z_low(q, r):
                dve.wait_ge(zh_set, q * 4 + (r + 1))
                nc.vector.tensor_tensor(zl[:, r % 2, :], banks[r % 2][0:ROWS, :], zh[:, r % 2, :].bitcast(F32),
                                        ALU.subtract).then_inc(z_lo, 1)

            in_step(dve, ET, 4, [(add_own, 1), (z_low, 2), (message2, 0)])
            phase_end(dve, 3)
            for n in range(DC):
                dve.wait_ge(wp_hi, n + 1)
                nc.vector.tensor_tensor(WpTl[:, n, :], banks[n % 2][:, :], WpTh[:, n, :].bitcast(F32), ALU.subtract).then_inc(wp_lo, 1)
            dve.wait_ge(p4_bv, 16)
            dve.wait_ge(p4_bias, 32)
            chain.link(nc.vector.memset(pairs[:, :, :, :], 0.0))
            H = P // 2
            for p in range(DC):
                for k in range(2):
                    c = slice(p * P + k * H, p * P + (k + 1) * H)
                    nc.vector.scalar_tensor_tensor(out=pairs[k * H:(k + 1) * H, p, k, 0:HD], in0=bv_bc[k * H:(k + 1) * H, c],
                                                   scalar=ctx_acc[k * H:(k + 1) * H, p, P:P + 1],
                                                   in1=ctx_acc[k * H:(k + 1) * H, p, k * H:(k + 1) * H],
                                                   op0=ALU.mult, op1=ALU.add)
            for k in range(2):
                last = nc.vector.tensor_copy(pairs[k * H:(k + 1) * H, :, k, HD:HD + 1], ctx_acc[k * H:(k + 1) * H, :, P:P + 1])
            chain.link(last)
            pair_cols = pairs[:, :, :, :].rearrange("p d k c -> p d (k c)")
            nc.vector.memset(ones_row[:, :].bitcast(F32), 1.0)
            nc.vector.memset(ones_row32[:, :], 1.0)
            nc.vector.tensor_copy(bp_h[:, :], bp_bc[0:1, :])
            chain.link(nc.vector.tensor_copy(pairs_h[:, :, :], pair_cols))
            nc.vector.tensor_tensor(bp_l[:, :], bp_bc[0:1, :], bp_h[:, :].bitcast(F32), ALU.subtract)
            nc.vector.tensor_tensor(pairs_l[:, :, :], pair_cols, pairs_h[:, :, :].bitcast(F32), ALU.subtract).then_inc(ctx_ready, 1)
            dve.wait_ge(const4, 3)
            nc.vector.tensor_copy(iota16[:, :], iota_f[:, :])
            nc.vector.tensor_copy(steps128[:, :], steps_i[:, :])
            nc.vector.memset(used[:, :], 0.0)
            chain.link(nc.vector.tensor_copy(rowid[0:ROWS, 0:1], row_0[:, :]))
            dve.wait_ge(p4_sb, 16)
            dve.sem_inc(orow_set, G)
            for s_ in (qt_lo, num_out, ot_lo, x1_set, row_free, rank_set):
                dve.sem_inc(s_, 1)
            NT = MACROS * SUBS

            def q_low(q, r):
                dve.wait_ge(qt_hi, q * G + (r + 1))
                nc.vector.tensor_tensor(qTl[:, r % 2, :, :], groups(banks[0][:, 0:MACRO], DC), qTh[:, r % 2, :, :].bitcast(F32),
                                        ALU.subtract).then_inc(qt_lo, 1)

            def o_low(q, r):
                dve.wait_ge(ot_hi, q * G + (r + 1))
                nc.vector.tensor_tensor(oTl[:, r % 2, :, :], groups(banks[3][:, 0:MACRO], DC), oTh[:, r % 2, :, :].bitcast(F32),
                                        ALU.subtract).then_inc(ot_lo, 1)

            def largest_y(q, r):
                dve.wait_ge(b_added, q * (2 * G) + (2 * r + 1))
                nc.vector.tensor_reduce(y_stat[:, r % 2, 0:1], y_in[:, r, :], AX.X, ALU.max, negate=True).then_inc(y_max, 1)

            def route_max(q, r):
                dve.wait_ge(rt_bank, q * G + (r + 1))
                nc.vector.tensor_reduce(lstat[:, r % 2, 0:1], banks[6][0:ROWS, 16 * (r % 2):16 * (r % 2) + 16], AX.X, ALU.max,
                                        negate=True).then_inc(rt_max, 1)

            def residual(q, r):
                j = r % 2
                dve.wait_ge(lse_set, q * G + (r + 1))
                dve.wait_ge(x1_store[r], q * 16 + 16)
                dve.wait_ge(orow_set, q * G + (r + 1))
                dve.wait_ge(b_added, q * (2 * G) + (2 * r + 2))
                dve.wait_ge(mix_bank, q * G + (r + 1))
                nc.vector.scalar_tensor_tensor(out=x1row[:, r, 0:D], in0=banks[4][0:ROWS, :], scalar=y_stat[:, j, 3:4],
                                               in1=x_in[:, r, :], op0=ALU.add, op1=ALU.add).then_inc(x1_set, 1)

            def x1_stats(q, r):
                dve.wait_ge(x1_set, q * G + (r + 2))
                dve.sem_inc(dve_settled, 1)
                chain.mark("stats", nc.vector.bn_stats(stats4[:, :], x1row[:, r, 0:D]))

            def x1_mean(q, r):
                chain.need("stats", dve_settled)
                chain.mark("mean", nc.vector.bn_aggr(mv4[:, r % 2, :], stats4[:, :]))

            def x1_var(q, r):
                chain.need("mean")
                nc.vector.tensor_scalar(veps4[:, r % 2, :], mv4[:, r % 2, 1:2], EPS, None, ALU.add).then_inc(v4_set, 1)

            def square(q, r):
                dve.wait_ge(r4_set, q * G + (r + 1))
                chain.mark("square", nc.vector.tensor_tensor(newt4[:, :], r4[:, r % 2, :], r4[:, r % 2, :], ALU.mult))

            def square_by_var(q, r):
                chain.need("square")
                chain.mark("by_var", nc.vector.tensor_tensor(newt4[:, :], newt4[:, :], veps4[:, r % 2, :], ALU.mult))

            def newton_factor(q, r):
                chain.need("by_var")
                chain.mark("factor", nc.vector.tensor_scalar(newt4[:, :], newt4[:, :], -0.5, 1.5, ALU.mult, ALU.add))

            def newton_rstd(q, r):
                chain.need("factor")
                chain.mark("rstd", nc.vector.tensor_tensor(x1row[:, r, D:D + 1], r4[:, r % 2, :], newt4[:, :], ALU.mult))

            def newton_shift(q, r):
                chain.need("rstd")
                nc.vector.scalar_tensor_tensor(out=x1row[:, r, D + 1:D + 2], in0=mv4[:, r % 2, 0:1], scalar=-1.0,
                                               in1=x1row[:, r, D:D + 1], op0=ALU.mult, op1=ALU.mult).then_inc(ln4_set, 1)

            def largest_prob(q, r):
                dve.wait_ge(rt_exp, q * G + (r + 1))
                dve.sem_inc(dve_settled, 1)
                chain.mark("top", nc.vector.max(top8[:, :], ex16[:, r % 2, :]))
                nc.vector.reciprocal(lstat[:, r % 2, 2:3], lstat[:, r % 2, 1:2])

            def its_expert(q, r):
                chain.need("top", dve_settled)
                chain.mark("arg", nc.vector.max_index(arg8[:, :], top8[:, :], ex16[:, r % 2, :]))

            def expert_number(q, r):
                chain.need("arg")
                chain.mark("argf", nc.vector.tensor_copy(argf[:, r % 2, :], arg8[:, 0:1]))
                nc.vector.tensor_tensor(x1row[:, r, D + 2:D + 3], top8[:, 0:1], lstat[:, r % 2, 2:3], ALU.mult)

            def one_hot(q, r):
                chain.need("argf")
                nc.vector.tensor_scalar(onehot[:, r % 2, :], iota16[0:ROWS, :], argf[:, r % 2, :], None, ALU.is_equal).then_inc(oh_set, 1)

            half = HEADS // 2
            heads = [groups(banks[1 + b][0:ROWS, 0:half * (HD + 1)], half) for b in range(2)]

            def attend_sums(q, r):
                dve.wait_ge(num_bank, q * G + (r + 1))
                for b in range(2):
                    last = nc.vector.reciprocal(den[:, r % 2, b * half:(b + 1) * half], heads[b][:, :, HD])
                chain.mark("den", last)

            def attend(q, r):
                j = r % 2
                chain.need("den")
                for b in range(2):
                    last = nc.vector.tensor_tensor(groups(attn[:, j, b * D // 2:(b + 1) * D // 2], half), heads[b][:, :, 0:HD],
                                                   spread(den[:, j, b * half:(b + 1) * half], HD), ALU.mult)
                last.then_inc(num_out, 1)

            def queue(q, r):
                dve.wait_ge(pf_bank, q * G + (r + 1))
                chain.mark("rank", nc.vector.tensor_tensor(rank[:, :], banks[7][0:ROWS, 0:16], used[:, :], ALU.add))

            def queue_ends(q, r):
                chain.need("rank")
                chain.mark("used", nc.vector.tensor_tensor(used[:, :], banks[7][0:ROWS, 16:32], used[:, :], ALU.add))
                nc.vector.scalar_tensor_tensor(out=rank[:, :], in0=rank[:, :], scalar=1.0, in1=onehot[:, r % 2, :],
                                               op0=ALU.mult, op1=ALU.mult, accum_out=small[:, 0:1]).then_inc(rank_set, 1)

            def slot_terms(q, r):
                dve.wait_ge(rank_set, q * G + (r + 2))
                nc.vector.tensor_scalar(steps_tmp[:, :], steps128[:, :], small[:, 0:1], None, ALU.is_le, ALU.add,
                                        accum_out=small[:, 1:2])
                nc.vector.tensor_scalar(small[:, 2:3], small[:, 0:1], float(SL), None, ALU.mult)
                nc.vector.tensor_scalar(small[:, 3:4], small[:, 0:1], float(CAP), float(FAR), ALU.is_ge, ALU.mult)
                chain.mark("terms", nc.vector.tensor_scalar(small[:, 4:5], small[:, 0:1], float(CAP), float(FAR),
                                                            ALU.is_lt, ALU.mult))

            def slot_place(q, r):
                chain.need("terms")
                chain.mark("slot", nc.vector.scalar_tensor_tensor(out=small[:, 5:6], in0=small[:, 1:2], scalar=float(1 - P * SL),
                                                                  in1=small[:, 2:3], op0=ALU.mult, op1=ALU.add))

            def slot_full(q, r):
                chain.need("slot")
                chain.mark("full", nc.vector.scalar_tensor_tensor(out=small[:, 6:7], in0=argf[:, r % 2, :], scalar=float(SLOTS),
                                                                  in1=small[:, 5:6], op0=ALU.mult, op1=ALU.add))

            def slot_rows(q, r):
                j = r % 2
                dve.wait_ge(row_free, q * G + (r + 1))
                nc.vector.tensor_tensor(row_i[:, j:j + 1], rowid[0:ROWS, 0:1], small[:, 4:5], ALU.add)
                nc.vector.tensor_scalar(drop_line[:, j, 0:1], x1row[:, r, D:D + 1], x1row[:, r, D + 2:D + 3], 1.0,
                                        ALU.mult, ALU.add)
                nc.vector.tensor_tensor(drop_line[:, j, 1:2], x1row[:, r, D + 1:D + 2], x1row[:, r, D + 2:D + 3], ALU.mult)
                chain.mark("token", nc.vector.tensor_copy(token_i[:, j:j + 1], rowid[0:ROWS, 0:1]))

            def slot_done(q, r):
                chain.need("token")
                chain.need("full")
                nc.vector.tensor_tensor(slot_i[:, r % 2:r % 2 + 1], small[:, 6:7], small[:, 3:4], ALU.add)
                nc.vector.tensor_scalar(rowid[0:ROWS, 0:1], rowid[0:ROWS, 0:1], float(ROWS), None, ALU.add).then_inc(row_set, 1)

            nc.vector.memset(x1row[:, :, D + 3:D + 4], 0.0)
            in_step(dve, NT, G, [
                (queue, 4), (q_low, 0), (queue_ends, 4), (residual, 2), (slot_terms, 4), (o_low, 1), (slot_place, 4),
                (x1_stats, 2), (slot_full, 4), (slot_rows, 4), (route_max, 3), (x1_mean, 2), (x1_var, 2),
                (slot_done, 4), (largest_y, 1), (square, 2), (largest_prob, 3), (square_by_var, 2), (its_expert, 3),
                (newton_factor, 2), (expert_number, 3), (newton_rstd, 2), (attend_sums, 0), (newton_shift, 2),
                (one_hot, 3), (attend, 0)],
                chain=chain, links=G * LINKS4)
            phase_end(dve, 4)
            dve.wait_ge(tok_load, 16)
            chain.link(nc.vector.tensor_copy(tok_f[:, :], tok_i[:, :]))
            nc.vector.tensor_scalar(from_i[:, :], tok_f[:, :], float(N - 1), None, ALU.min).then_inc(tok_set, 1)
            dve.sem_inc(y5_out, 2)
            dve.sem_inc(f_lo, 2)

            def expert_low(q, r):
                if r % SLOTS > 1:
                    return
                e, j = q * 2 + r // SLOTS, r // SLOTS
                for c in range(r % SLOTS * DC // 2, (r % SLOTS + 1) * DC // 2):
                    dve.wait_ge(we_hi, e * DC + (c + 1))
                    nc.vector.tensor_tensor(WeTl[:, j, c, :], banks[c % 2][:, :], WeTh[:, j, c, :].bitcast(F32),
                                            ALU.subtract).then_inc(we_lo, 1)

            def rows_low(q, r):
                dve.wait_ge(f_hi, q * (2 * SLOTS) + (r + 1))
                nc.vector.tensor_tensor(fTl[:, r % 2, :, :], groups(banks[2 + r % 2][:, :], DC),
                                        fTh[:, r % 2, :, :].bitcast(F32), ALU.subtract).then_inc(f_lo, 1)

            def finish_rows(q, r):
                u, j, k = q * (2 * SLOTS) + r, r % 2, r % ROW5
                if r % SLOTS == 0:
                    dve.wait_ge(eb_load[r // SLOTS], q * 16 + 16)
                dve.wait_ge(y5_bank, u + 1)
                nc.vector.tensor_tensor(yb5[:, j, :], banks[4 + j][:, :], eb_bc[:, r // SLOTS, :], ALU.add).then_inc(y5_out, 1)
                dve.wait_ge(y5_out, u + 3)
                if not isinstance(u, int) or u >= 2:
                    dve.wait_ge(res_store[j], q * (16 * SLOTS) + 16 * (r // 2))
                nc.vector.scalar_tensor_tensor(out=res5[:, j, :], in0=yb5[:, j, :], scalar=row5[:, k, D + 2:D + 3],
                                               in1=row5[:, k, 0:D], op0=ALU.mult, op1=ALU.add).then_inc(res_set, 1)

            in_step(dve, SL, 2 * SLOTS, [(expert_low, 0), (rows_low, 2), (finish_rows, 3)])

        @block.tensor
        def _(pe):
            pe.wait_ge(const_done, 1)
            for n in range(3 * DC):
                if n % DC == 0:
                    pe.wait_ge(wload["kvq"[n // DC]], 16)
                if n >= 2:
                    pe.wait_ge(wt_lo, n - 1)
                st = (wk_st, wv_st, wq_st)[n // DC]
                for c in range(DC):
                    last = nc.tensor.transpose(banks[n % 2][:, c * P:(c + 1) * P],
                                               st[:, c, (n % DC) * P:(n % DC + 1) * P], ident[:, :])
                last.then_inc(wt_bank, 1)
            pe.wait_ge(wt_lo, 3 * DC)

            def turn(m, subs):
                sub0 = m * SUBS
                for s in subs:
                    if s == 0:
                        pe.wait_ge(xn_ready, sub0 + SUBS)
                    if s >= 2:
                        pe.wait_ge(xt_lo, sub0 + (s - 1))
                    for c in range(DC):
                        last = nc.tensor.transpose(banks[s % 2][:, c * ROWS:(c + 1) * ROWS], xn[:, s, c * P:(c + 1) * P],
                                                   ident[0:ROWS, 0:ROWS])
                    last.then_inc(xt_bank, 1)

            turn(0, range(SUBS))
            pe.wait_ge(w_lo, 1)
            pe.wait_ge(w2_lo, 1)
            pe.wait_ge(ones_done, 1)
            def macro_tile(m, sub0, sub3, more):
                def context(s):
                    j = s % 2
                    pe.wait_ge(k_lo, sub0 + (s + 1))
                    pe.wait_ge(ctx_free, sub0 * 2 + (2 * s + 2))
                    for p in range(DC):
                        c = slice(p * P, (p + 1) * P)
                        last = products(banks[6 + p // 2][:, p % 2 * (P + 2):(p % 2 + 1) * (P + 2)],
                                        [(kh[:, j, c], kl[:, j, c], vh[:, j, p, :], vl[:, j, p, :])])
                    last.then_inc(ctx_bank, 1)

                for s in range(SUBS):
                    pe.wait_ge(xt_lo, sub0 + (s + 1) if s else sub0 + 1)
                    r = slice(s * ROWS, (s + 1) * ROWS)
                    for n, w in enumerate("kvq"):
                        u = 3 * s + n
                        if u >= 2:
                            pe.wait_ge(kvq_free, sub3 + (u - 1))
                        else:
                            pe.wait_ge(y_free, sub0 + (SUBS - 1 + u))
                        products(banks[2 + u % 2][0:ROWS, :], [(xTh[:, c, r], xTl[:, c, r], WTh[w][:, c, :], WTl[w][:, c, :])
                                                               for c in range(DC)]).then_inc(kvq_bank, 1)
                    if s == 0:
                        pe.wait_ge(xt_lo, sub0 + SUBS)
                    for f in (2 * s, 2 * s + 1):
                        if f >= 2:
                            pe.wait_ge(h_hi, sub0 * 2 + (f - 1))
                        fs = slice(f * P, (f + 1) * P)
                        products(banks[4 + f % 2][:, 0:MACRO], [(W1h[:, c, fs], W1l[:, c, fs], xTh[:, c, :], xTl[:, c, :])
                                                                for c in range(DC)]).then_inc(h_bank, 1)
                    if s:
                        context(s - 1)
                for s in range(SUBS):
                    r = slice(s * ROWS, (s + 1) * ROWS)
                    if s < 2:
                        pe.wait_ge(kvq_free, sub3 + (3 * SUBS - 1 + s))
                    else:
                        pe.wait_ge(y_free, sub0 + (SUBS + s - 1))
                    for f in range(FC):
                        if s == 0:
                            pe.wait_ge(h_lo, sub0 * 2 + (f + 1))
                        last = products(banks[2 + s % 2][0:ROWS, :], [(h1h[:, f, r], h1l[:, f, r], W2h[:, f, :], W2l[:, f, :])],
                                        first=f == 0, more=f < FC - 1)
                    last.then_inc(y_bank, 1)
                    if s == 0:
                        context(SUBS - 1)
                    elif s < 3 and more:
                        turn(m + 1, (2 * s - 2, 2 * s - 1))
            with pe.Fori(0, MACROS - 1) as m:
                macro_tile(m, pe.snap(m * SUBS), pe.snap(m * (3 * SUBS)), more=True)
            macro_tile(MACROS - 1, (MACROS - 1) * SUBS, (MACROS - 1) * (3 * SUBS), more=False)
            phase_end(pe, 1)
            pe.sem_inc(e_bank, 8)

            def edge_turn(q, r):
                t = q * 4 + r
                pe.wait_ge(e_xn, t + 1)
                for n, out_done in ((0, e_src_out), (1, e_dst_out)):
                    pe.wait_ge(out_done, t + 1)
                    for c in range(DC):
                        last = nc.tensor.transpose(banks[n][:, c * ROWS:(c + 1) * ROWS], gath[:, r, n, c * P:(c + 1) * P],
                                                   ident[0:ROWS, 0:ROWS])
                    last.then_inc(e_bank, 1)

            def edge_logits(q, r):
                t = q * 4 + r
                pe.wait_ge(e_src_out, t + 2)
                pe.wait_ge(e_dst_out, t + 2)
                pe.wait_ge(lg_out, t + 1)
                for n, (xT, a) in enumerate(((xsT, 0), (xdT, 40))):
                    for c in range(DC):
                        last = nc.tensor.matmul(banks[2 + r % 2][0:40, 0:ROWS], att1[:, c, a:a + 40],
                                                xT[:, c, bass.ds(t * ROWS, ROWS)], start=n + c == 0, stop=n == 1 and c == DC - 1)
                last.then_inc(lg_bank, 1)

            in_step(pe, ET, 4, [(edge_turn, 0), (edge_logits, 1)])
            weights_by_edge(pe, 0)
            pe.wait_ge(al_out[0], 1)
            pe.wait_ge(lg_out, ET + 2)

            def hidden_rows(t, first=False):
                pe.wait_ge(st_lo, t * 2 + 2)
                for h in range(2):
                    if not first:
                        pe.wait_ge(m_self, t * 2 + (h - 1))
                    for r in range(2):
                        last = products(banks[2 * h + r][0:ROWS, :],
                                        [(xsh[:, r, c, :], xsl[:, r, c, :], W1h[:, c, h * D:(h + 1) * D], W1l[:, c, h * D:(h + 1) * D])
                                         for c in range(DC)])
                    last.then_inc(hm_bank, 1)

            def aggregate(t):
                pe.wait_ge(mask_set, t + 1)
                pe.wait_ge(m_lo, t * 2 + 2)
                for f in range(FC):
                    c = (f % DC) * (ROWS + 1)
                    o = banks[4 + f // DC][:, c:c + ROWS + 1]
                    nc.tensor.matmul(o, msgh[:, f * P:(f + 1) * P], same_dst[:, :], start=True, stop=False)
                    last = nc.tensor.matmul(o, msgl[:, f * P:(f + 1) * P], same_dst[:, :], start=False, stop=True)
                last.then_inc(ag_bank, 1)

            def edge_rows(t):
                pe.wait_ge(ag_lo, t + 1)
                pe.wait_ge(ye_out, t + 1)
                products(banks[6][0:ROWS, :], [(aggh[:, f, :], aggl[:, f, :], W2h[:, f, :], W2l[:, f, :])
                                               for f in range(FC)]).then_inc(ye_bank, 1)

            hidden_rows(0, first=True)
            aggregate(0)
            with pe.Fori(0, ET - 1) as t:
                hidden_rows(t + 1)
                edge_rows(t)
                aggregate(t + 1)
            edge_rows(ET - 1)
            phase_end(pe, 2)
            pe.sem_inc(lt_bank, 2)
            with pe.Fori(0, ET // 2) as i:
                pair = pe.snap(i * 2)
                for j in range(2):
                    pe.wait_ge(logit2_set, pair + (j + 3))
                    pe.wait_ge(lt_out, pair + (j + 1))
                    nc.tensor.transpose(banks[j][0:HEADS, 0:ROWS], logit2[:, j, 0:HEADS], ident[0:ROWS, 0:ROWS])
                    nc.tensor.transpose(banks[j][0:HEADS, P:P + ROWS], logit2[:, j, HEADS:2 * HEADS],
                                        ident[0:ROWS, 0:ROWS]).then_inc(lt_bank, 1)
            pe.wait_ge(lt_out, ET + 2)
            weights_by_edge(pe, 1)
            pe.wait_ge(al_out[1], 1)
            def sum_by_target(q, r):
                t, j = q * 4 + r, r % 2
                pe.wait_ge(mask2_set, t + 1)
                pe.wait_ge(m2_lo, t + 1)
                if not isinstance(t, int) or t >= 2:
                    pe.wait_ge(z_hi, t - 1)
                z = banks[j][0:ROWS, :]
                nc.tensor.matmul(z, same2[:, j, :], m2h[:, j, :], start=True, stop=False)
                nc.tensor.matmul(z, same2[:, j, :], m2l[:, j, :], start=False, stop=False)
                pe.wait_ge(z_lo, t + 1)
                nc.tensor.matmul(z, goes2[:, j, :], zh[:, 1 - j, :], start=False, stop=False)
                nc.tensor.matmul(z, goes2[:, j, :], zl[:, 1 - j, :], start=False, stop=True).then_inc(z_bank, 1)

            in_step(pe, ET, 4, [(sum_by_target, 2)])
            phase_end(pe, 3)
            pe.wait_ge(p4_load, 16)
            for n in range(DC):
                if n >= 2:
                    pe.wait_ge(wp_lo, n - 1)
                for c in range(DC):
                    last = nc.tensor.transpose(banks[n % 2][:, c * P:(c + 1) * P], wp_st[:, c, n * P:(n + 1) * P], ident[:, :])
                last.then_inc(wp_bank, 1)
            pe.wait_ge(p4_sw, 16)
            for c in range(DC):
                last = nc.tensor.transpose(banks[2][:, c * EXPERTS:(c + 1) * EXPERTS], sw_st[:, c * P:(c + 1) * P],
                                           ident[0:EXPERTS, 0:EXPERTS])
            last.then_inc(sw_bank, 1)
            pe.wait_ge(sw_out, 1)
            pe.wait_ge(wp_lo, DC)
            pe.wait_ge(ctx_ready, 1)
            pe.wait_ge(p4_sb, 16)

            def q_turn(q, r):
                t = q * G + r
                pe.wait_ge(q4_load[r], q * 16 + 16)
                pe.wait_ge(qt_lo, t + 1)
                for c in range(DC):
                    last = nc.tensor.transpose(banks[0][:, c * ROWS:(c + 1) * ROWS], q_in[:, r, c * P:(c + 1) * P],
                                               ident[0:ROWS, 0:ROWS])
                last.then_inc(qt_bank, 1)

            def o_turn(q, r):
                t = q * G + r
                pe.wait_ge(o_set, t + 1)
                pe.wait_ge(ot_lo, t + 1)
                for c in range(DC):
                    last = nc.tensor.transpose(banks[3][:, c * ROWS:(c + 1) * ROWS], attn[:, r % 2, c * P:(c + 1) * P],
                                               ident[0:ROWS, 0:ROWS])
                last.then_inc(ot_bank, 1)

            def attention(q, r):
                t, j = q * G + r, r % 2
                pe.wait_ge(qt_lo, t + 2)
                pe.wait_ge(num_out, t + 1)
                W = 2 * (HD + 1)
                for p in range(DC):
                    last = products(banks[1 + p // 2][0:ROWS, p % 2 * W:(p % 2 + 1) * W],
                                    [(qTh[:, j, p, :], qTl[:, j, p, :], pairs_h[:, p, :], pairs_l[:, p, :])])
                last.then_inc(num_bank, 1)

            def xf_turn(q, r):
                t = q * G + r
                pe.wait_ge(xf_set, t + 1)
                pe.wait_ge(xft_out, t + 1)
                for c in range(DC):
                    last = nc.tensor.transpose(banks[5][:, c * ROWS:(c + 1) * ROWS], xf[:, r, c * P:(c + 1) * P],
                                               ident[0:ROWS, 0:ROWS])
                last.then_inc(xft_bank, 1)

            def mix(q, r):
                t, j = q * G + r, r % 2
                pe.wait_ge(ot_lo, t + 2)
                pe.wait_ge(x1_set, t + 1)
                products(banks[4][0:ROWS, :], [(oTh[:, j, c, :], oTl[:, j, c, :], WpTh[:, c, :], WpTl[:, c, :])
                                               for c in range(DC)], more=True)
                nc.tensor.matmul(banks[4][0:ROWS, :], ones_row[:, :], bp_h[:, :], start=False, stop=False)
                nc.tensor.matmul(banks[4][0:ROWS, :], ones_row[:, :], bp_l[:, :], start=False, stop=True).then_inc(mix_bank, 1)

            def route(q, r):
                t, j = q * G + r, r % 2
                pe.wait_ge(xft_out, t + 2)
                for c in range(DC):
                    nc.tensor.matmul(banks[6][0:ROWS, 16 * j:16 * j + 16], xfT[:, j, c, :], swT[:, c, :],
                                     start=c == 0, stop=False)
                last = nc.tensor.matmul(banks[6][0:ROWS, 16 * j:16 * j + 16], ones_row32[:, :], sb_bc[0:1, :],
                                        start=False, stop=True)
                last.then_inc(rt_bank, 1)

            def count_before(q, r):
                t, j = q * G + r, r % 2
                pe.wait_ge(oh_set, t + 1)
                pe.wait_ge(rank_set, t + 1)
                nc.tensor.matmul(banks[7][0:ROWS, 0:16], before[:, :], onehot[:, j, :], start=True, stop=True)
                nc.tensor.matmul(banks[7][0:ROWS, 16:32], ones_bf[:, :], onehot[:, j, :], start=True, stop=True).then_inc(pf_bank, 1)

            in_step(pe, MACROS * SUBS, G, [(count_before, 4), (q_turn, 0), (xf_turn, 3), (o_turn, 1), (route, 3), (attention, 0), (mix, 1)])
            phase_end(pe, 4)
            def expert_turn(q, r):
                if r % SLOTS > 1:
                    return
                e, j = q * 2 + r // SLOTS, r // SLOTS
                if r % SLOTS == 0:
                    pe.wait_ge(we_load[j], q * 16 + 16)
                for n in range(r % SLOTS * DC // 2, (r % SLOTS + 1) * DC // 2):
                    if n >= 2 or not isinstance(e, int) or e:
                        pe.wait_ge(we_lo, e * DC + (n - 1))
                    for c in range(DC):
                        last = nc.tensor.transpose(banks[n % 2][:, c * P:(c + 1) * P], we_st[:, j, c, n * P:(n + 1) * P], ident[:, :])
                    last.then_inc(we_bank, 1)

            def rows_turn(q, r):
                u, j = q * (2 * SLOTS) + r, r % 2
                pe.wait_ge(x5_set, u + 1)
                pe.wait_ge(f_lo, u + 1)
                for c in range(DC):
                    last = nc.tensor.transpose(banks[2 + j][:, c * P:(c + 1) * P], xf5[:, j, c * P:(c + 1) * P], ident[:, :])
                last.then_inc(f_bank, 1)

            def expert_rows(q, r):
                u, j, k = q * (2 * SLOTS) + r, r % 2, r // SLOTS
                if r % SLOTS == 0:
                    pe.wait_ge(we_lo, q * (2 * DC) + (k * DC + DC))
                pe.wait_ge(f_lo, u + 3)
                pe.wait_ge(y5_out, u + 1)
                products(banks[4 + j][:, :], [(fTh[:, j, c, :], fTl[:, j, c, :], WeTh[:, k, c, :], WeTl[:, k, c, :])
                                              for c in range(DC)]).then_inc(y5_bank, 1)

            in_step(pe, SL, 2 * SLOTS, [(expert_turn, 0), (rows_turn, 2), (expert_rows, 3)])


_INPUTS = ["x", "src", "dst"] + ["L0_" + n for n in (
    "gnn_W1", "gnn_att_src1", "gnn_att_dst1", "gnn_b1", "gnn_W2", "gnn_att_src2", "gnn_att_dst2", "gnn_b2",
    "mix_Wq", "mix_bq", "mix_Wk", "mix_bk", "mix_Wv", "mix_bv", "mix_Wp", "mix_bp",
    "ffn_switch_w", "ffn_switch_b", "ffn_expert_w", "ffn_expert_b")]


def kernel(**inputs):
    import numpy as np
    import concourse.bacc as bacc
    from concourse import mybir as ir
    from concourse.bass_utils import run_bass_kernel_spmd

    nc = bacc.Bacc("TRN2", target_bir_lowering=False, num_devices=1)
    arrays, args = {}, []
    for name in _INPUTS:
        a = np.ascontiguousarray(inputs[name])
        arrays[f"in_{name}"] = a
        args.append(nc.dram_tensor(f"in_{name}", a.shape, ir.dt.from_np(a.dtype), kind="ExternalInput").ap())
    n, d = arrays["in_x"].shape
    args.append(nc.dram_tensor("out", (n, d), ir.dt.float32, kind="ExternalOutput").ap())
    for name, shape, dt in scratch_tables(n, d, arrays["in_L0_ffn_switch_w"].shape[0], arrays["in_src"].shape[0]):
        args.append(nc.dram_tensor(name, shape, dt, kind="Internal").ap())
    gps_layer(nc, *args)
    r = run_bass_kernel_spmd(nc, [arrays], core_ids=[0])
    return r.results[0]["out"]
```
